# Optimizing a Trainium2 kernel written in Bass

```python
import numpy as np
import jax
import jax.numpy as jnp

def _softmax(x, axis=-1):
    return jax.nn.softmax(x, axis=axis)

def _gelu(x):
    return jax.nn.gelu(x, approximate=True)

def _silu(x):
    return jax.nn.silu(x)

def _sigmoid(x):
    return jax.nn.sigmoid(x)

def _layernorm(x, axis=-1, eps=1e-05):
    m = jnp.mean(x, axis=axis, keepdims=True)
    v = jnp.var(x, axis=axis, keepdims=True)
    return (x - m) / jnp.sqrt(v + eps)

def _scatter_add(tgt, idx, src, axis=0):
    return tgt.at[idx].add(src)

def _segment_sum(src, seg, n):
    return jax.ops.segment_sum(src, seg, n)
kernel_name = 'mk_prb_d2_jaxref_r8_ee9512'

def setup_inputs(seed: int=0):
    np.random.seed(seed)
    _w = jnp.asarray

    def _L0_attn_setup():
        import jax, jax.numpy as jnp
        import numpy as np
        B, S, D_IN = (2, 256, 128)
        H, D_HEAD = (16, 64)
        key = jax.random.key(seed)
        k1, k2, k3 = jax.random.split(key, 3)
        x = jax.random.normal(k1, (B, S, D_IN), dtype=jnp.float32)
        kernel = jax.random.normal(k2, (3, H, D_IN, D_HEAD), dtype=jnp.float32) * np.float32(np.sqrt(2.0 / D_IN))
        WO = jax.random.normal(k3, (1, H * D_HEAD, D_IN), dtype=jnp.float32) * np.float32(np.sqrt(2.0 / (H * D_HEAD)))
        return {'x': x, 'kernel': kernel, 'WO': WO}
    _L0_attn_in = _L0_attn_setup()

    def _L0_ffn_setup():
        import jax, jax.numpy as jnp
        import numpy as np
        DIM = 128

        def _reference_tuple_inner(x, W_r, W_k, W_v, mu_r, mu_k):
            B, T, C = x.shape
            x_prev = jnp.concatenate([jnp.zeros((B, 1, C), x.dtype), x[:, :-1, :]], axis=1)
            xr = mu_r * x + (1.0 - mu_r) * x_prev
            xk = mu_k * x + (1.0 - mu_k) * x_prev
            r = jax.nn.sigmoid(jnp.einsum('btc,dc->btd', xr, W_r))
            k = jnp.einsum('btc,dc->btd', xk, W_k)
            k_act = jnp.square(jax.nn.relu(k))
            out = r * jnp.einsum('btc,dc->btd', k_act, W_v)
            new_state = x[:, -1, :]
            return (out, new_state)
        key = jax.random.key(seed)
        ks = jax.random.split(key, 6)
        B, T, C = (8, 256, DIM)
        x = jax.random.normal(ks[0], (B, T, C), dtype=jnp.float32)
        s = 1.0 / np.sqrt(C)
        W_r = jax.random.uniform(ks[1], (C, C), jnp.float32, -s, s)
        W_k = jax.random.uniform(ks[2], (C, C), jnp.float32, -s, s)
        W_v = jax.random.uniform(ks[3], (C, C), jnp.float32, -s, s)
        mu_r = jax.random.uniform(ks[4], (C,), jnp.float32)
        mu_k = jax.random.uniform(ks[5], (C,), jnp.float32)
        return {'x': x, 'W_r': W_r, 'W_k': W_k, 'W_v': W_v, 'mu_r': mu_r, 'mu_k': mu_k}
    _L0_ffn_in = _L0_ffn_setup()

    def _L1_attn_setup():
        import jax, jax.numpy as jnp
        import numpy as np
        HID = 128
        HEADS = 16
        FEAT = 16
        HD = HID // HEADS
        EPS = 1e-05
        LN_EPS = 1e-05
        B, T = (1, 128)
        IU, JU = np.triu_indices(FEAT, 1)

        def _feature_map(x, gamma, beta):
            mu = x.mean(axis=-1, keepdims=True)
            var = ((x - mu) ** 2).mean(axis=-1, keepdims=True)
            xn = (x - mu) / jnp.sqrt(var + LN_EPS) * gamma + beta
            diag = xn * xn
            off = xn[..., IU] * xn[..., JU]
            return jnp.concatenate([diag * FEAT ** (-0.5), off * (2.0 / FEAT) ** 0.5], axis=-1)
        key = jax.random.key(seed)
        ks = jax.random.split(key, 5)
        s = 0.02
        return {'hidden_states': jax.random.normal(ks[0], (B, T, HID), dtype=jnp.float32), 'Wq': jax.random.normal(ks[1], (FEAT * HEADS, HID), dtype=jnp.float32) * s, 'Wk': jax.random.normal(ks[2], (FEAT * HEADS, HID), dtype=jnp.float32) * s, 'Wv': jax.random.normal(ks[3], (HEADS * HD, HID), dtype=jnp.float32) * s, 'Wo': jax.random.normal(ks[4], (HID, HEADS * HD), dtype=jnp.float32) * s, 'gamma': jnp.ones((FEAT,), dtype=jnp.float32), 'beta': jnp.zeros((FEAT,), dtype=jnp.float32)}
    _L1_attn_in = _L1_attn_setup()

    def _L1_ffn_setup():
        import jax, jax.numpy as jnp
        import numpy as np
        DIM = 128
        NUM_EXPERTS = 8
        HIDDEN = 512
        CAP_FACTOR = 2.0
        B, S = (4, 256)
        key = jax.random.key(seed)
        ks = jax.random.split(key, 6)
        scale_r = 1.0 / np.sqrt(DIM)
        scale_1 = 1.0 / np.sqrt(DIM)
        scale_2 = 1.0 / np.sqrt(HIDDEN)
        return {'x': jax.random.normal(ks[0], (B, S, DIM), dtype=jnp.float32), 'router_w': jax.random.uniform(ks[1], (NUM_EXPERTS, DIM), jnp.float32, -scale_r, scale_r), 'w1': jax.random.uniform(ks[2], (NUM_EXPERTS, DIM, HIDDEN), jnp.float32, -scale_1, scale_1), 'b1': jax.random.uniform(ks[3], (NUM_EXPERTS, HIDDEN), jnp.float32, -scale_1, scale_1), 'w2': jax.random.uniform(ks[4], (NUM_EXPERTS, HIDDEN, DIM), jnp.float32, -scale_2, scale_2), 'b2': jax.random.uniform(ks[5], (NUM_EXPERTS, DIM), jnp.float32, -scale_2, scale_2)}
    _L1_ffn_in = _L1_ffn_setup()
    _d = {'L0_attn_x': _L0_attn_in['x'], 'L0_attn_kernel': _L0_attn_in['kernel'], 'L0_attn_WO': _L0_attn_in['WO'], 'L0_ffn_W_r': _L0_ffn_in['W_r'], 'L0_ffn_W_k': _L0_ffn_in['W_k'], 'L0_ffn_W_v': _L0_ffn_in['W_v'], 'L0_ffn_mu_r': _L0_ffn_in['mu_r'], 'L0_ffn_mu_k': _L0_ffn_in['mu_k'], 'L1_attn_Wq': _L1_attn_in['Wq'], 'L1_attn_Wk': _L1_attn_in['Wk'], 'L1_attn_Wv': _L1_attn_in['Wv'], 'L1_attn_Wo': _L1_attn_in['Wo'], 'L1_attn_gamma': _L1_attn_in['gamma'], 'L1_attn_beta': _L1_attn_in['beta'], 'L1_ffn_router_w': _L1_ffn_in['router_w'], 'L1_ffn_w1': _L1_ffn_in['w1'], 'L1_ffn_b1': _L1_ffn_in['b1'], 'L1_ffn_w2': _L1_ffn_in['w2'], 'L1_ffn_b2': _L1_ffn_in['b2']}
    _x0 = _d['L0_attn_x']
    _d['L0_attn_x'] = jax.random.normal(jax.random.fold_in(jax.random.key(seed), 1), (8, 512, 128), dtype=_x0.dtype)
    del _x0
    return _d

def reference(L0_attn_x, L0_attn_kernel, L0_attn_WO, L0_ffn_W_r, L0_ffn_W_k, L0_ffn_W_v, L0_ffn_mu_r, L0_ffn_mu_k, L1_attn_Wq, L1_attn_Wk, L1_attn_Wv, L1_attn_Wo, L1_attn_gamma, L1_attn_beta, L1_ffn_router_w, L1_ffn_w1, L1_ffn_b1, L1_ffn_w2, L1_ffn_b2):

    def _L0_attn_ref(x, kernel, WO):
        import jax, jax.numpy as jnp
        import numpy as np
        B, S, D_IN = (2, 256, 128)
        H, D_HEAD = (16, 64)
        b, s, _ = x.shape
        h, d = (kernel.shape[1], kernel.shape[3])
        q = jnp.einsum('bsm,hmd->bhsd', x, kernel[0])
        k = jnp.einsum('bsm,hmd->bhsd', x, kernel[1])
        v = jnp.einsum('bsm,hmd->bhsd', x, kernel[2])
        scale = jnp.float32(1.0 / (d * d * h))
        scores = jnp.einsum('bhsd,bhtd->bhst', q, k) * scale
        attn = jax.nn.softmax(scores, axis=-1)
        out = jnp.einsum('bhst,bhtd->bhsd', attn, v)
        out = jnp.transpose(out, (0, 2, 3, 1)).reshape(b, s, d * h)
        out = jnp.einsum('bsf,fm->bsm', out, WO[0])
        return out

    def _L0_ffn_ref(x, W_r, W_k, W_v, mu_r, mu_k):
        import jax, jax.numpy as jnp
        import numpy as np
        DIM = 128

        def _reference_tuple_inner(x, W_r, W_k, W_v, mu_r, mu_k):
            B, T, C = x.shape
            x_prev = jnp.concatenate([jnp.zeros((B, 1, C), x.dtype), x[:, :-1, :]], axis=1)
            xr = mu_r * x + (1.0 - mu_r) * x_prev
            xk = mu_k * x + (1.0 - mu_k) * x_prev
            r = jax.nn.sigmoid(jnp.einsum('btc,dc->btd', xr, W_r))
            k = jnp.einsum('btc,dc->btd', xk, W_k)
            k_act = jnp.square(jax.nn.relu(k))
            out = r * jnp.einsum('btc,dc->btd', k_act, W_v)
            new_state = x[:, -1, :]
            return (out, new_state)
        return _reference_tuple_inner(x, W_r, W_k, W_v, mu_r, mu_k)[0]

    def _L1_attn_ref(hidden_states, Wq, Wk, Wv, Wo, gamma, beta):
        import jax, jax.numpy as jnp
        import numpy as np
        HID = 128
        HEADS = 16
        FEAT = 16
        HD = HID // HEADS
        EPS = 1e-05
        LN_EPS = 1e-05
        B, T = (1, 128)
        IU, JU = np.triu_indices(FEAT, 1)

        def _feature_map(x, gamma, beta):
            mu = x.mean(axis=-1, keepdims=True)
            var = ((x - mu) ** 2).mean(axis=-1, keepdims=True)
            xn = (x - mu) / jnp.sqrt(var + LN_EPS) * gamma + beta
            diag = xn * xn
            off = xn[..., IU] * xn[..., JU]
            return jnp.concatenate([diag * FEAT ** (-0.5), off * (2.0 / FEAT) ** 0.5], axis=-1)
        b, t, _ = hidden_states.shape
        q = (hidden_states @ Wq.T).reshape(b, t, HEADS, FEAT).transpose(0, 2, 1, 3)
        k = (hidden_states @ Wk.T).reshape(b, t, HEADS, FEAT).transpose(0, 2, 1, 3)
        v = (hidden_states @ Wv.T).reshape(b, t, HEADS, HD).transpose(0, 2, 1, 3)
        phi_q = _feature_map(q, gamma, beta)
        phi_k = _feature_map(k, gamma, beta)
        kv_cum = jnp.cumsum(phi_k[..., :, None] * v[..., None, :], axis=2)
        num = jnp.einsum('bhtf,bhtfd->bhtd', phi_q, kv_cum)
        den = jnp.einsum('bhtf,bhtf->bht', phi_q, jnp.cumsum(phi_k, axis=2))[..., None] + EPS
        y = (num / den).transpose(0, 2, 1, 3).reshape(b, t, HEADS * HD)
        return y @ Wo.T

    def _L1_ffn_ref(x, router_w, w1, b1, w2, b2):
        import jax, jax.numpy as jnp
        import numpy as np
        DIM = 128
        NUM_EXPERTS = 8
        HIDDEN = 512
        CAP_FACTOR = 2.0
        B, S = (4, 256)
        Bz, Sz, Dz = x.shape
        E = router_w.shape[0]
        capacity = max(1, int(Sz * CAP_FACTOR / E) + 1)
        scores = jax.nn.softmax(jnp.einsum('bsd,ed->bse', x, router_w), axis=-1)
        scores_t = jnp.swapaxes(scores, 1, 2)
        gate_vals, sel_idx = jax.lax.top_k(scores_t, capacity)
        b_idx = jnp.arange(Bz)[:, None, None]
        tokens = x[b_idx, sel_idx]
        h = jnp.einsum('becd,edh->bech', tokens, w1) + b1[None, :, None, :]
        h = jax.nn.gelu(h, approximate=False)
        y = jnp.einsum('bech,ehd->becd', h, w2) + b2[None, :, None, :]
        gated = y * gate_vals[..., None]
        out = jnp.zeros_like(x).at[b_idx, sel_idx].add(gated)
        return out
    x = L0_attn_x
    xn = _layernorm(x, axis=-1)
    x = x + _L0_attn_ref(xn, L0_attn_kernel, L0_attn_WO) + _L0_ffn_ref(xn, L0_ffn_W_r, L0_ffn_W_k, L0_ffn_W_v, L0_ffn_mu_r, L0_ffn_mu_k)
    xn = _layernorm(x, axis=-1)
    x = x + _L1_attn_ref(xn, L1_attn_Wq, L1_attn_Wk, L1_attn_Wv, L1_attn_Wo, L1_attn_gamma, L1_attn_beta) + _L1_ffn_ref(xn, L1_ffn_router_w, L1_ffn_w1, L1_ffn_b1, L1_ffn_w2, L1_ffn_b2)
    return x

_drawn_inputs = setup_inputs


def setup_inputs(seed=0):
    import zlib

    import numpy as np

    out = dict(_drawn_inputs(seed))
    spreads = {'L1_attn_gamma': (1.0, 0.6), 'L1_attn_beta': (0.0, 0.8)}
    factors = {'L0_ffn_W_r': 3.035,
     'L0_ffn_mu_r': 5.764,
     'L1_attn_Wq': 8.0,
     'L1_attn_Wk': 8.0,
     'L1_attn_Wv': 5.772,
     'L1_attn_Wo': 5.749,
     'L1_ffn_b1': 8.0,
     'L1_ffn_b2': 6.743}
    for name, (base, spread) in spreads.items():
        noise = np.random.default_rng([zlib.crc32(name.encode()), seed]).standard_normal(out[name].shape)
        drawn = base * np.exp(spread * noise) if base else spread * noise
        out[name] = jnp.asarray(drawn.astype(out[name].dtype))
    for name, factor in factors.items():
        out[name] = (out[name] * factor).astype(out[name].dtype)
    return out
```

```python
import concourse.bass as bass
from concourse import mybir
from contextlib import ExitStack

F32 = mybir.dt.float32
ALU = mybir.AluOpType
ACT = mybir.ActivationFunctionType
AX = mybir.AxisListType

P = 128
B, S, D = 8, 512, 128
TILES = S // P
NT = B * TILES
H, DH = 16, 64
PAIRS = H // 2
SCALE = 1.0 / (DH * DH * H)
H1, FEAT, HD = 16, 16, 8
FT = H1 * FEAT // P
HPT = P // FEAT
SLOT = 32
GROUPS = H1 * SLOT // P
HPG = P // SLOT
E, HID = 8, 512
HT = HID // P
CAPACITY = max(1, int(S * 2.0 / E) + 1)
LN_EPS = 1e-05
DEN_EPS = 1e-05


AHEAD = 1


class Links:

    def __init__(self, eng, sem, base=0):
        self.eng, self.sem, self.base, self.n = eng, sem, base, 0

    def __call__(self, ins):
        self.n += 1
        ins.then_inc(self.sem, 1)
        self.eng.wait_ge(self.sem, self.base + self.n)


def prob_d2_kernel(nc, x, kern, wo0, w_r, w_k, w_v, mu_r, mu_k, wq1, wk1, wv1, wo1, gamma, beta,
                   router, w1, b1, w2, b2, out):
    gate_dram = nc.dram_tensor("gate_scratch", [B * E, S], F32, kind="Internal").ap()
    ctx = ExitStack()
    with ctx:
        def sb(name, shape):
            return ctx.enter_context(nc.sbuf_tensor(name, shape, F32))

        def sem(name):
            return ctx.enter_context(nc.semaphore(name))

        X = sb("X", [P, NT, D])
        XNT = sb("XNT", [P, (B + 1) * S])
        ACCT = sb("ACCT", [P, (B + 1) * S])
        ident = sb("ident", [P, P])
        causal = sb("causal", [P, TILES, P])
        block_mean = sb("block_mean", [P, P])
        centre = sb("centre", [P, P])
        head_mask = sb("head_mask", [P, HPT])
        M = sb("M", [P, 2, PAIRS, P])
        WV = sb("WV", [P, H * DH])
        WO = sb("WO", [P, PAIRS, D])
        WR_T = sb("WR_T", [P, 3, P])
        WVO_T = sb("WVO_T", [P, 2, P])
        WQK_T = sb("WQK_T", [P, 2 * FT, P])
        WO_PAD = sb("WO_PAD", [P, GROUPS, D])
        RT = sb("RT", [P, E])
        B1_T = sb("B1_T", [P, E * HT])
        B2_T = sb("B2_T", [P, E])
        MU = sb("MU", [P, 2])
        GB = sb("GB", [P, 2])
        GM = sb("GM", [P, 2, HPT])
        SC = sb("SC", [P, TILES, B * E])
        STATS = sb("STATS", [P, NT, 6])
        MEAN = sb("MEAN", [P, NT])
        RSTD = sb("RSTD", [P, NT])
        LN = sb("LN", [P, 4, NT])

        PS = ctx.enter_context(nc.psum_tensor("PS", [P, 8, 512], F32))

        with ExitStack() as st:
            def tb(name, shape):
                return st.enter_context(nc.sbuf_tensor(name, shape, F32))
            WQS = tb("WQS", [P, H, DH])
            WKS = tb("WKS", [P, H, DH])
            WQT = tb("WQT", [P, PAIRS, P])
            WKT = tb("WKT", [P, PAIRS, P])
            RAW = tb("RAW", [P, 5, P])
            RAW1 = tb("RAW1", [P, 2 * FT, P])
            RAWR = tb("RAWR", [E, P])
            RAWB1 = tb("RAWB1", [E * HT, P])
            RAWB2 = tb("RAWB2", [E, P])
            loaded = st.enter_context(nc.semaphore("loaded"))
            x_loaded = st.enter_context(nc.semaphore("x_loaded"))
            consts = st.enter_context(nc.semaphore("consts"))
            zeroed = st.enter_context(nc.semaphore("zeroed"))
            transposed = st.enter_context(nc.semaphore("transposed"))
            copied = st.enter_context(nc.semaphore("copied"))
            padded = st.enter_context(nc.semaphore("padded"))
            v_links = st.enter_context(nc.semaphore("v_links0"))
            g_links = st.enter_context(nc.semaphore("g_links0"))
            with nc.Block() as block:
                NLOAD = 22

                @block.sync
                def _(sp):
                    def load(dst, src):
                        sp.dma_start(dst, src).then_inc(loaded, 16)
                    load(WQS[:], kern[0].rearrange("h m d -> m h d"))
                    load(WKS[:], kern[1].rearrange("h m d -> m h d"))
                    load(WV[:].rearrange("m (h d) -> m h d", h=H), kern[2].rearrange("h m d -> m h d"))
                    wo_v = wo0[0].rearrange("(d j s) m -> s d j m", j=PAIRS, s=2)
                    for s in range(2):
                        load(WO[DH * s:DH * (s + 1), :, :], wo_v[s])
                    for k, w in enumerate((w_r, w_k, w_v, wv1, wo1)):
                        load(RAW[:, k, :], w)
                    load(RAW1[:, 0:FT, :], wq1.rearrange("(f p) c -> p f c", p=P))
                    load(RAW1[:, FT:2 * FT, :], wk1.rearrange("(f p) c -> p f c", p=P))
                    load(RAWR[:], router)
                    load(RAWB1[:], b1.rearrange("e (j p) -> (e j) p", p=P))
                    load(RAWB2[:], b2)
                    load(MU[:, 0:1], mu_r.rearrange("(p a) -> p a", a=1))
                    load(MU[:, 1:2], mu_k.rearrange("(p a) -> p a", a=1))
                    for k, w in enumerate((gamma, beta)):
                        g = w.rearrange("(p a) -> p a", a=1)
                        for r in range(HPT):
                            sp.dma_start(GB[FEAT * r:FEAT * (r + 1), k:k + 1], g).then_inc(loaded, 16)
                    for q in range(4):
                        sp.dma_start(X[:, q * NT // 4:(q + 1) * NT // 4, :],
                                     x.rearrange("b (t p) d -> p (b t) d", p=P)[:, q * NT // 4:(q + 1) * NT // 4, :]
                                     ).then_inc(x_loaded, 16)
                    sp.wait_ge(x_loaded, 64)
                    sp.wait_ge(zeroed, 1)
                    sp.wait_ge(copied, 1)
                    for r in range(GROUPS):
                        for g in range(HPG):
                            row = HD * (HPG * r + g)
                            sp.dma_start(WO_PAD[SLOT * g:SLOT * g + HD, r, :], WVO_T[row:row + HD, 1, :]).then_inc(padded, 16)
                    sp.wait_ge(padded, 16 * GROUPS * HPG)

                LOADS = (17 + 2 * HPT) * 16

                @block.gpsimd
                def _(pool):
                    link = Links(pool, g_links)
                    nc.gpsimd.memset(WO_PAD[:], 0.0).then_inc(zeroed, 1)
                    link(nc.gpsimd.memset(ident[:], 0.0))
                    link(nc.gpsimd.affine_select(out=ident[:], in_=ident[:], compare_op=ALU.not_equal, fill=1.0,
                                                 base=0, pattern=[[-1, P]], channel_multiplier=1))
                    bm = block_mean[:].rearrange("p (g j) -> p g j", j=FEAT)
                    link(nc.gpsimd.memset(block_mean[:], 1.0 / FEAT))
                    link(nc.gpsimd.affine_select(out=bm, in_=bm, compare_op=ALU.is_ge, fill=0.0,
                                                 base=0, pattern=[[-FEAT, HPT], [0, FEAT]], channel_multiplier=1))
                    link(nc.gpsimd.affine_select(out=bm, in_=bm, compare_op=ALU.is_ge, fill=0.0,
                                                 base=FEAT - 1, pattern=[[FEAT, HPT], [0, FEAT]], channel_multiplier=-1))
                    link(nc.gpsimd.memset(head_mask[:], 1.0))
                    link(nc.gpsimd.affine_select(out=head_mask[:], in_=head_mask[:], compare_op=ALU.is_ge, fill=0.0,
                                                 base=0, pattern=[[-FEAT, HPT]], channel_multiplier=1))
                    link(nc.gpsimd.affine_select(out=head_mask[:], in_=head_mask[:], compare_op=ALU.is_ge, fill=0.0,
                                                 base=FEAT - 1, pattern=[[FEAT, HPT]], channel_multiplier=-1))
                    link(nc.gpsimd.memset(causal[:], 1.0))
                    link(nc.gpsimd.affine_select(out=causal[:], in_=causal[:], compare_op=ALU.is_ge, fill=0.0,
                                                 base=0, pattern=[[0, TILES], [1, P]], channel_multiplier=-1))
                    nc.gpsimd.tensor_tensor(centre[:], ident[:], block_mean[:], ALU.subtract).then_inc(consts, 1)

                @block.tensor
                def _(pe):
                    pe.wait_ge(consts, 1)
                    pe.wait_ge(loaded, LOADS)
                    for k in range(3):
                        nc.tensor.transpose(PS[:, 0, k * P:(k + 1) * P], RAW[:, k, :], ident[:])
                    for k in range(2):
                        nc.tensor.transpose(PS[:, 1, k * P:(k + 1) * P], RAW[:, 3 + k, :], ident[:])
                    nc.tensor.transpose(PS[:, 1, 256:256 + E], RAWR[:], ident[0:E, 0:E])
                    nc.tensor.transpose(PS[:, 1, 288:288 + E * HT], RAWB1[:], ident[0:E * HT, 0:E * HT])
                    nc.tensor.transpose(PS[:, 1, 352:352 + E], RAWB2[:], ident[0:E, 0:E])
                    for f in range(2 * FT):
                        nc.tensor.matmul(PS[:, 2, f * P:(f + 1) * P], RAW1[:, f, :], centre[:], start=True, stop=True)
                    for w, bank in ((WQS, 3), (WKS, 5)):
                        for j in range(PAIRS):
                            last = nc.tensor.transpose(PS[:, bank + j // 4, (j % 4) * P:(j % 4 + 1) * P],
                                                       w[:, 2 * j:2 * j + 2, :].rearrange("p s d -> p (s d)"), ident[:])
                    last.then_inc(transposed, 1)
                    pe.wait_ge(copied, 2)
                    for s in range(2):
                        for j in range(PAIRS):
                            last = nc.tensor.matmul(PS[:, 2 * s + j // 4, (j % 4) * P:(j % 4 + 1) * P],
                                                    WQT[DH * s:DH * (s + 1), j, :], WKT[DH * s:DH * (s + 1), j, :],
                                                    start=True, stop=True)
                    last.then_inc(transposed, 1)

                @block.vector
                def _(dve):
                    dve.wait_ge(transposed, 1)
                    nc.vector.tensor_copy(WVO_T[:].rearrange("p k n -> p (k n)"), PS[:, 1, 0:256]).then_inc(copied, 1)
                    nc.vector.tensor_copy(WQT[:].rearrange("p j n -> p (j n)"), PS[:, 3:5, :].rearrange("p a n -> p (a n)"))
                    nc.vector.tensor_copy(WKT[:].rearrange("p j n -> p (j n)"), PS[:, 5:7, :].rearrange("p a n -> p (a n)"))
                    nc.vector.tensor_copy(WR_T[:].rearrange("p k n -> p (k n)"), PS[:, 0, 0:384])
                    nc.vector.tensor_copy(RT[:], PS[:, 1, 256:256 + E])
                    nc.vector.tensor_copy(B1_T[:], PS[:, 1, 288:288 + E * HT])
                    nc.vector.tensor_copy(B2_T[:], PS[:, 1, 352:352 + E])
                    nc.vector.tensor_copy(WQK_T[:].rearrange("p f n -> p (f n)"), PS[:, 2, :]).then_inc(copied, 1)
                    for k in range(2):
                        nc.vector.tensor_scalar(GM[:, k, :], head_mask[:], GB[:, k:k + 1], None, ALU.mult)
                    dve.wait_ge(transposed, 2)
                    nc.vector.tensor_scalar(M[:].rearrange("p s j n -> p (s j n)"), PS[:, 0:4, :].rearrange("p a n -> p (a n)"),
                                            SCALE, None, ALU.mult)


        def moments(dve, link):
            n = NT
            link(nc.vector.tensor_tensor(LN[:, 0, :], STATS[:, :, 1], STATS[:, :, 4], ALU.add))
            link(nc.vector.tensor_tensor(LN[:, 1, :], STATS[:, :, 1], STATS[:, :, 4], ALU.subtract))
            link(nc.vector.tensor_scalar(MEAN[:], LN[:, 0, :], 0.5, None, ALU.mult))
            link(nc.vector.tensor_tensor(LN[:, 2, :], STATS[:, :, 2], STATS[:, :, 5], ALU.add))
            link(nc.vector.scalar_tensor_tensor(LN[:, 1, :], LN[:, 1, :], 0.25, LN[:, 1, :], ALU.mult, ALU.mult))
            link(nc.vector.scalar_tensor_tensor(LN[:, 2, :], LN[:, 2, :], 1.0 / D, LN[:, 1, :], ALU.mult, ALU.add))
            link(nc.vector.tensor_scalar(LN[:, 2, :], LN[:, 2, :], LN_EPS, None, ALU.add))

        def rstd(dve, link):
            link(nc.vector.reciprocal(LN[:, 0, :], LN[:, 3, :]))
            link(nc.vector.tensor_tensor(LN[:, 0, :], LN[:, 0, :], LN[:, 2, :], ALU.mult))
            link(nc.vector.tensor_tensor(LN[:, 0, :], LN[:, 0, :], LN[:, 3, :], ALU.add))
            link(nc.vector.tensor_scalar(LN[:, 0, :], LN[:, 0, :], 0.5, None, ALU.mult))
            link(nc.vector.reciprocal(RSTD[:], LN[:, 0, :]))

        def layernorm_stage(tag, with_stats, with_router):
            with ExitStack() as st:
                def tb(name, shape):
                    return st.enter_context(nc.sbuf_tensor(name + tag, shape, F32))

                def tsem(name):
                    return st.enter_context(nc.semaphore(name + tag))
                XS = tb("XS", [P, 2, TILES, D])
                XT = tb("XT", [P, 2, S])
                LG = tb("LG", [P, 2, TILES, E])
                LX = tb("LX", [P, 2, TILES])
                v_links, stats_done, var_ready, root_ready = tsem("v_links"), tsem("stats"), tsem("var"), tsem("root")
                normed, turned, stored, kept, logits, shifted, expd, scored = map(
                    tsem, ("normed", "turned", "stored", "kept", "logits", "shifted", "expd", "scored"))
                with nc.Block() as block:
                    @block.scalar
                    def _(act):
                        act.wait_ge(var_ready, 1)
                        nc.scalar.activation(LN[:, 3, :], LN[:, 2, :], ACT.Sqrt).then_inc(root_ready, 1)
                        if with_router:
                            with act.Fori(0, B // 2) as b0_half:
                                b0 = 2 * b0_half
                                for p in range(2):
                                    b = b0 + p
                                    act.wait_ge(turned, b + 1)
                                    nc.scalar.activation(XT[:, p, :], PS[:, p, :], ACT.Copy).then_inc(kept, 1)
                                    act.wait_ge(shifted, b + 1)
                                    nc.scalar.activation(LG[:, p, :, :], LG[:, p, :, :], ACT.Exp).then_inc(expd, 1)

                    @block.tensor
                    def _(pe):
                        with pe.Fori(0, B // 2) as b0_half:
                            b0 = 2 * b0_half
                            for p in range(2):
                                b = b0 + p
                                pe.wait_ge(normed, b + 1)
                                for t in range(TILES):
                                    last = nc.tensor.transpose(PS[:, p, t * P:(t + 1) * P], XS[:, p, t, :], ident[:])
                                last.then_inc(turned, 1)
                                if with_router:
                                    pe.wait_ge(kept, b + 1)
                                    for t in range(TILES):
                                        last = nc.tensor.matmul(PS[:, 2 + p, t * E:(t + 1) * E], XT[:, p, t * P:(t + 1) * P],
                                                                RT[:], start=True, stop=True)
                                    last.then_inc(logits, 1)

                    @block.vector
                    def _(dve):
                        link = Links(dve, v_links)
                        if with_stats:
                            for t in range(NT):
                                last = nc.vector.bn_stats(STATS[:, t, :], X[:, t, :])
                            link(last)
                            if tag == "1":
                                nc.vector.memset(XNT[:, B * S:(B + 1) * S], 0.0)
                                nc.vector.memset(ACCT[:, 0:S], 0.0)
                        moments(dve, link)
                        nc.vector.tensor_scalar(LN[:, 1, :], LN[:, 1, :], 1.0, None, ALU.mult).then_inc(var_ready, 1)
                        dve.wait_ge(root_ready, 1)
                        rstd(dve, link)
                        before = link.n
                        per_b = 5 if with_router else 0
                        with dve.Fori(0, B // 2) as b0_half:
                            b0 = 2 * b0_half
                            for p in range(2):
                                b = b0 + p
                                inner = Links(dve, v_links, before + b * per_b)
                                for t in range(TILES):
                                    tok = b * TILES + t
                                    last = nc.vector.tensor_scalar(XS[:, p, t, :], X[:, bass.ds(tok, 1), :].rearrange("p a d -> p (a d)"),
                                                                   MEAN[:, bass.ds(tok, 1)], RSTD[:, bass.ds(tok, 1)],
                                                                   ALU.subtract, ALU.mult)
                                last.then_inc(normed, 1)
                                if with_router:
                                    dve.wait_ge(kept, b + 1)
                                    nc.vector.tensor_copy(XNT[:, bass.ds(b * S, S)], XT[:, p, :]).then_inc(stored, 1)
                                else:
                                    dve.wait_ge(turned, b + 1)
                                    nc.vector.tensor_copy(XNT[:, bass.ds(b * S, S)], PS[:, p, :]).then_inc(stored, 1)
                                if with_router:
                                    dve.wait_ge(logits, b + 1)
                                    lg = PS[:, 2 + p, 0:TILES * E].rearrange("p (t e) -> p t e", e=E)
                                    inner(nc.vector.tensor_reduce(LX[:, p, :], lg, AX.X, ALU.max))
                                    nc.vector.tensor_tensor(LG[:, p, :, :], lg, LX[:, p, :].unsqueeze(2).broadcast_to([P, TILES, E]),
                                                            ALU.subtract).then_inc(shifted, 1)
                                    dve.wait_ge(expd, b + 1)
                                    inner(nc.vector.tensor_reduce(LX[:, p, :], LG[:, p, :, :], AX.X, ALU.add))
                                    inner(nc.vector.reciprocal(LX[:, p, :], LX[:, p, :]))
                                    inner(nc.vector.tensor_tensor(SC[:, :, bass.ds(b * E, E)], LG[:, p, :, :],
                                                                  LX[:, p, :].unsqueeze(2).broadcast_to([P, TILES, E]), ALU.mult))
                                    inner(nc.vector.tensor_copy(LX[:, p, 0:1], LX[:, p, 1:2]))

        layernorm_stage("1", True, False)

        with ExitStack() as st:
            def tb(name, shape):
                return st.enter_context(nc.sbuf_tensor(name, shape, F32))

            def tsem(name):
                return st.enter_context(nc.semaphore(name))
            G = tb("G", [P, 2, 2, S])
            PR = tb("PR", [P, 2, 2, S])
            PT = tb("PT", [P, 2, 2, TILES, S])
            VT = tb("VT", [P, S])
            V = tb("V", [P, 2, TILES, P])
            OT = tb("OT", [P, S])
            NMAX = tb("NMAX", [P, 2, 2])
            RSUM = tb("RSUM", [P, 2, 2])
            RINV = tb("RINV", [P, 2, 2])
            GP, VP, OP = 6, 6, 7
            s_ready = tsem("s_ready")
            max_ready = tsem("max_ready")
            exp_ready = tsem("exp_ready")
            inv_ready = tsem("inv_ready")
            p_ready = tsem("p_ready")
            t_ready = tsem("t_ready")
            ta_copied = tsem("ta_copied")
            tb_copied = tsem("tb_copied")
            ga_ready = tsem("ga_ready")
            gb_ready = tsem("gb_ready")
            ga_copied = tsem("ga_copied")
            gb_copied = tsem("gb_copied")
            vt_ready = tsem("vt_ready")
            vt_copied = tsem("vt_copied")
            v_ready = tsem("v_ready")
            v_copied = tsem("v_copied")
            o_ready = tsem("o_ready")
            o_copied = tsem("o_copied")
            wo_ready = tsem("wo_ready")
            added = tsem("added")
            zeros = tsem("zeros")

            with nc.Block() as block:
                @block.tensor
                def _(pe):
                    def scores(n, par, i, b):
                        if i == 0:
                            pe.wait_ge(ga_copied, n + 1)
                            pe.wait_ge(gb_copied, n + 1)
                        for s in range(2):
                            last = nc.tensor.matmul(PS[:, 2 * (i % 2) + s, :], G[:, par, s, i * P:(i + 1) * P],
                                                    XNT[:, bass.ds(b * S, S)], start=True, stop=True)
                        last.then_inc(s_ready, 1)

                    def project_a(n, pair, b):
                        nc.tensor.matmul(PS[:, 6, :], M[:, 0, pair, :], XNT[:, bass.ds(b * S, S)],
                                         start=True, stop=True).then_inc(ga_ready, 1)

                    def project_b(n, pair, b):
                        nc.tensor.matmul(PS[:, 7, :], M[:, 1, pair, :], XNT[:, bass.ds(b * S, S)],
                                         start=True, stop=True).then_inc(gb_ready, 1)

                    def values_t(n, pair, b):
                        pe.wait_ge(ga_copied, n + 1)
                        nc.tensor.matmul(PS[:, 6, :], WV[:, pair * P:(pair + 1) * P], XNT[:, bass.ds(b * S, S)],
                                         start=True, stop=True).then_inc(vt_ready, 1)

                    def values(n):
                        pe.wait_ge(vt_copied, n + 1)
                        for t in range(TILES):
                            last = nc.tensor.transpose(PS[:, 7, t * P:(t + 1) * P], VT[:, t * P:(t + 1) * P], ident[:])
                        last.then_inc(v_ready, 1)

                    def turn(c, par):
                        pe.wait_ge(p_ready, c + 1 + AHEAD)
                        pe.wait_ge(ta_copied, c + 1 + AHEAD)
                        pe.wait_ge(tb_copied, c + 1 + AHEAD)
                        for s in range(2):
                            for t in range(TILES):
                                last = nc.tensor.transpose(PS[:, 4 + s, t * P:(t + 1) * P], PR[:, par, s, t * P:(t + 1) * P],
                                                           ident[:])
                        last.then_inc(t_ready, 1)

                    def outputs(n, par, tiles):
                        if tiles[0] == 0:
                            pe.wait_ge(ta_copied, 4 * n + 5 + AHEAD)
                            pe.wait_ge(tb_copied, 4 * n + 5 + AHEAD)
                            pe.wait_ge(v_copied, n + 1 + AHEAD)
                        for t in tiles:
                            for s in range(2):
                                last = nc.tensor.matmul(PS[DH * s:DH * (s + 1), 7, :], V[:, par, t, DH * s:DH * (s + 1)],
                                                        PT[:, par, s, t, :], start=(t == 0), stop=(t == TILES - 1),
                                                        skip_group_check=True)
                        if tiles[-1] == TILES - 1:
                            last.then_inc(o_ready, 1)

                    def project_out(n, pair):
                        pe.wait_ge(o_copied, n + 2)
                        nc.tensor.matmul(PS[:, 6, :], WO[:, pair, :], OT[:], start=True, stop=True).then_inc(wo_ready, 1)

                    pe.wait_ge(zeros, 1)
                    project_a(0, 0, 0)
                    project_b(0, 0, 0)
                    values_t(0, 0, 0)
                    pe.wait_ge(gb_copied, 1)
                    values(0)
                    with pe.Fori(0, B) as b:
                        for h in range(PAIRS):
                            n = b * PAIRS + h
                            par, nxt = h % 2, (h + 1) % PAIRS
                            nb = b + (h + 1) // PAIRS
                            scores(n, par, 0, b)
                            pe.wait_ge(added, n + AHEAD)
                            project_a(n + 1, nxt, nb)
                            pe.wait_ge(v_copied, n + 1 + AHEAD)
                            project_b(n + 1, nxt, nb)
                            turn(4 * n - 1, 1)
                            scores(n, par, 1, b)
                            values_t(n + 1, nxt, nb)
                            pe.wait_ge(gb_copied, n + 2)
                            outputs(n - 1, 1 - par, range(0, 2))
                            turn(4 * n, 0)
                            scores(n, par, 2, b)
                            outputs(n - 1, 1 - par, range(2, TILES))
                            turn(4 * n + 1, 1)
                            scores(n, par, 3, b)
                            pe.wait_ge(vt_copied, n + 2)
                            project_out(n - 1, (h - 1) % PAIRS)
                            values(n + 1)
                            turn(4 * n + 2, 0)
                    n = B * PAIRS
                    turn(4 * n - 1, 1)
                    pe.wait_ge(v_copied, n + 1 + AHEAD)
                    outputs(n - 1, 1, range(TILES))
                    pe.wait_ge(added, n + AHEAD)
                    project_out(n - 1, PAIRS - 1)

                @block.vector
                def _(dve):
                    def row_max(c, par):
                        dve.wait_ge(s_ready, c + 1)
                        nc.vector.tensor_reduce(NMAX[:, par, :], PS[:, 2 * par:2 * par + 2, :], AX.X, ALU.max,
                                                negate=True).then_inc(max_ready, 1)

                    def invert(c, par):
                        dve.wait_ge(exp_ready, c + 1)
                        nc.vector.reciprocal(RINV[:, par, :], RSUM[:, par, :]).then_inc(inv_ready, 1)

                    def copy_turned(c, par, i):
                        dve.wait_ge(t_ready, c + 2)
                        nc.vector.tensor_copy(PT[:, par, 0, :, i * P:(i + 1) * P],
                                              PS[:, 4, :].rearrange("p (t q) -> p t q", q=P)).then_inc(ta_copied, 1)

                    def copy_vt(n):
                        dve.wait_ge(vt_ready, n + 1)
                        nc.vector.tensor_copy(VT[:], PS[:, 6, :]).then_inc(vt_copied, 1)

                    def copy_o(n):
                        dve.wait_ge(o_ready, n + 2)
                        nc.vector.tensor_copy(OT[:], PS[:, 7, :]).then_inc(o_copied, 1)

                    def accumulate(n, block_at, first):
                        dve.wait_ge(wo_ready, n + 2)
                        dve.wait_ge(added, n + 1 + AHEAD)
                        acc = ACCT[:, bass.ds(block_at * S, S)]
                        if first:
                            nc.vector.tensor_copy(acc, PS[:, 6, :]).then_inc(added, 1)
                        else:
                            nc.vector.tensor_tensor(acc, PS[:, 6, :], acc, ALU.add).then_inc(added, 1)

                    dve.sem_inc(ta_copied, AHEAD)
                    dve.sem_inc(added, AHEAD)
                    nc.vector.memset(PR[:, 1, :, :], 0.0)
                    nc.vector.memset(PT[:, 1, :, :, :], 0.0)
                    nc.vector.memset(V[:, 1, :, :], 0.0).then_inc(zeros, 1)
                    copy_vt(0)
                    with dve.Fori(0, B) as b:
                        for h in range(PAIRS):
                            n = b * PAIRS + h
                            par = h % 2
                            row_max(4 * n, 0)
                            copy_turned(4 * n - 1, 1 - par, 3)
                            invert(4 * n, 0)
                            row_max(4 * n + 1, 1)
                            copy_vt(n + 1)
                            invert(4 * n + 1, 1)
                            copy_turned(4 * n, par, 0)
                            row_max(4 * n + 2, 0)
                            copy_o(n - 1)
                            invert(4 * n + 2, 0)
                            copy_turned(4 * n + 1, par, 1)
                            row_max(4 * n + 3, 1)
                            accumulate(n - 1, b if h == 0 else b + 1, h == 1)
                            invert(4 * n + 3, 1)
                            copy_turned(4 * n + 2, par, 2)
                    n = B * PAIRS
                    copy_turned(4 * n - 1, 1, 3)
                    copy_o(n - 1)
                    accumulate(n - 1, B, False)

                @block.scalar
                def _(act):
                    def exps(c, par):
                        act.wait_ge(max_ready, c + 1)
                        for s in range(2):
                            last = nc.scalar.activation(PR[:, par, s, :], PS[:, 2 * par + s, :], ACT.Exp,
                                                        bias=NMAX[:, par, s:s + 1], accum_out=RSUM[:, par, s:s + 1])
                        last.then_inc(exp_ready, 1)

                    def copy_g(n, par, s):
                        act.wait_ge((ga_ready, gb_ready)[s], n + 1)
                        nc.scalar.activation(G[:, par, s, :], PS[:, 6 + s, :], ACT.Copy).then_inc((ga_copied, gb_copied)[s], 1)

                    def copy_turned(c, par, i):
                        act.wait_ge(t_ready, c + 2)
                        nc.scalar.activation(PT[:, par, 1, :, i * P:(i + 1) * P],
                                             PS[:, 5, :].rearrange("p (t q) -> p t q", q=P), ACT.Copy).then_inc(tb_copied, 1)

                    def copy_v(n, par):
                        act.wait_ge(v_ready, n + 1)
                        nc.scalar.activation(V[:, par, :, :], PS[:, 7, :].rearrange("p (t q) -> p t q", q=P),
                                             ACT.Copy).then_inc(v_copied, 1)

                    act.sem_inc(tb_copied, AHEAD)
                    act.sem_inc(v_copied, AHEAD)
                    copy_g(0, 0, 0)
                    copy_g(0, 0, 1)
                    copy_v(0, 0)
                    with act.Fori(0, B) as b:
                        for h in range(PAIRS):
                            n = b * PAIRS + h
                            par = h % 2
                            copy_g(n + 1, 1 - par, 0)
                            exps(4 * n, 0)
                            copy_g(n + 1, 1 - par, 1)
                            copy_turned(4 * n - 1, 1 - par, 3)
                            exps(4 * n + 1, 1)
                            copy_turned(4 * n, par, 0)
                            exps(4 * n + 2, 0)
                            copy_turned(4 * n + 1, par, 1)
                            exps(4 * n + 3, 1)
                            copy_v(n + 1, 1 - par)
                            copy_turned(4 * n + 2, par, 2)
                    copy_turned(4 * B * PAIRS - 1, 1, 3)

                @block.gpsimd
                def _(pool):
                    def normalise(c, par):
                        pool.wait_ge(inv_ready, c + 1)
                        for s in range(2):
                            last = nc.gpsimd.tensor_tensor(PR[:, par, s, :], PR[:, par, s, :],
                                                           RINV[:, par, s:s + 1].broadcast_to([P, S]), ALU.mult)
                        last.then_inc(p_ready, 1)

                    pool.sem_inc(p_ready, AHEAD)
                    with pool.Fori(0, 2 * B * PAIRS) as c0_half:
                        c0 = 2 * c0_half
                        for p in range(2):
                            normalise(c0 + p, p)

        with ExitStack() as st:
            def tb(name, shape):
                return st.enter_context(nc.sbuf_tensor(name, shape, F32))

            def tsem(name):
                return st.enter_context(nc.semaphore(name))
            XP = tb("XP", [P, 2, S + 1])
            XD = tb("XD", [P, 2, S])
            XR = tb("XR", [P, 2, 2, S])
            R = tb("R", [P, 2, S])
            K = tb("K", [P, 2, S])
            Y = tb("Y", [P, 2, S])
            X1 = tb("X1", [P, 2, TILES, D])
            links, mixed, rk_ready, r_done, k_done, v_ready, y_done, y_turned, x1_done, x1_kept = map(
                tsem, ("links2", "mixed", "rk_ready", "r_done", "k_done", "v2_ready", "y_done", "y_turned", "x1_done", "x1_kept"))
            k_pos = tsem("k_pos")
            with nc.Block() as block:
                @block.vector
                def _(dve):
                    def mix(b, p):
                        link = Links(dve, links, 2 + 5 * b)
                        link(nc.vector.tensor_copy(XP[:, p, 1:S + 1], XNT[:, bass.ds(b * S, S)]))
                        link(nc.vector.tensor_tensor(XD[:, p, :], XP[:, p, 1:S + 1], XP[:, p, 0:S], ALU.subtract))
                        for k in range(2):
                            last = nc.vector.scalar_tensor_tensor(XR[:, p, k, :], XD[:, p, :], MU[:, k:k + 1], XP[:, p, 0:S],
                                                                  ALU.mult, ALU.add)
                        last.then_inc(mixed, 1)
                        return link

                    def finish(b, p):
                        link = Links(dve, links, 4 + 5 * b)
                        dve.wait_ge(v_ready, b + 1)
                        dve.wait_ge(r_done, b + 1)
                        link(nc.vector.tensor_tensor(Y[:, p, :], PS[:, 4 + p, :], R[:, p, :], ALU.mult))
                        nc.vector.tensor_tensor(Y[:, p, :], Y[:, p, :], ACCT[:, bass.ds((b + 1) * S, S)],
                                                ALU.add).then_inc(y_done, 1)
                        dve.wait_ge(y_turned, b + 1)
                        link(nc.vector.tensor_tensor(X1[:, p, :, :], PS[:, 6 + p, :].rearrange("p (t d) -> p t d", d=D),
                                                     X[:, bass.ds(b * TILES, TILES), :], ALU.add))
                        for t in range(TILES):
                            nc.vector.bn_stats(STATS[:, bass.ds(b * TILES + t, 1), :].rearrange("p a s -> p (a s)"), X1[:, p, t, :])
                        link(nc.vector.tensor_copy(X[:, bass.ds(b * TILES, TILES), :], X1[:, p, :, :]))

                    link = Links(dve, links)
                    link(nc.vector.memset(XP[:, 0, 0:1], 0.0))
                    link(nc.vector.memset(XP[:, 1, 0:1], 0.0))
                    with dve.Fori(0, B // 2) as b0_half:
                        b0 = 2 * b0_half
                        for p in range(2):
                            mix(b0 + p, p)
                            finish(b0 + p, p)

                @block.tensor
                def _(pe):
                    with pe.Fori(0, B // 2) as b0_half:
                        b0 = 2 * b0_half
                        for p in range(2):
                            b = b0 + p
                            pe.wait_ge(mixed, b + 1)
                            for k in range(2):
                                last = nc.tensor.matmul(PS[:, 2 * p + k, :], WR_T[:, k, :], XR[:, p, k, :], start=True, stop=True)
                            last.then_inc(rk_ready, 1)
                            pe.wait_ge(k_done, b + 1)
                            nc.tensor.matmul(PS[:, 4 + p, :], WR_T[:, 2, :], K[:, p, :], start=True, stop=True).then_inc(v_ready, 1)
                            pe.wait_ge(y_done, b + 1)
                            for t in range(TILES):
                                last = nc.tensor.transpose(PS[:, 6 + p, t * P:(t + 1) * P], Y[:, p, t * P:(t + 1) * P], ident[:])
                            last.then_inc(y_turned, 1)

                @block.scalar
                def _(act):
                    with act.Fori(0, B // 2) as b0_half:
                        b0 = 2 * b0_half
                        for p in range(2):
                            b = b0 + p
                            act.wait_ge(rk_ready, b + 1)
                            nc.scalar.activation(K[:, p, :], PS[:, 2 * p + 1, :], ACT.Relu).then_inc(k_pos, 1)
                            nc.scalar.activation(R[:, p, :], PS[:, 2 * p, :], ACT.Sigmoid).then_inc(r_done, 1)
                            act.wait_ge(k_pos, b + 1)
                            nc.scalar.activation(K[:, p, :], K[:, p, :], ACT.Square).then_inc(k_done, 1)

        layernorm_stage("2", False, True)

        with ExitStack() as st:
            def tb(name, shape):
                return st.enter_context(nc.sbuf_tensor(name, shape, F32))

            def tsem(name):
                return st.enter_context(nc.semaphore(name))
            SCT = tb("SCT", [B * E, S])
            LEFT = tb("LEFT", [B * E, S])
            TOP = tb("TOP", [B * E, 8])
            LAST = tb("LAST", [B * E, 8])
            GATE = tb("GATE", [B * E, S])
            turned, links, gated, stored = map(tsem, ("sc_turned", "links3", "gated", "gate_stored"))
            with nc.Block() as block:
                @block.tensor
                def _(pe):
                    for t in range(TILES):
                        last = nc.tensor.transpose(PS[0:B * E, 0, t * P:(t + 1) * P], SC[:, t, :], ident[:])
                    last.then_inc(turned, 1)

                @block.vector
                def _(dve):
                    link = Links(dve, links)
                    dve.wait_ge(turned, 1)
                    nc.vector.tensor_copy(SCT[:], PS[0:B * E, 0, :])
                    link(nc.vector.tensor_copy(LEFT[:], PS[0:B * E, 0, :]))
                    full, rest = divmod(CAPACITY, 8)
                    for _ in range(full):
                        link(nc.vector.max(TOP[:], LEFT[:]))
                        link(nc.vector.match_replace(LEFT[:], TOP[:], LEFT[:], -1.0))
                    if rest:
                        link(nc.vector.memset(LAST[:], -1.0))
                        link(nc.vector.max(TOP[:], LEFT[:]))
                        link(nc.vector.tensor_copy(LAST[:, 0:rest], TOP[:, 0:rest]))
                        link(nc.vector.match_replace(LEFT[:], LAST[:], LEFT[:], -1.0))
                    nc.vector.scalar_tensor_tensor(GATE[:], LEFT[:], 0.0, SCT[:], ALU.is_lt, ALU.mult).then_inc(gated, 1)

                @block.sync
                def _(sp):
                    sp.wait_ge(gated, 1)
                    sp.dma_start(gate_dram, GATE[:]).then_inc(stored, 16)
                    sp.wait_ge(stored, 16)

        with ExitStack() as st:
            def tb(name, shape):
                return st.enter_context(nc.sbuf_tensor(name, shape, F32))

            def tsem(name):
                return st.enter_context(nc.semaphore(name))
            QK = tb("QK", [P, 2 * FT, S])
            SQ = tb("SQ", [P, 2 * FT, S])
            QN = tb("QN", [P, FT, S])
            KN = tb("KN", [P, FT, S])
            KH = tb("KH", [P, HPT, FT, S])
            VT1 = tb("VT1", [P, S])
            V1 = tb("V1", [P, TILES, H1, SLOT])
            ONES = tb("ONES", [P, SLOT])
            A = tb("A", [P, 4, TILES, S])
            DEN = tb("DEN", [P, 2, S])
            YT = tb("YT", [P, 2, S])
            EPS = tb("EPS", [P, 2])
            links, zeros = tsem("links4"), tsem("zeros4")
            qk_ready, sq_ready, var_ready, root_ready, heads_ready, keys_ready = map(
                tsem, ("qk4", "sq4", "var4", "root4", "heads4", "keys4"))
            vt_ready, vt_copied, v_ready, v_copied = map(tsem, ("vt4", "vtc4", "v4", "vc4"))
            sc_ready, sq_done, masked, nd_ready, den_ready, y_ready, wo_ready, added = map(
                tsem, ("sc4", "sqd4", "masked4", "nd4", "den4", "y4", "wo4", "added4"))
            LENS = [S - t * P for t in range(TILES)]
            with nc.Block() as block:
                @block.tensor
                def _(pe):
                    pe.sem_inc(nd_ready, AHEAD)
                    with pe.Fori(0, B) as b:
                        xb = XNT[:, bass.ds(b * S, S)]
                        pe.wait_ge(zeros, 1)
                        pe.wait_ge(sq_done, b * H1 * TILES + AHEAD)
                        for f in range(2 * FT):
                            last = nc.tensor.matmul(PS[:, f, :], WQK_T[:, f, :], xb, start=True, stop=True)
                        last.then_inc(qk_ready, 1)
                        nc.tensor.matmul(PS[:, 4, :], WVO_T[:, 0, :], xb, start=True, stop=True).then_inc(vt_ready, 1)
                        pe.wait_ge(sq_ready, b + 1)
                        for f in range(2 * FT):
                            last = nc.tensor.matmul(PS[:, f, :], block_mean[:], SQ[:, f, :], start=True, stop=True)
                        last.then_inc(var_ready, 1)
                        pe.wait_ge(vt_copied, b + 1)
                        for t in range(TILES):
                            last = nc.tensor.transpose(PS[:, 5, t * P:(t + 1) * P], VT1[:, t * P:(t + 1) * P], ident[:])
                        last.then_inc(v_ready, 1)
                        pe.wait_ge(heads_ready, b + 1)
                        pe.wait_ge(v_copied, b + 1)

                        def scores(h):
                            f, r = divmod(h, HPT)
                            for t in range(TILES):
                                if t == 0:
                                    pe.wait_ge(sq_done, (b * H1 + h) * TILES + AHEAD)
                                last = nc.tensor.matmul(PS[:, t, t * P:S], KH[:, r, f, t * P:(t + 1) * P], QN[:, f, t * P:S],
                                                        start=True, stop=True)
                                last.then_inc(sc_ready, 1)

                        def outputs(r):
                            pe.wait_ge(masked, b * H1 + HPG * (r + 1))
                            pe.wait_ge(y_ready, b * GROUPS + r + AHEAD)
                            for t in range(TILES):
                                for g in range(HPG):
                                    nc.tensor.matmul(PS[SLOT * g:SLOT * (g + 1), 6, t * P:S], V1[:, t, HPG * r + g, :],
                                                     A[:, g, t, t * P:S], start=(t == 0), stop=(t == TILES - 1),
                                                     skip_group_check=True)
                            for t in range(TILES):
                                for g in range(HPG):
                                    last = nc.tensor.matmul(PS[SLOT * g:SLOT * (g + 1), 7, t * P:S], ONES[:],
                                                            A[:, g, t, t * P:S], start=(t == 0), stop=(t == TILES - 1),
                                                            skip_group_check=True)
                            last.then_inc(nd_ready, 1)

                        def project_out(r):
                            pe.wait_ge(y_ready, b * GROUPS + r + 1 + AHEAD)
                            last = nc.tensor.matmul(PS[:, 4, :], WO_PAD[:, r, :], YT[:, r % 2, :], start=(r == 0),
                                                    stop=(r == GROUPS - 1), skip_group_check=True)
                            if r == GROUPS - 1:
                                last.then_inc(wo_ready, 1)

                        for r in range(GROUPS):
                            for g in range(HPG):
                                scores(HPG * r + g)
                            outputs(r)
                            if r >= 1:
                                project_out(r - 1)
                        project_out(GROUPS - 1)
                        pe.wait_ge(added, b + 1)

                @block.scalar
                def _(act):
                    act.sem_inc(sq_done, AHEAD)
                    act.wait_ge(zeros, 1)
                    with act.Fori(0, B) as b:
                        act.wait_ge(qk_ready, b + 1)
                        ps = PS[:, 0:4, :].rearrange("p f n -> p (f n)")
                        nc.scalar.activation(SQ[:].rearrange("p f n -> p (f n)"), ps, ACT.Square)
                        nc.scalar.activation(QK[:].rearrange("p f n -> p (f n)"), ps, ACT.Copy).then_inc(sq_ready, 1)
                        act.wait_ge(var_ready, b + 1)
                        nc.scalar.activation(SQ[:].rearrange("p f n -> p (f n)"), ps, ACT.Sqrt,
                                             bias=EPS[:, 0:1]).then_inc(root_ready, 1)
                        for h in range(H1):
                            if h % HPG == 0:
                                act.wait_ge(nd_ready, b * GROUPS + h // HPG + AHEAD)
                            for t in range(TILES):
                                act.wait_ge(sc_ready, (b * H1 + h) * TILES + t + 1)
                                nc.scalar.activation(A[:, h % 4, t, t * P:S], PS[:, t, t * P:S], ACT.Square,
                                                     scale=FEAT ** -0.5).then_inc(sq_done, 1)
                            if h % HPG == 3:
                                r = h // HPG
                                act.wait_ge(nd_ready, b * GROUPS + r + 1 + AHEAD)
                                act.wait_ge(y_ready, b * GROUPS + r + AHEAD)
                                nc.scalar.activation(DEN[:, r % 2, :], PS[:, 7, :], ACT.Identity, bias=EPS[:, 1:2]).then_inc(den_ready, 1)

                @block.vector
                def _(dve):
                    dve.sem_inc(y_ready, AHEAD)
                    nc.vector.memset(EPS[:, 0:1], LN_EPS)
                    nc.vector.memset(EPS[:, 1:2], DEN_EPS)
                    nc.vector.memset(ONES[:], 1.0)
                    nc.vector.memset(V1[:], 0.0).then_inc(zeros, 1)
                    dve.wait_ge(zeros, 1)
                    PER_B = 3 + GROUPS
                    with dve.Fori(0, B) as b:
                        link = Links(dve, links, b * PER_B)
                        dve.wait_ge(vt_ready, b + 1)
                        nc.vector.tensor_copy(VT1[:], PS[:, 4, :]).then_inc(vt_copied, 1)
                        dve.wait_ge(root_ready, b + 1)
                        link(nc.vector.reciprocal(SQ[:].rearrange("p f n -> p (f n)"), SQ[:].rearrange("p f n -> p (f n)")))
                        link(nc.vector.tensor_tensor(QN[:], QK[:, 0:FT, :], SQ[:, 0:FT, :], ALU.mult))
                        link(nc.vector.tensor_tensor(KN[:], QK[:, FT:2 * FT, :], SQ[:, FT:2 * FT, :], ALU.mult))
                        nc.vector.tensor_scalar(QN[:], QN[:], GB[:, 0:1], GB[:, 1:2], ALU.mult, ALU.add)
                        for r in range(HPT):
                            last = nc.vector.tensor_scalar(KH[:, r, :, :], KN[:], GM[:, 0, r:r + 1], GM[:, 1, r:r + 1],
                                                           ALU.mult, ALU.add)
                        last.then_inc(heads_ready, 1)
                        dve.wait_ge(v_ready, b + 1)
                        for t in range(TILES):
                            last = nc.vector.tensor_copy(V1[:, t, :, 0:HD],
                                                         PS[:, 5, t * P:(t + 1) * P].rearrange("p (h d) -> p h d", d=HD))
                        last.then_inc(v_copied, 1)
                        for r in range(GROUPS):
                            dve.wait_ge(den_ready, b * GROUPS + r + 1)
                            link(nc.vector.reciprocal(DEN[:, r % 2, :], DEN[:, r % 2, :]))
                            nc.vector.tensor_tensor(YT[:, r % 2, :], PS[:, 6, :], DEN[:, r % 2, :], ALU.mult).then_inc(y_ready, 1)
                        dve.wait_ge(wo_ready, b + 1)
                        nc.vector.tensor_copy(ACCT[:, bass.ds((b + 1) * S, S)], PS[:, 4, :]).then_inc(added, 1)

                @block.gpsimd
                def _(pool):
                    with pool.Fori(0, B) as b:
                        for h in range(H1):
                            pool.wait_ge(sq_done, (b * H1 + h + 1) * TILES + AHEAD)
                            diag = bass.AP(A[:, h % 4, 0, 0:P].tensor, A[:, h % 4, 0, 0:P].offset,
                                           [A[:].ap[0], [S + P, TILES], [1, P]])
                            nc.gpsimd.tensor_tensor(diag, diag, causal[:], ALU.mult).then_inc(masked, 1)

        with ExitStack() as st:
            def tb(name, shape):
                return st.enter_context(nc.sbuf_tensor(name, shape, F32))

            def tsem(name):
                return st.enter_context(nc.semaphore(name))
            W1 = tb("W1", [P, 2, HID])
            W2 = tb("W2", [P, 2, HT, D])
            BC = tb("BC", [P, 2, HT + 1])
            HB = tb("HB", [P, 2, HT, S])
            GT = tb("GT", [P, 2, S])
            TMP = tb("TMP", [P, 2, S])
            w_sem = [tsem(f"w_loaded{k}") for k in range(2)]
            g_sem = [tsem(f"gates_loaded{k}") for k in range(2)]
            b_ready, h_ready, gelu_done, y_ready, scaled, added, links = map(
                tsem, ("b_ready", "h5", "gelu5", "y5", "scaled5", "added5", "links5"))
            NSTEP = B * E
            with nc.Block() as block:
                @block.sync
                def _(sp):
                    with sp.Fori(0, E // 2) as e0_half:
                        e0 = 2 * e0_half
                        for pe_ in range(2):
                            e = e0 + pe_
                            sp.dma_start(W1[:, pe_, :], w1[bass.ds(e, 1)].rearrange("a d n -> (a d) n")).then_inc(w_sem[pe_], 16)
                            sp.dma_start(W2[:, pe_, :, :], w2[bass.ds(e, 1)].rearrange("a (j p) d -> (a p) j d", p=P)).then_inc(w_sem[pe_], 16)
                            with sp.Fori(0, B // 2) as b0_half:
                                b0 = 2 * b0_half
                                for p in range(2):
                                    n = e * B + b0 + p
                                    sp.wait_ge(scaled, n + AHEAD)
                                    sp.dma_start(GT[:, p, :], gate_dram[bass.ds((b0 + p) * E + e, 1), :].broadcast_to([P, S])
                                                 ).then_inc(g_sem[p], 16)

                @block.tensor
                def _(pe):
                    with pe.Fori(0, E // 2) as e0_half:
                        e0 = 2 * e0_half
                        for pe_ in range(2):
                            e = e0 + pe_
                            with pe.Fori(0, B // 2) as b0_half:
                                b0 = 2 * b0_half
                                for p in range(2):
                                    b = b0 + p
                                    n = e * B + b
                                    pe.wait_ge(w_sem[pe_], e0 * 16 + 32)
                                    pe.wait_ge(gelu_done, n * HT + AHEAD)
                                    for j in range(HT):
                                        nc.tensor.matmul(PS[:, j, :], W1[:, pe_, j * P:(j + 1) * P], XNT[:, bass.ds(b * S, S)],
                                                         start=True, stop=True).then_inc(h_ready, 1)
                                    for j in range(HT):
                                        pe.wait_ge(gelu_done, n * HT + j + 1 + AHEAD)
                                        if j == 0:
                                            pe.wait_ge(scaled, n + AHEAD)
                                        last = nc.tensor.matmul(PS[:, 4 + p, :], W2[:, pe_, j, :], HB[:, p, j, :],
                                                                start=(j == 0), stop=(j == HT - 1))
                                    last.then_inc(y_ready, 1)

                @block.scalar
                def _(act):
                    act.sem_inc(gelu_done, AHEAD)
                    with act.Fori(0, E // 2) as e0_half:
                        e0 = 2 * e0_half
                        for pe_ in range(2):
                            e = e0 + pe_
                            act.wait_ge(b_ready, e + 1)
                            with act.Fori(0, B // 2) as b0_half:
                                b0 = 2 * b0_half
                                for p in range(2):
                                    n = e * B + b0 + p
                                    for j in range(HT):
                                        act.wait_ge(h_ready, n * HT + j + 1)
                                        nc.scalar.activation(HB[:, p, j, :], PS[:, j, :], ACT.Gelu,
                                                             bias=BC[:, pe_, j:j + 1]).then_inc(gelu_done, 1)

                @block.vector
                def _(dve):
                    dve.sem_inc(scaled, AHEAD)
                    dve.sem_inc(added, AHEAD)
                    with dve.Fori(0, E // 2) as e0_half:
                        e0 = 2 * e0_half
                        for pe_ in range(2):
                            e = e0 + pe_
                            nc.vector.tensor_copy(BC[:, pe_, 0:HT], B1_T[:, bass.ds(e * HT, HT)])
                            nc.vector.tensor_copy(BC[:, pe_, HT:HT + 1], B2_T[:, bass.ds(e, 1)]).then_inc(b_ready, 1)
                            with dve.Fori(0, B // 2) as b0_half:
                                b0 = 2 * b0_half
                                for p in range(2):
                                    b = b0 + p
                                    n = e * B + b
                                    dve.wait_ge(b_ready, e + 1)
                                    dve.wait_ge(y_ready, n + 1)
                                    dve.wait_ge(g_sem[p], (n - p) * 8 + 16)
                                    dve.wait_ge(added, n + AHEAD)
                                    nc.vector.scalar_tensor_tensor(TMP[:, p, :], PS[:, 4 + p, :], BC[:, pe_, HT:HT + 1], GT[:, p, :],
                                                                   ALU.add, ALU.mult).then_inc(scaled, 1)
                                    dve.wait_ge(scaled, n + 1 + AHEAD)
                                    acc = ACCT[:, bass.ds((b + 1) * S, S)]
                                    nc.vector.tensor_tensor(acc, acc, TMP[:, p, :], ALU.add).then_inc(added, 1)

        with ExitStack() as st:
            def tb(name, shape):
                return st.enter_context(nc.sbuf_tensor(name, shape, F32))

            def tsem(name):
                return st.enter_context(nc.semaphore(name))
            YC = tb("YC", [P, 2, S])
            RES = tb("RES", [P, 2, TILES, D])
            copied, turned, summed = map(tsem, ("copied6", "turned6", "summed6"))
            out_sem = [tsem(f"stored6_{p}") for p in range(2)]
            with nc.Block() as block:
                @block.vector
                def _(dve):
                    with dve.Fori(0, B // 2) as b0_half:
                        b0 = 2 * b0_half
                        for p in range(2):
                            b = b0 + p
                            nc.vector.tensor_copy(YC[:, p, :], ACCT[:, bass.ds((b + 1) * S, S)]).then_inc(copied, 1)
                        for p in range(2):
                            b = b0 + p
                            dve.wait_ge(turned, b + 1)
                            dve.wait_ge(out_sem[p], b0 * 8 + 16)
                            nc.vector.tensor_tensor(RES[:, p, :, :], PS[:, p, :].rearrange("p (t d) -> p t d", d=D),
                                                    X[:, bass.ds(b * TILES, TILES), :], ALU.add).then_inc(summed, 1)

                @block.tensor
                def _(pe):
                    with pe.Fori(0, B // 2) as b0_half:
                        b0 = 2 * b0_half
                        for p in range(2):
                            b = b0 + p
                            pe.wait_ge(copied, b + 1)
                            for t in range(TILES):
                                last = nc.tensor.transpose(PS[:, p, t * P:(t + 1) * P], YC[:, p, t * P:(t + 1) * P], ident[:])
                            last.then_inc(turned, 1)

                @block.sync
                def _(sp):
                    for p in range(2):
                        sp.sem_inc(out_sem[p], 16)
                    with sp.Fori(0, B // 2) as b0_half:
                        b0 = 2 * b0_half
                        for p in range(2):
                            b = b0 + p
                            sp.wait_ge(summed, b + 1)
                            sp.dma_start(out[bass.ds(b, 1)].rearrange("a (t p) d -> p (a t) d", p=P), RES[:, p, :, :]
                                         ).then_inc(out_sem[p], 16)
                    for p in range(2):
                        sp.wait_ge(out_sem[p], B // 2 * 16 + 16)


_INS = ['L0_attn_x', 'L0_attn_kernel', 'L0_attn_WO', 'L0_ffn_W_r', 'L0_ffn_W_k', 'L0_ffn_W_v', 'L0_ffn_mu_r',
        'L0_ffn_mu_k', 'L1_attn_Wq', 'L1_attn_Wk', 'L1_attn_Wv', 'L1_attn_Wo', 'L1_attn_gamma', 'L1_attn_beta',
        'L1_ffn_router_w', 'L1_ffn_w1', 'L1_ffn_b1', 'L1_ffn_w2', 'L1_ffn_b2']


def kernel(**inputs):
    import numpy as _np
    import concourse.bacc as _bacc
    from concourse import mybir as _mybir
    from concourse.bass_utils import run_bass_kernel_spmd as _run

    nc = _bacc.Bacc("TRN2", target_bir_lowering=False, num_devices=1)
    arrays, args = {}, []
    for name in _INS:
        a = _np.ascontiguousarray(inputs[name])
        arrays[f"in_{name}_dram"] = a
        args.append(nc.dram_tensor(f"in_{name}_dram", a.shape, _mybir.dt.from_np(a.dtype), kind="ExternalInput").ap())
    args.append(nc.dram_tensor("out_dram", (8, 512, 128), _mybir.dt.float32, kind="ExternalOutput").ap())
    prob_d2_kernel(nc, *args)
    r = _run(nc, [arrays], core_ids=[0])
    return r.results[0]["out_dram"]
```

```python
import concourse.bass as bass
from concourse import mybir
from contextlib import ExitStack

F32 = mybir.dt.float32
F32R = mybir.dt.float32r
ALU = mybir.AluOpType
ACT = mybir.ActivationFunctionType
AX = mybir.AxisListType

P = 128
B, S, D = 8, 512, 128
TILES = S // P
NT = B * TILES
H, DH = 16, 64
PAIRS = H // 2
SCALE = 1.0 / (DH * DH * H)
H1, FEAT, HD = 16, 16, 8
FT = H1 * FEAT // P
HPT = P // FEAT
SLOT = 32
GROUPS = H1 * SLOT // P
HPG = P // SLOT
E, HID = 8, 512
HT = HID // P
CAPACITY = max(1, int(S * 2.0 / E) + 1)
LN_EPS = 1e-05
DEN_EPS = 1e-05


AHEAD = 1


class Links:

    def __init__(self, eng, sem, base=0):
        self.eng, self.sem, self.base, self.n = eng, sem, base, 0

    def __call__(self, ins):
        self.n += 1
        ins.then_inc(self.sem, 1)
        self.eng.wait_ge(self.sem, self.base + self.n)


def split_lo(nc, lo, src, hi):
    return nc.vector.tensor_tensor(lo, src, hi.bitcast(F32), ALU.subtract)


def product(nc, out, w, x, start=True, stop=True):
    (wh, wl), (xh, xl) = w, x
    nc.tensor.matmul(out, wl, xh, start=start, stop=False)
    nc.tensor.matmul(out, wh, xh, start=False, stop=False)
    return nc.tensor.matmul(out, wh, xl, start=False, stop=stop)


def prob_d2_kernel(nc, x, kern, wo0, w_r, w_k, w_v, mu_r, mu_k, wq1, wk1, wv1, wo1, gamma, beta,
                   router, w1, b1, w2, b2, out):
    gate_dram = nc.dram_tensor("gate_scratch", [B * E, S], F32, kind="Internal").ap()
    ctx = ExitStack()
    with ctx:
        def sb(name, shape, dt=F32):
            return ctx.enter_context(nc.sbuf_tensor(name, shape, dt))

        def sem(name):
            return ctx.enter_context(nc.semaphore(name))

        X = sb("X", [P, NT, D])
        XH = sb("XH", [P, (B + 1) * S], F32R)
        XL = sb("XL", [P, (B + 1) * S], F32R)
        ACCT = sb("ACCT", [P, (B + 1) * S])
        ident = sb("ident", [P, P])
        causal = sb("causal", [P, P])
        block_mean = sb("block_mean", [P, P])
        head_mask = sb("head_mask", [P, HPT])
        WVO_T = sb("WVO_T", [P, 2, P])
        WV1H = sb("WV1H", [P, P], F32R)
        WV1L = sb("WV1L", [P, P], F32R)
        WQKH = sb("WQKH", [P, 2 * FT, P], F32R)
        WQKL = sb("WQKL", [P, 2 * FT, P], F32R)
        WO_PAD = sb("WO_PAD", [P, GROUPS, D])
        RT = sb("RT", [P, E])
        B1_T = sb("B1_T", [P, (E + 1) * HT])
        B2_T = sb("B2_T", [P, E + 1])
        MU = sb("MU", [P, 2])
        GB = sb("GB", [P, 2])
        SC = sb("SC", [P, TILES, B * E])
        STATS = sb("STATS", [P, NT, 6])
        MEAN = sb("MEAN", [P, NT])
        RSTD = sb("RSTD", [P, NT])
        LN = sb("LN", [P, 4, NT])

        first_layer = ctx.enter_context(ExitStack())

        def sb1(name, shape, dt=F32):
            return first_layer.enter_context(nc.sbuf_tensor(name, shape, dt))

        MH = sb1("MH", [P, 2, PAIRS, P], F32R)
        ML = sb1("ML", [P, 2, PAIRS, P], F32R)
        WVH = sb1("WVH", [P, H * DH], F32R)
        WVL = sb1("WVL", [P, H * DH], F32R)
        WO = sb1("WO", [P, PAIRS, D])
        WR_T = sb1("WR_T", [P, 3, P])

        def batch(b):
            return XH[:, bass.ds(b * S, S)], XL[:, bass.ds(b * S, S)]

        PS = ctx.enter_context(nc.psum_tensor("PS", [P, 8, 512], F32))

        with ExitStack() as st:
            def tb(name, shape, dt=F32):
                return st.enter_context(nc.sbuf_tensor(name, shape, dt))
            WVS = tb("WVS", [P, H * DH])
            WQS = tb("WQS", [P, H, DH])
            WKS = tb("WKS", [P, H, DH])
            WQT = tb("WQT", [P, PAIRS, P])
            WKT = tb("WKT", [P, PAIRS, P])
            centre = tb("centre", [P, P])
            RAW = tb("RAW", [P, 5, P])
            RAW1 = tb("RAW1", [P, 2 * FT, P])
            RAWR = tb("RAWR", [E, P])
            RAWB1 = tb("RAWB1", [E * HT, P])
            RAWB2 = tb("RAWB2", [E, P])
            loaded = st.enter_context(nc.semaphore("loaded"))
            x_loaded = [st.enter_context(nc.semaphore(f"x_loaded{q}")) for q in range(4)]
            consts = st.enter_context(nc.semaphore("consts"))
            zeroed = st.enter_context(nc.semaphore("zeroed"))
            transposed = st.enter_context(nc.semaphore("transposed"))
            copied = st.enter_context(nc.semaphore("copied"))
            padded = st.enter_context(nc.semaphore("padded"))
            v_links = st.enter_context(nc.semaphore("v_links0"))
            g_links = st.enter_context(nc.semaphore("g_links0"))
            with nc.Block() as block:
                @block.scalar
                def _(act):
                    for q in range(4):
                        act.dma_start(X[:, q * NT // 4:(q + 1) * NT // 4, :],
                                      x.rearrange("b (t p) d -> p (b t) d", p=P)[:, q * NT // 4:(q + 1) * NT // 4, :]
                                      ).then_inc(x_loaded[q], 16)

                @block.sync
                def _(sp):
                    def load(dst, src):
                        sp.dma_start(dst, src).then_inc(loaded, 16)
                    load(WQS[:], kern[0].rearrange("h m d -> m h d"))
                    load(WKS[:], kern[1].rearrange("h m d -> m h d"))
                    load(WVS[:].rearrange("m (h d) -> m h d", h=H), kern[2].rearrange("h m d -> m h d"))
                    wo_v = wo0[0].rearrange("(d j s) m -> s d j m", j=PAIRS, s=2)
                    for s in range(2):
                        load(WO[DH * s:DH * (s + 1), :, :], wo_v[s])
                    for k, w in enumerate((w_r, w_k, w_v, wv1, wo1)):
                        load(RAW[:, k, :], w)
                    load(RAW1[:, 0:FT, :], wq1.rearrange("(f p) c -> p f c", p=P))
                    load(RAW1[:, FT:2 * FT, :], wk1.rearrange("(f p) c -> p f c", p=P))
                    load(RAWR[:], router)
                    load(RAWB1[:], b1.rearrange("e (j p) -> (e j) p", p=P))
                    load(RAWB2[:], b2)
                    load(MU[:, 0:1], mu_r.rearrange("(p a) -> p a", a=1))
                    load(MU[:, 1:2], mu_k.rearrange("(p a) -> p a", a=1))
                    for k, w in enumerate((gamma, beta)):
                        g = w.rearrange("(p a) -> p a", a=1)
                        for r in range(HPT):
                            sp.dma_start(GB[FEAT * r:FEAT * (r + 1), k:k + 1], g).then_inc(loaded, 16)
                    sp.wait_ge(zeroed, 1)
                    sp.wait_ge(copied, 1)
                    for r in range(GROUPS):
                        for g in range(HPG):
                            row = HD * (HPG * r + g)
                            sp.dma_start(WO_PAD[SLOT * g:SLOT * g + HD, r, :], WVO_T[row:row + HD, 1, :]).then_inc(padded, 16)
                    sp.wait_ge(padded, 16 * GROUPS * HPG)

                LOADS = (17 + 2 * HPT) * 16

                @block.gpsimd
                def _(pool):
                    link = Links(pool, g_links)
                    nc.gpsimd.memset(WO_PAD[:], 0.0).then_inc(zeroed, 1)
                    link(nc.gpsimd.memset(ident[:], 0.0))
                    link(nc.gpsimd.affine_select(out=ident[:], in_=ident[:], compare_op=ALU.not_equal, fill=1.0,
                                                 base=0, pattern=[[-1, P]], channel_multiplier=1))
                    bm = block_mean[:].rearrange("p (g j) -> p g j", j=FEAT)
                    link(nc.gpsimd.memset(block_mean[:], 1.0 / FEAT))
                    link(nc.gpsimd.affine_select(out=bm, in_=bm, compare_op=ALU.is_ge, fill=0.0,
                                                 base=0, pattern=[[-FEAT, HPT], [0, FEAT]], channel_multiplier=1))
                    link(nc.gpsimd.affine_select(out=bm, in_=bm, compare_op=ALU.is_ge, fill=0.0,
                                                 base=FEAT - 1, pattern=[[FEAT, HPT], [0, FEAT]], channel_multiplier=-1))
                    link(nc.gpsimd.memset(head_mask[:], 1.0))
                    link(nc.gpsimd.affine_select(out=head_mask[:], in_=head_mask[:], compare_op=ALU.is_ge, fill=0.0,
                                                 base=0, pattern=[[-FEAT, HPT]], channel_multiplier=1))
                    link(nc.gpsimd.affine_select(out=head_mask[:], in_=head_mask[:], compare_op=ALU.is_ge, fill=0.0,
                                                 base=FEAT - 1, pattern=[[FEAT, HPT]], channel_multiplier=-1))
                    link(nc.gpsimd.memset(causal[:], 1.0))
                    link(nc.gpsimd.affine_select(out=causal[:], in_=causal[:], compare_op=ALU.is_ge, fill=0.0,
                                                 base=0, pattern=[[1, P]], channel_multiplier=-1))
                    nc.gpsimd.tensor_tensor(centre[:], ident[:], block_mean[:], ALU.subtract).then_inc(consts, 1)

                @block.tensor
                def _(pe):
                    pe.wait_ge(consts, 1)
                    pe.wait_ge(loaded, LOADS)
                    for k in range(3):
                        nc.tensor.transpose(PS[:, 0, k * P:(k + 1) * P], RAW[:, k, :], ident[:])
                    for k in range(2):
                        nc.tensor.transpose(PS[:, 1, k * P:(k + 1) * P], RAW[:, 3 + k, :], ident[:])
                    nc.tensor.transpose(PS[:, 1, 256:256 + E], RAWR[:], ident[0:E, 0:E])
                    nc.tensor.transpose(PS[:, 1, 288:288 + E * HT], RAWB1[:], ident[0:E * HT, 0:E * HT])
                    nc.tensor.transpose(PS[:, 1, 352:352 + E], RAWB2[:], ident[0:E, 0:E])
                    for f in range(2 * FT):
                        nc.tensor.matmul(PS[:, 2, f * P:(f + 1) * P], RAW1[:, f, :], centre[:], start=True, stop=True)
                    for w, bank in ((WQS, 3), (WKS, 5)):
                        for j in range(PAIRS):
                            last = nc.tensor.transpose(PS[:, bank + j // 4, (j % 4) * P:(j % 4 + 1) * P],
                                                       w[:, 2 * j:2 * j + 2, :].rearrange("p s d -> p (s d)"), ident[:])
                    last.then_inc(transposed, 1)
                    pe.wait_ge(copied, 2)
                    for s in range(2):
                        for j in range(PAIRS):
                            last = nc.tensor.matmul(PS[:, 2 * s + j // 4, (j % 4) * P:(j % 4 + 1) * P],
                                                    WQT[DH * s:DH * (s + 1), j, :], WKT[DH * s:DH * (s + 1), j, :],
                                                    start=True, stop=True)
                    last.then_inc(transposed, 1)

                @block.vector
                def _(dve):
                    link = Links(dve, v_links)
                    nc.vector.memset(XH[:, B * S:(B + 1) * S].bitcast(F32), 0.0)
                    nc.vector.memset(XL[:, B * S:(B + 1) * S].bitcast(F32), 0.0)
                    nc.vector.memset(ACCT[:, 0:S], 0.0)
                    for t in range(NT):
                        if t % (NT // 4) == 0:
                            dve.wait_ge(x_loaded[t // (NT // 4)], 16)
                        nc.vector.bn_stats(STATS[:, t, :], X[:, t, :])
                    dve.wait_ge(loaded, LOADS)
                    link(nc.vector.tensor_copy(WVH[:], WVS[:]))
                    split_lo(nc, WVL[:], WVS[:], WVH[:])
                    dve.wait_ge(transposed, 1)
                    nc.vector.tensor_copy(WQT[:].rearrange("p j n -> p (j n)"), PS[:, 3:5, :].rearrange("p a n -> p (a n)"))
                    nc.vector.tensor_copy(WKT[:].rearrange("p j n -> p (j n)"), PS[:, 5:7, :].rearrange("p a n -> p (a n)"))
                    nc.vector.tensor_copy(WVO_T[:].rearrange("p k n -> p (k n)"), PS[:, 1, 0:256])
                    nc.vector.tensor_copy(WR_T[:].rearrange("p k n -> p (k n)"), PS[:, 0, 0:384])
                    nc.vector.tensor_copy(RT[:], PS[:, 1, 256:256 + E])
                    nc.vector.memset(B1_T[:, E * HT:], 0.0)
                    nc.vector.memset(B2_T[:, E:], 0.0)
                    nc.vector.tensor_copy(B1_T[:, 0:E * HT], PS[:, 1, 288:288 + E * HT])
                    nc.vector.tensor_copy(B2_T[:, 0:E], PS[:, 1, 352:352 + E])
                    link(nc.vector.tensor_copy(WV1H[:], PS[:, 1, 0:P]))
                    split_lo(nc, WV1L[:], PS[:, 1, 0:P], WV1H[:])
                    qk = PS[:, 2, :].rearrange("p (f n) -> p f n", n=P)
                    link(nc.vector.tensor_copy(WQKH[:], qk))
                    split_lo(nc, WQKL[:], qk, WQKH[:]).then_inc(copied, 2)
                    dve.wait_ge(transposed, 2)
                    m = PS[:, 0:4, :].rearrange("p a n -> p (a n)").rearrange("p (s j n) -> p s j n", s=2, j=PAIRS)
                    link(nc.vector.tensor_scalar(MH[:], m, SCALE, None, ALU.mult))
                    nc.vector.scalar_tensor_tensor(ML[:].rearrange("p s j n -> p (s j n)"),
                                                   PS[:, 0:4, :].rearrange("p a n -> p (a n)"), SCALE,
                                                   MH[:].rearrange("p s j n -> p (s j n)").bitcast(F32), ALU.mult, ALU.subtract)

        def moments(dve, link):
            n = NT
            link(nc.vector.tensor_tensor(LN[:, 0, :], STATS[:, :, 1], STATS[:, :, 4], ALU.add))
            link(nc.vector.tensor_tensor(LN[:, 1, :], STATS[:, :, 1], STATS[:, :, 4], ALU.subtract))
            link(nc.vector.tensor_scalar(MEAN[:], LN[:, 0, :], 0.5, None, ALU.mult))
            link(nc.vector.tensor_tensor(LN[:, 2, :], STATS[:, :, 2], STATS[:, :, 5], ALU.add))
            link(nc.vector.scalar_tensor_tensor(LN[:, 1, :], LN[:, 1, :], 0.25, LN[:, 1, :], ALU.mult, ALU.mult))
            link(nc.vector.scalar_tensor_tensor(LN[:, 2, :], LN[:, 2, :], 1.0 / D, LN[:, 1, :], ALU.mult, ALU.add))
            link(nc.vector.tensor_scalar(LN[:, 2, :], LN[:, 2, :], LN_EPS, None, ALU.add))

        def rstd(dve, link):
            link(nc.vector.reciprocal(LN[:, 0, :], LN[:, 3, :]))
            link(nc.vector.tensor_tensor(LN[:, 0, :], LN[:, 0, :], LN[:, 2, :], ALU.mult))
            link(nc.vector.tensor_tensor(LN[:, 0, :], LN[:, 0, :], LN[:, 3, :], ALU.add))
            link(nc.vector.tensor_scalar(LN[:, 0, :], LN[:, 0, :], 0.5, None, ALU.mult))
            link(nc.vector.reciprocal(RSTD[:], LN[:, 0, :]))

        def layernorm_stage(tag, with_router):
            with ExitStack() as st:
                def tb(name, shape, dt=F32):
                    return st.enter_context(nc.sbuf_tensor(name + tag, shape, dt))

                def tsem(name):
                    return st.enter_context(nc.semaphore(name + tag))
                XS = tb("XS", [P, 2, TILES, D])
                XT = tb("XT", [P, 2, S])
                LG = tb("LG", [P, NT, E])
                LX = tb("LX", [P, NT])
                v_links, var_ready, root_ready = tsem("v_links"), tsem("var"), tsem("root")
                normed, turned, stored, kept, logits, shifted, expd = map(
                    tsem, ("normed", "turned", "stored", "kept", "logits", "shifted", "expd"))
                with nc.Block() as block:
                    @block.scalar
                    def _(act):
                        act.wait_ge(var_ready, 1)
                        nc.scalar.activation(LN[:, 3, :], LN[:, 2, :], ACT.Sqrt).then_inc(root_ready, 1)
                        with act.Fori(0, B // 2) as b0_half:
                            for p in range(2):
                                b = 2 * b0_half + p
                                act.wait_ge(turned, b + 1)
                                nc.scalar.activation(XT[:, p, :], PS[:, p, :], ACT.Copy).then_inc(kept, 1)
                        if with_router:
                            act.wait_ge(shifted, 1)
                            nc.scalar.activation(LG[:], LG[:], ACT.Exp).then_inc(expd, 1)

                    @block.tensor
                    def _(pe):
                        with pe.Fori(0, B // 2) as b0_half:
                            for p in range(2):
                                b = 2 * b0_half + p
                                pe.wait_ge(normed, b + 1)
                                for t in range(TILES):
                                    last = nc.tensor.transpose(PS[:, p, t * P:(t + 1) * P], XS[:, p, t, :], ident[:])
                                last.then_inc(turned, 1)
                            if with_router:
                                for p in range(2):
                                    b = 2 * b0_half + p
                                    pe.wait_ge(kept, b + 1)
                                    for t in range(TILES):
                                        last = nc.tensor.matmul(PS[:, 2, bass.ds((b * TILES + t) * E, E)],
                                                                XT[:, p, t * P:(t + 1) * P], RT[:], start=True, stop=True)
                                    last.then_inc(logits, 1)

                    @block.vector
                    def _(dve):
                        link = Links(dve, v_links)
                        moments(dve, link)
                        nc.vector.tensor_scalar(LN[:, 1, :], LN[:, 1, :], 1.0, None, ALU.mult).then_inc(var_ready, 1)
                        dve.wait_ge(root_ready, 1)
                        rstd(dve, link)
                        before = link.n
                        with dve.Fori(0, B // 2) as b0_half:
                            for p in range(2):
                                b = 2 * b0_half + p
                                if with_router:
                                    dve.wait_ge(logits, b0_half * 2 + AHEAD)
                                for t in range(TILES):
                                    tok = b * TILES + t
                                    last = nc.vector.tensor_scalar(XS[:, p, t, :], X[:, bass.ds(tok, 1), :].rearrange("p a d -> p (a d)"),
                                                                   MEAN[:, bass.ds(tok, 1)], RSTD[:, bass.ds(tok, 1)],
                                                                   ALU.subtract, ALU.mult)
                                last.then_inc(normed, 1)
                            for p in range(2):
                                b = 2 * b0_half + p
                                inner = Links(dve, v_links, before + b)
                                dve.wait_ge(kept, b + 1)
                                hi, lo = batch(b)
                                inner(nc.vector.tensor_copy(hi, XT[:, p, :]))
                                split_lo(nc, lo, XT[:, p, :], hi)
                        if with_router:
                            link.n = before + B
                            dve.wait_ge(logits, B + AHEAD)
                            lg = PS[:, 2, 0:NT * E].rearrange("p (t e) -> p t e", e=E)
                            wide = LX[:].unsqueeze(2).broadcast_to([P, NT, E])
                            link(nc.vector.tensor_reduce(LX[:], lg, AX.X, ALU.max))
                            nc.vector.tensor_tensor(LG[:], lg, wide, ALU.subtract).then_inc(shifted, 1)
                            dve.wait_ge(expd, 1)
                            link(nc.vector.tensor_reduce(LX[:], LG[:], AX.X, ALU.add))
                            link(nc.vector.reciprocal(LX[:], LX[:]))
                            for b in range(B):
                                nc.vector.tensor_tensor(SC[:, :, b * E:(b + 1) * E], LG[:, b * TILES:(b + 1) * TILES, :],
                                                        LX[:, b * TILES:(b + 1) * TILES].unsqueeze(2).broadcast_to([P, TILES, E]),
                                                        ALU.mult)

                    if with_router:
                        @block.sync
                        def _(sp):
                            sp.sem_inc(logits, AHEAD)

        layernorm_stage("1", False)

        with ExitStack() as st:
            def tb(name, shape, dt=F32):
                return st.enter_context(nc.sbuf_tensor(name, shape, dt))

            def tsem(name):
                return st.enter_context(nc.semaphore(name))
            GH = tb("GH", [P, 2, 2, S], F32R)
            GL = tb("GL", [P, 2, 2, S], F32R)
            PR = tb("PR", [P, 2, 2, S])
            PT = tb("PT", [P, 2, 2, TILES, S])
            VT = tb("VT", [P, S])
            V = tb("V", [P, 2, TILES, P])
            OT = tb("OT", [P, S])
            NMAX = tb("NMAX", [P, 2, 2])
            RSUM = tb("RSUM", [P, 2, 2])
            RINV = tb("RINV", [P, 2, 2])
            s_ready = tsem("s_ready")
            max_ready = tsem("max_ready")
            exp_ready = tsem("exp_ready")
            inv_ready = tsem("inv_ready")
            p_ready = tsem("p_ready")
            t_ready = tsem("t_ready")
            ta_copied = tsem("ta_copied")
            tb_copied = tsem("tb_copied")
            ga_ready = tsem("ga_ready")
            gb_ready = tsem("gb_ready")
            ga_copied = tsem("ga_copied")
            gb_copied = tsem("gb_copied")
            vt_ready = tsem("vt_ready")
            vt_copied = tsem("vt_copied")
            v_ready = tsem("v_ready")
            v_copied = tsem("v_copied")
            o_ready = tsem("o_ready")
            o_copied = tsem("o_copied")
            wo_ready = tsem("wo_ready")
            added = tsem("added")
            zeros = tsem("zeros")
            gh_ready = tsem("gh_ready")
            norm_begun = tsem("norm_begun")

            with nc.Block() as block:
                @block.tensor
                def _(pe):
                    def scores(n, par, i, b):
                        if i == 0:
                            pe.wait_ge(ga_copied, n + 1)
                            pe.wait_ge(gb_copied, n + 1)
                        for s in range(2):
                            last = product(nc, PS[:, 2 * (i % 2) + s, :],
                                           (GH[:, par, s, i * P:(i + 1) * P], GL[:, par, s, i * P:(i + 1) * P]), batch(b))
                        last.then_inc(s_ready, 1)

                    def project_a(n, pair, b):
                        product(nc, PS[:, 6, :], (MH[:, 0, pair, :], ML[:, 0, pair, :]), batch(b)).then_inc(ga_ready, 1)

                    def project_b(n, pair, b):
                        product(nc, PS[:, 7, :], (MH[:, 1, pair, :], ML[:, 1, pair, :]), batch(b)).then_inc(gb_ready, 1)

                    def values_t(n, pair, b):
                        pe.wait_ge(ga_copied, n + 1)
                        cols = slice(pair * P, (pair + 1) * P)
                        product(nc, PS[:, 6, :], (WVH[:, cols], WVL[:, cols]), batch(b)).then_inc(vt_ready, 1)

                    def values(n):
                        pe.wait_ge(vt_copied, n + 1)
                        for t in range(TILES):
                            last = nc.tensor.transpose(PS[:, 7, t * P:(t + 1) * P], VT[:, t * P:(t + 1) * P], ident[:])
                        last.then_inc(v_ready, 1)

                    def turn(c, par):
                        pe.wait_ge(p_ready, c + 1 + AHEAD)
                        pe.wait_ge(ta_copied, c + 1 + AHEAD)
                        pe.wait_ge(tb_copied, c + 1 + AHEAD)
                        for s in range(2):
                            for t in range(TILES):
                                last = nc.tensor.transpose(PS[:, 4 + s, t * P:(t + 1) * P], PR[:, par, s, t * P:(t + 1) * P],
                                                           ident[:])
                        last.then_inc(t_ready, 1)

                    def outputs(n, par, tiles):
                        if tiles[0] == 0:
                            pe.wait_ge(ta_copied, 4 * n + 5 + AHEAD)
                            pe.wait_ge(tb_copied, 4 * n + 5 + AHEAD)
                            pe.wait_ge(v_copied, n + 1 + AHEAD)
                        for t in tiles:
                            for s in range(2):
                                last = nc.tensor.matmul(PS[DH * s:DH * (s + 1), 7, :], V[:, par, t, DH * s:DH * (s + 1)],
                                                        PT[:, par, s, t, :], start=(t == 0), stop=(t == TILES - 1),
                                                        skip_group_check=True)
                        if tiles[-1] == TILES - 1:
                            last.then_inc(o_ready, 1)

                    def project_out(n, pair):
                        pe.wait_ge(o_copied, n + 2)
                        nc.tensor.matmul(PS[:, 6, :], WO[:, pair, :], OT[:], start=True, stop=True).then_inc(wo_ready, 1)

                    pe.wait_ge(zeros, 1)
                    project_a(0, 0, 0)
                    project_b(0, 0, 0)
                    values_t(0, 0, 0)
                    pe.wait_ge(gb_copied, 1)
                    values(0)
                    with pe.Fori(0, B) as b:
                        for h in range(PAIRS):
                            n = b * PAIRS + h
                            par, nxt = h % 2, (h + 1) % PAIRS
                            nb = b + (h + 1) // PAIRS
                            scores(n, par, 0, b)
                            pe.wait_ge(added, n + AHEAD)
                            project_a(n + 1, nxt, nb)
                            pe.wait_ge(v_copied, n + 1 + AHEAD)
                            project_b(n + 1, nxt, nb)
                            turn(4 * n - 1, 1)
                            scores(n, par, 1, b)
                            values_t(n + 1, nxt, nb)
                            pe.wait_ge(gb_copied, n + 2)
                            outputs(n - 1, 1 - par, range(0, 2))
                            turn(4 * n, 0)
                            scores(n, par, 2, b)
                            outputs(n - 1, 1 - par, range(2, TILES))
                            turn(4 * n + 1, 1)
                            scores(n, par, 3, b)
                            pe.wait_ge(vt_copied, n + 2)
                            project_out(n - 1, (h - 1) % PAIRS)
                            values(n + 1)
                            turn(4 * n + 2, 0)
                    n = B * PAIRS
                    turn(4 * n - 1, 1)
                    pe.wait_ge(v_copied, n + 1 + AHEAD)
                    outputs(n - 1, 1, range(TILES))
                    pe.wait_ge(added, n + AHEAD)
                    project_out(n - 1, PAIRS - 1)

                @block.vector
                def _(dve):
                    def row_max(c, par):
                        dve.wait_ge(s_ready, c + 1)
                        nc.vector.tensor_reduce(NMAX[:, par, :], PS[:, 2 * par:2 * par + 2, :], AX.X, ALU.max,
                                                negate=True).then_inc(max_ready, 1)

                    def invert(c, par):
                        dve.wait_ge(exp_ready, c + 1)
                        nc.vector.reciprocal(RINV[:, par, :], RSUM[:, par, :]).then_inc(inv_ready, 1)

                    def copy_turned(c, par, i):
                        dve.wait_ge(t_ready, c + 2)
                        nc.vector.tensor_copy(PT[:, par, 0, :, i * P:(i + 1) * P],
                                              PS[:, 4, :].rearrange("p (t q) -> p t q", q=P)).then_inc(ta_copied, 1)

                    def split_g(n, par, s):
                        dve.wait_ge(gh_ready, 2 * n + s + 1)
                        split_lo(nc, GL[:, par, s, :], PS[:, 6 + s, :], GH[:, par, s, :]).then_inc((ga_copied, gb_copied)[s], 1)

                    def copy_vt(n):
                        dve.wait_ge(vt_ready, n + 1)
                        nc.vector.tensor_copy(VT[:], PS[:, 6, :]).then_inc(vt_copied, 1)

                    def copy_o(n):
                        dve.wait_ge(o_ready, n + 2)
                        nc.vector.tensor_copy(OT[:], PS[:, 7, :]).then_inc(o_copied, 1)

                    def accumulate(n, block_at, first):
                        dve.wait_ge(wo_ready, n + 2)
                        dve.wait_ge(added, n + 1 + AHEAD)
                        acc = ACCT[:, bass.ds(block_at * S, S)]
                        if first:
                            nc.vector.tensor_copy(acc, PS[:, 6, :]).then_inc(added, 1)
                        else:
                            nc.vector.tensor_tensor(acc, PS[:, 6, :], acc, ALU.add).then_inc(added, 1)

                    dve.sem_inc(ta_copied, AHEAD)
                    dve.sem_inc(added, AHEAD)
                    nc.vector.memset(PR[:, 1, :, :], 0.0)
                    nc.vector.memset(PT[:, 1, :, :, :], 0.0)
                    nc.vector.memset(V[:, 1, :, :], 0.0).then_inc(zeros, 1)
                    split_g(0, 0, 0)
                    split_g(0, 0, 1)
                    copy_vt(0)
                    with dve.Fori(0, B) as b:
                        for h in range(PAIRS):
                            n = b * PAIRS + h
                            par = h % 2
                            row_max(4 * n, 0)
                            split_g(n + 1, 1 - par, 0)
                            split_g(n + 1, 1 - par, 1)
                            copy_turned(4 * n - 1, 1 - par, 3)
                            invert(4 * n, 0)
                            row_max(4 * n + 1, 1)
                            copy_vt(n + 1)
                            invert(4 * n + 1, 1)
                            copy_turned(4 * n, par, 0)
                            row_max(4 * n + 2, 0)
                            copy_o(n - 1)
                            invert(4 * n + 2, 0)
                            copy_turned(4 * n + 1, par, 1)
                            row_max(4 * n + 3, 1)
                            accumulate(n - 1, b if h == 0 else b + 1, h == 1)
                            invert(4 * n + 3, 1)
                            copy_turned(4 * n + 2, par, 2)
                    n = B * PAIRS
                    copy_turned(4 * n - 1, 1, 3)
                    copy_o(n - 1)
                    accumulate(n - 1, B, False)

                @block.scalar
                def _(act):
                    def exps(c, par):
                        act.wait_ge(max_ready, c + 1)
                        for s in range(2):
                            last = nc.scalar.activation(PR[:, par, s, :], PS[:, 2 * par + s, :], ACT.Exp,
                                                        bias=NMAX[:, par, s:s + 1], accum_out=RSUM[:, par, s:s + 1])
                        last.then_inc(exp_ready, 1)

                    def copy_g(n, par, s):
                        act.wait_ge((ga_ready, gb_ready)[s], n + 1)
                        nc.scalar.activation(GH[:, par, s, :], PS[:, 6 + s, :], ACT.Copy).then_inc(gh_ready, 1)

                    def copy_turned(c, par, i):
                        act.wait_ge(t_ready, c + 2)
                        nc.scalar.activation(PT[:, par, 1, :, i * P:(i + 1) * P],
                                             PS[:, 5, :].rearrange("p (t q) -> p t q", q=P), ACT.Copy).then_inc(tb_copied, 1)

                    def copy_v(n, par):
                        act.wait_ge(v_ready, n + 1)
                        nc.scalar.activation(V[:, par, :, :], PS[:, 7, :].rearrange("p (t q) -> p t q", q=P),
                                             ACT.Copy).then_inc(v_copied, 1)

                    act.sem_inc(tb_copied, AHEAD)
                    act.sem_inc(v_copied, AHEAD)
                    copy_g(0, 0, 0)
                    copy_g(0, 0, 1)
                    copy_v(0, 0)
                    with act.Fori(0, B) as b:
                        for h in range(PAIRS):
                            n = b * PAIRS + h
                            par = h % 2
                            copy_g(n + 1, 1 - par, 0)
                            copy_g(n + 1, 1 - par, 1)
                            exps(4 * n, 0)
                            copy_turned(4 * n - 1, 1 - par, 3)
                            exps(4 * n + 1, 1)
                            copy_turned(4 * n, par, 0)
                            exps(4 * n + 2, 0)
                            copy_turned(4 * n + 1, par, 1)
                            exps(4 * n + 3, 1)
                            copy_v(n + 1, 1 - par)
                            copy_turned(4 * n + 2, par, 2)
                    copy_turned(4 * B * PAIRS - 1, 1, 3)

                @block.gpsimd
                def _(pool):
                    def normalise(c, par):
                        pool.wait_ge(inv_ready, c + 1)
                        pool.sem_inc(norm_begun, 1)
                        for s in range(2):
                            last = nc.gpsimd.tensor_scalar(PR[:, par, s, :], PR[:, par, s, :], RINV[:, par, s:s + 1], 1.0,
                                                           ALU.mult, ALU.mult)
                        last.then_inc(p_ready, 1)

                    pool.sem_inc(p_ready, AHEAD)
                    with pool.Fori(0, 2 * B * PAIRS) as c0_half:
                        c0 = 2 * c0_half
                        for p in range(2):
                            normalise(c0 + p, p)

        with ExitStack() as st:
            def tb(name, shape, dt=F32):
                return st.enter_context(nc.sbuf_tensor(name, shape, dt))

            def tsem(name):
                return st.enter_context(nc.semaphore(name))
            XP = tb("XP", [P, 2, S + 1])
            XD = tb("XD", [P, 2, S])
            XR = tb("XR", [P, 2, 2, S])
            R = tb("R", [P, 2, S])
            K = tb("K", [P, 2, S])
            Y = tb("Y", [P, 2, S])
            X1 = tb("X1", [P, 2, TILES, D])
            links, mixed, rk_ready, r_done, k_done, v_ready, y_done, y_turned, x1_done, x1_kept = map(
                tsem, ("links2", "mixed", "rk_ready", "r_done", "k_done", "v2_ready", "y_done", "y_turned", "x1_done", "x1_kept"))
            k_pos = tsem("k_pos")
            with nc.Block() as block:
                @block.vector
                def _(dve):
                    def mix(b, p, base):
                        link = Links(dve, links, base)
                        hi, lo = batch(b)
                        link(nc.vector.tensor_tensor(XP[:, p, 1:S + 1], hi.bitcast(F32), lo.bitcast(F32), ALU.add))
                        link(nc.vector.tensor_tensor(XD[:, p, :], XP[:, p, 1:S + 1], XP[:, p, 0:S], ALU.subtract))
                        for k in range(2):
                            last = nc.vector.scalar_tensor_tensor(XR[:, p, k, :], XD[:, p, :], MU[:, k:k + 1], XP[:, p, 0:S],
                                                                  ALU.mult, ALU.add)
                        last.then_inc(mixed, 1)
                        return link

                    def finish(b, p):
                        link = Links(dve, links, 6 + 5 * b)
                        dve.wait_ge(v_ready, b + 1)
                        dve.wait_ge(r_done, b + 1)
                        link(nc.vector.tensor_tensor(Y[:, p, :], PS[:, 4 + p, :], R[:, p, :], ALU.mult))
                        nc.vector.tensor_tensor(Y[:, p, :], Y[:, p, :], ACCT[:, bass.ds((b + 1) * S, S)],
                                                ALU.add).then_inc(y_done, 1)
                        dve.wait_ge(y_turned, b + 1)
                        link(nc.vector.tensor_tensor(X1[:, p, :, :], PS[:, 6 + p, :].rearrange("p (t d) -> p t d", d=D),
                                                     X[:, bass.ds(b * TILES, TILES), :], ALU.add))
                        for t in range(TILES):
                            nc.vector.bn_stats(STATS[:, bass.ds(b * TILES + t, 1), :].rearrange("p a s -> p (a s)"), X1[:, p, t, :])
                        link(nc.vector.tensor_copy(X[:, bass.ds(b * TILES, TILES), :], X1[:, p, :, :]))

                    link = Links(dve, links)
                    link(nc.vector.memset(XP[:, 0, 0:1], 0.0))
                    link(nc.vector.memset(XP[:, 1, 0:1], 0.0))
                    mix(0, 0, 2)
                    with dve.Fori(0, B // 2) as b0_half:
                        b0 = 2 * b0_half
                        for p in range(2):
                            mix(b0 + p + 1, 1 - p, 4 + 5 * (b0 + p))
                            finish(b0 + p, p)

                @block.tensor
                def _(pe):
                    def receptance_and_key(b, p):
                        pe.wait_ge(mixed, b + 1)
                        for k in range(2):
                            last = nc.tensor.matmul(PS[:, 2 * p + k, :], WR_T[:, k, :], XR[:, p, k, :], start=True, stop=True)
                        last.then_inc(rk_ready, 1)

                    receptance_and_key(0, 0)
                    with pe.Fori(0, B // 2) as b0_half:
                        for p in range(2):
                            b = 2 * b0_half + p
                            receptance_and_key(b + 1, 1 - p)
                            pe.wait_ge(k_done, b + 1)
                            nc.tensor.matmul(PS[:, 4 + p, :], WR_T[:, 2, :], K[:, p, :], start=True, stop=True).then_inc(v_ready, 1)
                            pe.wait_ge(y_done, b + 1)
                            for t in range(TILES):
                                last = nc.tensor.transpose(PS[:, 6 + p, t * P:(t + 1) * P], Y[:, p, t * P:(t + 1) * P], ident[:])
                            last.then_inc(y_turned, 1)

                @block.scalar
                def _(act):
                    def gates(b, p):
                        act.wait_ge(rk_ready, b + 1)
                        nc.scalar.activation(K[:, p, :], PS[:, 2 * p + 1, :], ACT.Relu).then_inc(k_pos, 1)
                        nc.scalar.activation(R[:, p, :], PS[:, 2 * p, :], ACT.Sigmoid).then_inc(r_done, 1)
                        act.wait_ge(k_pos, b + 1)
                        nc.scalar.activation(K[:, p, :], K[:, p, :], ACT.Square).then_inc(k_done, 1)

                    gates(0, 0)
                    with act.Fori(0, B // 2) as b0_half:
                        for p in range(2):
                            gates(2 * b0_half + p + 1, 1 - p)

        first_layer.close()
        layernorm_stage("2", True)

        with ExitStack() as st:
            def tb(name, shape, dt=F32):
                return st.enter_context(nc.sbuf_tensor(name, shape, dt))

            def tsem(name):
                return st.enter_context(nc.semaphore(name))
            RING, AWAY = 4, 2
            SC_AHEAD = RING * TILES
            Y_AHEAD = 2
            V1 = tb("V1", [P, TILES, H1, SLOT])
            A = tb("A", [P, 2 * HPG, TILES, S])
            YT = tb("YT", [P, GROUPS, S])
            EPS = tb("EPS", [P, 2])
            EP4 = tb("EP4", [P, HPG])
            selection = st.enter_context(ExitStack())

            def tb3(name, shape):
                return selection.enter_context(nc.sbuf_tensor(name, shape, F32))
            SCT = tb3("SCT", [B * E, S])
            LEFT = tb3("LEFT", [B * E, S])
            TOP = tb3("TOP", [B * E, 8])
            LAST = tb3("LAST", [B * E, 8])
            GATE = tb3("GATE", [B * E, S])
            turned, links, gated, stored, cleared = map(tsem, ("sc_turned", "links3", "gated", "gate_stored", "cleared"))
            with nc.Block() as block:
                @block.tensor
                def _(pe):
                    for t in range(TILES):
                        last = nc.tensor.transpose(PS[0:B * E, 0, t * P:(t + 1) * P], SC[:, t, :], ident[:])
                    last.then_inc(turned, 1)

                @block.vector
                def _(dve):
                    link = Links(dve, links)
                    dve.wait_ge(turned, 1)
                    nc.vector.tensor_copy(SCT[:], PS[0:B * E, 0, :])
                    link(nc.vector.tensor_copy(LEFT[:], PS[0:B * E, 0, :]))
                    full, rest = divmod(CAPACITY, 8)
                    for _ in range(full):
                        link(nc.vector.max(TOP[:], LEFT[:]))
                        link(nc.vector.match_replace(LEFT[:], TOP[:], LEFT[:], -1.0))
                    if rest:
                        link(nc.vector.memset(LAST[:], -1.0))
                        link(nc.vector.max(TOP[:], LEFT[:]))
                        link(nc.vector.tensor_copy(LAST[:, 0:rest], TOP[:, 0:rest]))
                        link(nc.vector.match_replace(LEFT[:], LAST[:], LEFT[:], -1.0))
                    nc.vector.scalar_tensor_tensor(GATE[:], LEFT[:], 0.0, SCT[:], ALU.is_lt, ALU.mult).then_inc(gated, 1)

                @block.gpsimd
                def _(pool):
                    nc.gpsimd.memset(V1[:], 0.0).then_inc(cleared, 1)
                    pool.wait_ge(cleared, 1)
                    nc.gpsimd.memset(V1[:, :, :, HD:2 * HD], 1.0)
                    nc.gpsimd.memset(A[:, HPG:2 * HPG, :, :], 0.0)
                    nc.gpsimd.memset(YT[:], 0.0)
                    nc.gpsimd.memset(EPS[:, 0:1], LN_EPS)
                    nc.gpsimd.memset(EPS[:, 1:2], 0.0).then_inc(cleared, 1)
                    pool.wait_ge(cleared, 2)
                    nc.gpsimd.memset(EP4[:], DEN_EPS).then_inc(cleared, 1)
                    pool.wait_ge(cleared, 3)
                    for n, (base, sign) in enumerate(((-HD, 1), (2 * HD - 1, -1))):
                        nc.gpsimd.affine_select(out=EP4[:], in_=EP4[:], compare_op=ALU.is_ge, fill=0.0, base=base,
                                                pattern=[[-SLOT * sign, HPG]], channel_multiplier=sign).then_inc(cleared, 1)
                        pool.wait_ge(cleared, 4 + n)
                    for i in range(HPG):
                        nc.gpsimd.tensor_tensor(EPS[:, 1:2], EPS[:, 1:2], EP4[:, i:i + 1], ALU.add).then_inc(cleared, 1)
                        pool.wait_ge(cleared, 6 + i)

                @block.sync
                def _(sp):
                    sp.wait_ge(gated, 1)
                    sp.dma_start(gate_dram, GATE[:]).then_inc(stored, 16)
                    sp.wait_ge(stored, 16)
            selection.close()
            SQ = tb("SQ", [P, 2, S])
            QKC = tb("QKC", [P, 2, S])
            QH = tb("QH", [P, FT, S], F32R)
            QL = tb("QL", [P, FT, S], F32R)
            KH = tb("KH", [P, FT, S], F32R)
            KL = tb("KL", [P, FT, S], F32R)
            KMH = tb("KMH", [P, RING, S], F32R)
            KML = tb("KML", [P, RING, S], F32R)
            VT1 = tb("VT1", [P, S])
            DN = tb("DN", [P, S])
            links, pj_ready, pj_copied, var_ready, root_done, q_ready, k_ready, kh_ready, kl_ready = map(
                tsem, ("links4", "pj_ready", "pj_copied", "var_ready", "root_done", "q_ready", "k_ready", "kh_ready", "kl_ready"))
            sc_ready, sq_done, masked, nd_ready, nd_copied, y_ready, wo_ready, added = map(
                tsem, ("sc_ready", "sq_done", "masked", "nd_ready", "nd_copied", "y_ready4", "wo_ready4", "added4"))
            vt_ready, vt_copied, v_ready, v_copied, divide_begun, mask_begun = map(
                tsem, ("vt_ready4", "vt_copied4", "v_ready4", "v_copied4", "divide_begun", "mask_begun"))
            with nc.Block() as block:
                @block.tensor
                def _(pe):
                    def project(m, u, f, b):
                        product(nc, PS[:, 6, :], (WQKH[:, FT * m + f, :], WQKL[:, FT * m + f, :]), batch(b)).then_inc(pj_ready, 1)

                    def variance(m, u):
                        pe.wait_ge(pj_copied, 2 * u + m + 1)
                        nc.tensor.matmul(PS[:, 7, :], block_mean[:], SQ[:, m, :], start=True, stop=True).then_inc(var_ready, 1)

                    def scores(hh, h, u, f):
                        if h % HPT == 0:
                            pe.wait_ge(q_ready, u + 1)
                        pe.wait_ge(kh_ready, hh + 1)
                        pe.wait_ge(kl_ready, hh + 1)
                        slot = h % RING
                        for t in range(TILES):
                            pe.wait_ge(sq_done, TILES * hh + t + 1)
                            keys = slice(t * P, (t + 1) * P)
                            product(nc, PS[:, t, t * P:S], (KMH[:, slot, keys], KML[:, slot, keys]),
                                    (QH[:, f, t * P:S], QL[:, f, t * P:S])).then_inc(sc_ready, 1)

                    def outputs(g, r):
                        pe.wait_ge(masked, HPG * (g + 1) + AHEAD)
                        pe.wait_ge(nd_copied, g + 1 + AHEAD)
                        for t in range(TILES):
                            for i in range(HPG):
                                last = nc.tensor.matmul(PS[SLOT * i:SLOT * (i + 1), 4, t * P:S], V1[:, t, HPG * (r % GROUPS) + i, :],
                                                        A[:, HPG * (r % 2) + i, t, t * P:S], start=(t == 0), stop=(t == TILES - 1),
                                                        skip_group_check=True)
                        last.then_inc(nd_ready, 1)

                    def project_out(b):
                        pe.wait_ge(y_ready, GROUPS * b + GROUPS + 1 + Y_AHEAD)
                        pe.wait_ge(added, b + 1 + AHEAD)
                        for r in range(GROUPS):
                            last = nc.tensor.matmul(PS[:, 5, :], WO_PAD[:, r, :], YT[:, r, :], start=(r == 0), stop=(r == GROUPS - 1))
                        last.then_inc(wo_ready, 1)

                    pe.sem_inc(sc_ready, SC_AHEAD)
                    project(0, 0, 0, 0)
                    pe.wait_ge(pj_copied, 1)
                    project(1, 0, 0, 0)
                    variance(0, 0)
                    pe.wait_ge(root_done, 1)
                    variance(1, 0)
                    pe.wait_ge(root_done, 2)
                    with pe.Fori(0, B) as b:
                        for f in range(FT):
                            u = FT * b + f
                            nf, nb = (f + 1) % FT, b + (f + 1) // FT
                            for k in range(HPT):
                                h = HPT * f + k
                                if f == 0 and k == 4:
                                    pe.wait_ge(vt_copied, b + 1)
                                    pe.wait_ge(root_done, 2 * u + 4)
                                    for t in range(TILES):
                                        last = nc.tensor.transpose(PS[:, 7, t * P:(t + 1) * P], VT1[:, t * P:(t + 1) * P], ident[:])
                                    last.then_inc(v_ready, 1)
                                scores(H1 * b + h, h, u, f)
                                if k == 0:
                                    if f == 1:
                                        pe.wait_ge(vt_copied, b + 1)
                                    project(0, u + 1, nf, nb)
                                elif k == 1:
                                    outputs(GROUPS * b + 2 * f - 1, 2 * f - 1)
                                    pe.wait_ge(pj_copied, 2 * u + 3)
                                    project(1, u + 1, nf, nb)
                                elif k == 2:
                                    if f == 1:
                                        pe.wait_ge(v_copied, b + 1)
                                    variance(0, u + 1)
                                    if f == 0:
                                        pe.wait_ge(pj_copied, 2 * u + 4)
                                        product(nc, PS[:, 6, :], (WV1H[:], WV1L[:]), batch(b)).then_inc(vt_ready, 1)
                                elif k == 3:
                                    pe.wait_ge(root_done, 2 * u + 3)
                                    variance(1, u + 1)
                                    if f == 0:
                                        project_out(b - 1)
                                elif k == 5:
                                    if f == 0:
                                        pe.wait_ge(v_copied, b + 1)
                                    outputs(GROUPS * b + 2 * f, 2 * f)
                    outputs(GROUPS * B - 1, GROUPS - 1)
                    project_out(B - 1)

                @block.scalar
                def _(act):
                    def squares(hh, h):
                        for t in range(TILES):
                            act.wait_ge(sc_ready, TILES * hh + t + 1 + SC_AHEAD)
                            nc.scalar.activation(A[:, h % (2 * HPG), t, t * P:S], PS[:, t, t * P:S], ACT.Square,
                                                 scale=FEAT ** -0.5).then_inc(sq_done, 1)

                    def copy_projection(m, u):
                        act.wait_ge(pj_ready, 2 * u + m + 1)
                        nc.scalar.activation(SQ[:, m, :], PS[:, 6, :], ACT.Square)
                        nc.scalar.activation(QKC[:, m, :], PS[:, 6, :], ACT.Copy).then_inc(pj_copied, 1)

                    def root(m, u):
                        act.wait_ge(var_ready, 2 * u + m + 1)
                        nc.scalar.activation(SQ[:, m, :], PS[:, 7, :], ACT.Sqrt, bias=EPS[:, 0:1]).then_inc(root_done, 1)

                    def copy_outputs(g, r):
                        act.wait_ge(nd_ready, g + 2)
                        nc.scalar.activation(YT[:, r % GROUPS, :], PS[:, 4, :], ACT.Identity, bias=EPS[:, 1:2]).then_inc(nd_copied, 1)

                    act.sem_inc(sq_done, TILES)
                    act.sem_inc(nd_copied, AHEAD)
                    copy_projection(0, 0)
                    copy_projection(1, 0)
                    root(0, 0)
                    root(1, 0)
                    with act.Fori(0, B) as b:
                        for f in range(FT):
                            u = FT * b + f
                            for k in range(HPT):
                                h = HPT * f + k
                                squares(H1 * b + h, h)
                                if k == 0:
                                    copy_projection(0, u + 1)
                                elif k == 1:
                                    copy_outputs(GROUPS * b + 2 * f - 1, 2 * f - 1)
                                    copy_projection(1, u + 1)
                                elif k == 2:
                                    root(0, u + 1)
                                elif k == 3:
                                    root(1, u + 1)
                                elif k == 5:
                                    if f == 0:
                                        act.wait_ge(wo_ready, b + 1)
                                    copy_outputs(GROUPS * b + 2 * f, 2 * f)
                    copy_outputs(GROUPS * B - 1, GROUPS - 1)

                @block.vector
                def _(dve):
                    def norm(m, u, par, base):
                        link = Links(dve, links, base)
                        dve.wait_ge(root_done, 2 * u + m + 1)
                        link(nc.vector.reciprocal(SQ[:, m, :], SQ[:, m, :]))
                        link(nc.vector.tensor_tensor(QKC[:, m, :], QKC[:, m, :], SQ[:, m, :], ALU.mult))
                        link(nc.vector.tensor_scalar(QKC[:, m, :], QKC[:, m, :], GB[:, 0:1], GB[:, 1:2], ALU.mult, ALU.add))
                        hi, lo = ((QH, QL), (KH, KL))[m]
                        link(nc.vector.tensor_copy(hi[:, par, :], QKC[:, m, :]))
                        split_lo(nc, lo[:, par, :], QKC[:, m, :], hi[:, par, :]).then_inc((q_ready, k_ready)[m], 1)

                    def mask_high(hh, h, par):
                        dve.wait_ge(sc_ready, TILES * (hh - RING + 1) + SC_AHEAD)
                        nc.vector.tensor_scalar(KMH[:, h % RING, :], KH[:, par, :].bitcast(F32), head_mask[:, h % HPT:h % HPT + 1],
                                                None, ALU.mult).then_inc(kh_ready, 1)

                    def divide(g, r, base):
                        link = Links(dve, links, base)
                        dve.wait_ge(nd_copied, g + 2 + AHEAD)
                        dve.wait_ge(y_ready, g + 1 + Y_AHEAD)
                        dve.sem_inc(divide_begun, 1)
                        y = YT[:, r % GROUPS, :]
                        link(nc.vector.stream_shuffle(DN[:], y, [HD + i % HD for i in range(SLOT)]))
                        link(nc.vector.reciprocal(DN[:], DN[:]))
                        nc.vector.tensor_tensor(y, y, DN[:], ALU.mult).then_inc(y_ready, 1)

                    def add_output(b):
                        dve.wait_ge(wo_ready, b + 2)
                        nc.vector.tensor_copy(ACCT[:, bass.ds((b + 1) * S, S)], PS[:, 5, :]).then_inc(added, 1)

                    dve.sem_inc(y_ready, Y_AHEAD)
                    dve.sem_inc(added, AHEAD)
                    norm(0, 0, 0, 0)
                    norm(1, 0, 0, 4)
                    dve.wait_ge(k_ready, 1)
                    mask_high(0, 0, 0)
                    mask_high(1, 1, 0)
                    PER_U = 12
                    with dve.Fori(0, B) as b:
                        for f in range(FT):
                            u = FT * b + f
                            at = 8 + PER_U * u
                            for k in range(HPT):
                                h = HPT * f + k
                                if k == HPT - AWAY:
                                    dve.wait_ge(k_ready, u + 2)
                                mask_high(H1 * b + h + AWAY, (h + AWAY) % H1, f if k < HPT - AWAY else 1 - f)
                                if k == 2:
                                    divide(GROUPS * b + 2 * f - 1, 2 * f - 1, at)
                                elif k == 3:
                                    if f == 0:
                                        dve.wait_ge(vt_ready, b + 1)
                                        nc.vector.tensor_copy(VT1[:], PS[:, 6, :]).then_inc(vt_copied, 1)
                                    norm(0, u + 1, 1 - f, at + 2)
                                elif k == 4:
                                    norm(1, u + 1, 1 - f, at + 6)
                                    if f == 0:
                                        dve.wait_ge(v_ready, b + 1)
                                        nc.vector.tensor_copy(V1[:, :, :, 0:HD].rearrange("p t h d -> p (t h) d"),
                                                              PS[:, 7, :].rearrange("p (c d) -> p c d", d=HD)).then_inc(v_copied, 1)
                                        add_output(b - 1)
                                elif k == 6:
                                    divide(GROUPS * b + 2 * f, 2 * f, at + 10)
                    divide(GROUPS * B - 1, GROUPS - 1, 8 + PER_U * FT * B)
                    add_output(B - 1)

                @block.gpsimd
                def _(pool):
                    def mask_low(hh, h, par):
                        pool.wait_ge(sc_ready, TILES * (hh - RING + 1) + SC_AHEAD)
                        pool.sem_inc(mask_begun, 1)
                        nc.gpsimd.tensor_scalar(KML[:, h % RING, :], KL[:, par, :].bitcast(F32), head_mask[:, h % HPT:h % HPT + 1],
                                                1.0, ALU.mult, ALU.mult).then_inc(kl_ready, 1)

                    pool.sem_inc(masked, AHEAD)
                    pool.wait_ge(k_ready, 1)
                    mask_low(0, 0, 0)
                    mask_low(1, 1, 0)
                    with pool.Fori(0, B) as b:
                        for f in range(FT):
                            u = FT * b + f
                            for k in range(HPT):
                                h = HPT * f + k
                                if k == HPT - AWAY:
                                    pool.wait_ge(k_ready, u + 2)
                                mask_low(H1 * b + h + AWAY, (h + AWAY) % H1, f if k < HPT - AWAY else 1 - f)
                                pool.wait_ge(sq_done, TILES * (H1 * b + h + 1) + TILES)
                                slot = A[:, h % (2 * HPG), 0, 0:P]
                                diag = bass.AP(slot.tensor, slot.offset, [A[:].ap[0], [S + P, TILES], [1, P]])
                                nc.gpsimd.tensor_tensor(diag, diag, causal[:].unsqueeze(1).broadcast_to([P, TILES, P]), ALU.mult).then_inc(masked, 1)

        with ExitStack() as st:
            def tb(name, shape, dt=F32):
                return st.enter_context(nc.sbuf_tensor(name, shape, dt))

            def tsem(name):
                return st.enter_context(nc.semaphore(name))
            W1 = tb("W1", [P, 2, HID])
            W2 = tb("W2", [P, 2, HID])
            W1H = tb("W1H", [P, 2, HID], F32R)
            W1L = tb("W1L", [P, 2, HID], F32R)
            W2H = tb("W2H", [P, 2, HID], F32R)
            W2L = tb("W2L", [P, 2, HID], F32R)
            BC = tb("BC", [P, 2, HT + 1])
            HB = tb("HB", [P, 2, HT, S])
            HH = tb("HH", [P, 2, HT, S], F32R)
            HL = tb("HL", [P, 2, HT, S], F32R)
            GT = tb("GT", [P, 2, S])
            TMP = tb("TMP", [P, 2, S])
            w_sem = [tsem(f"w_loaded{k}") for k in range(2)]
            g_sem = [tsem(f"gates_loaded{k}") for k in range(2)]
            b_ready, h_ready, gelu_done, high_done, low_done, y_ready, scaled, added, w_split, links = map(
                tsem, ("b_ready", "h_ready5", "gelu_done", "high_done", "low_done", "y_ready5", "scaled", "added5", "w_split", "links5"))
            w_high, add_begun, e_begun = map(tsem, ("w_high", "add_begun", "e_begun"))
            TWO = 2
            with nc.Block() as block:
                @block.sync
                def _(sp):
                    def load_weights(e, k):
                        sp.dma_start(W1[:, k, :], w1[bass.ds(e, 1)].rearrange("a d n -> (a d) n")).then_inc(w_sem[k], 16)
                        sp.dma_start(W2[:, k, :].rearrange("p (j d) -> p j d", d=D),
                                     w2[bass.ds(e, 1)].rearrange("a (j p) d -> (a p) j d", p=P)).then_inc(w_sem[k], 16)

                    def gates_of(e):
                        with sp.Fori(0, B // 2) as b_half:
                            for p in range(2):
                                b = 2 * b_half + p
                                sp.wait_ge(scaled, e * B + b - 1 + TWO)
                                sp.dma_start(GT[:, p, :], gate_dram[bass.ds(b * E + e, 1), :].broadcast_to([P, S])).then_inc(g_sem[p], 16)

                    load_weights(0, 0)
                    load_weights(1, 1)
                    with sp.Fori(0, E // 2 - 1) as e_half:
                        for k in range(2):
                            sp.wait_ge(w_split, 2 * e_half + k + 1)
                            load_weights(2 * e_half + k + 2, k)
                            gates_of(2 * e_half + k)
                    gates_of(E - 2)
                    sp.wait_ge(w_split, E - 1)
                    sp.sem_inc(w_sem[0], 32)
                    gates_of(E - 1)

                @block.tensor
                def _(pe):
                    def hidden(n, k, b, j):
                        cols = slice(j * P, (j + 1) * P)
                        pe.wait_ge(gelu_done, HT * n + j + 1)
                        product(nc, PS[:, j, :], (W1H[:, k, cols], W1L[:, k, cols]), batch(b)).then_inc(h_ready, 1)

                    def output(n, k, p, j):
                        cols = slice(j * P, (j + 1) * P)
                        pe.wait_ge(low_done, HT * n + j + 1)
                        last = product(nc, PS[:, 4 + p, :], (W2H[:, k, cols], W2L[:, k, cols]),
                                       (HH[:, p, j, :], HL[:, p, j, :]), start=(j == 0), stop=(j == HT - 1))
                        if j == HT - 1:
                            last.then_inc(y_ready, 1)

                    def step(n, k, p, next_k, next_b):
                        hidden(n + 1, next_k, next_b, 0)
                        hidden(n + 1, next_k, next_b, 1)
                        pe.wait_ge(scaled, n - 1 + TWO)
                        output(n, k, p, 0)
                        hidden(n + 1, next_k, next_b, 2)
                        output(n, k, p, 1)
                        hidden(n + 1, next_k, next_b, 3)
                        output(n, k, p, 2)
                        output(n, k, p, 3)

                    pe.wait_ge(w_split, 1)
                    for j in range(HT):
                        hidden(0, 0, 0, j)
                    with pe.Fori(0, E // 2) as e_half:
                        for k in range(2):
                            e = 2 * e_half + k
                            with pe.Fori(0, B // 2 - 1) as b_half:
                                for p in range(2):
                                    b = 2 * b_half + p
                                    step(e * B + b, k, p, k, b + 1)
                            step(e * B + B - 2, k, 0, k, B - 1)
                            pe.wait_ge(w_split, e + 2)
                            step(e * B + B - 1, k, 1, 1 - k, 0)

                @block.scalar
                def _(act):
                    def high(n, p, j):
                        act.wait_ge(gelu_done, HT * n + j + 1 + HT)
                        nc.scalar.activation(HH[:, p, j, :], HB[:, p, j, :], ACT.Copy).then_inc(high_done, 1)

                    act.sem_inc(gelu_done, HT)
                    with act.Fori(0, E // 2) as e_half:
                        for k in range(2):
                            e = 2 * e_half + k
                            act.wait_ge(b_ready, e + 1)
                            act.sem_inc(e_begun, 1)
                            with act.Fori(0, B // 2) as b_half:
                                for p in range(2):
                                    n = e * B + 2 * b_half + p
                                    for j in range(HT):
                                        act.wait_ge(h_ready, HT * n + j + 1)
                                        nc.scalar.activation(HB[:, p, j, :], PS[:, j, :], ACT.Gelu,
                                                             bias=BC[:, k, j:j + 1]).then_inc(gelu_done, 1)
                                        if j:
                                            high(n, p, j - 1)
                                    high(n, p, HT - 1)

                @block.vector
                def _(dve):
                    def prepare(e, k):
                        nc.vector.tensor_copy(BC[:, k, 0:HT], B1_T[:, bass.ds(e * HT, HT)])
                        nc.vector.tensor_copy(BC[:, k, HT:HT + 1], B2_T[:, bass.ds(e, 1)]).then_inc(b_ready, 1)
                        dve.wait_ge(w_sem[k], 16 * e + 32 - 16 * k)
                        nc.vector.tensor_copy(W1H[:, k, :], W1[:, k, :])
                        nc.vector.tensor_copy(W2H[:, k, :], W2[:, k, :]).then_inc(w_high, 1)
                        dve.wait_ge(w_high, e + 1)
                        split_lo(nc, W1L[:, k, :], W1[:, k, :], W1H[:, k, :])
                        split_lo(nc, W2L[:, k, :], W2[:, k, :], W2H[:, k, :]).then_inc(w_split, 1)

                    dve.sem_inc(scaled, TWO)
                    prepare(0, 0)
                    with dve.Fori(0, E // 2) as e_half:
                        for k in range(2):
                            e = 2 * e_half + k
                            dve.wait_ge(scaled, e * B + TWO)
                            prepare(e + 1, 1 - k)
                            with dve.Fori(0, B // 2) as b_half:
                                for p in range(2):
                                    b = 2 * b_half + p
                                    n = e * B + b
                                    for j in range(HT):
                                        dve.wait_ge(high_done, HT * n + j + 1)
                                        split_lo(nc, HL[:, p, j, :], HB[:, p, j, :], HH[:, p, j, :]).then_inc(low_done, 1)
                                    dve.wait_ge(y_ready, n + 1)
                                    dve.wait_ge(g_sem[p], 16 * e * (B // 2) + 16 * b_half + 16)
                                    dve.wait_ge(added, n - 1 + TWO)
                                    nc.vector.scalar_tensor_tensor(TMP[:, p, :], PS[:, 4 + p, :], BC[:, k, HT:HT + 1], GT[:, p, :],
                                                                   ALU.add, ALU.mult).then_inc(scaled, 1)

                @block.gpsimd
                def _(pool):
                    pool.sem_inc(added, TWO)
                    with pool.Fori(0, E) as e:
                        with pool.Fori(0, B // 2) as b_half:
                            for p in range(2):
                                b = 2 * b_half + p
                                n = e * B + b
                                pool.wait_ge(added, n + TWO)
                                pool.wait_ge(scaled, n + 1 + TWO)
                                pool.sem_inc(add_begun, 1)
                                acc = ACCT[:, bass.ds((b + 1) * S, S)]
                                nc.gpsimd.tensor_tensor(acc, acc, TMP[:, p, :], ALU.add).then_inc(added, 1)

        with ExitStack() as st:
            def tb(name, shape, dt=F32):
                return st.enter_context(nc.sbuf_tensor(name, shape, dt))

            def tsem(name):
                return st.enter_context(nc.semaphore(name))
            YC = tb("YC", [P, 2, S])
            RES = tb("RES", [P, 2, TILES, D])
            copied, turned, summed = map(tsem, ("copied6", "turned6", "summed6"))
            out_sem = [tsem(f"stored6_{p}") for p in range(2)]
            with nc.Block() as block:
                @block.vector
                def _(dve):
                    with dve.Fori(0, B // 2) as b0_half:
                        b0 = 2 * b0_half
                        for p in range(2):
                            b = b0 + p
                            nc.vector.tensor_copy(YC[:, p, :], ACCT[:, bass.ds((b + 1) * S, S)]).then_inc(copied, 1)
                        for p in range(2):
                            b = b0 + p
                            dve.wait_ge(turned, b + 1)
                            dve.wait_ge(out_sem[p], b0 * 8 + 16)
                            nc.vector.tensor_tensor(RES[:, p, :, :], PS[:, p, :].rearrange("p (t d) -> p t d", d=D),
                                                    X[:, bass.ds(b * TILES, TILES), :], ALU.add).then_inc(summed, 1)

                @block.tensor
                def _(pe):
                    with pe.Fori(0, B // 2) as b0_half:
                        b0 = 2 * b0_half
                        for p in range(2):
                            b = b0 + p
                            pe.wait_ge(copied, b + 1)
                            for t in range(TILES):
                                last = nc.tensor.transpose(PS[:, p, t * P:(t + 1) * P], YC[:, p, t * P:(t + 1) * P], ident[:])
                            last.then_inc(turned, 1)

                @block.sync
                def _(sp):
                    for p in range(2):
                        sp.sem_inc(out_sem[p], 16)
                    with sp.Fori(0, B // 2) as b0_half:
                        b0 = 2 * b0_half
                        for p in range(2):
                            b = b0 + p
                            sp.wait_ge(summed, b + 1)
                            sp.dma_start(out[bass.ds(b, 1)].rearrange("a (t p) d -> p (a t) d", p=P), RES[:, p, :, :]
                                         ).then_inc(out_sem[p], 16)
                    for p in range(2):
                        sp.wait_ge(out_sem[p], B // 2 * 16 + 16)


_INS = ['L0_attn_x', 'L0_attn_kernel', 'L0_attn_WO', 'L0_ffn_W_r', 'L0_ffn_W_k', 'L0_ffn_W_v', 'L0_ffn_mu_r',
        'L0_ffn_mu_k', 'L1_attn_Wq', 'L1_attn_Wk', 'L1_attn_Wv', 'L1_attn_Wo', 'L1_attn_gamma', 'L1_attn_beta',
        'L1_ffn_router_w', 'L1_ffn_w1', 'L1_ffn_b1', 'L1_ffn_w2', 'L1_ffn_b2']


def kernel(**inputs):
    import numpy as _np
    import concourse.bacc as _bacc
    from concourse import mybir as _mybir
    from concourse.bass_utils import run_bass_kernel_spmd as _run

    nc = _bacc.Bacc("TRN2", target_bir_lowering=False, num_devices=1)
    arrays, args = {}, []
    for name in _INS:
        a = _np.ascontiguousarray(inputs[name])
        arrays[f"in_{name}_dram"] = a
        args.append(nc.dram_tensor(f"in_{name}_dram", a.shape, _mybir.dt.from_np(a.dtype), kind="ExternalInput").ap())
    args.append(nc.dram_tensor("out_dram", (8, 512, 128), _mybir.dt.float32, kind="ExternalOutput").ap())
    prob_d2_kernel(nc, *args)
    r = _run(nc, [arrays], core_ids=[0])
    return r.results[0]["out_dram"]
```

```python
import concourse.bass as bass
from concourse import mybir
from contextlib import ExitStack

F32 = mybir.dt.float32
F32R = mybir.dt.float32r
ALU = mybir.AluOpType
ACT = mybir.ActivationFunctionType
AX = mybir.AxisListType

P = 128
B, S, D = 8, 512, 128
TILES = S // P
NT = B * TILES
H, DH = 16, 64
PAIRS = H // 2
SCALE = 1.0 / (DH * DH * H)
H1, FEAT, HD = 16, 16, 8
FT = H1 * FEAT // P
HPT = P // FEAT
SLOT = 32
GROUPS = H1 * SLOT // P
HPG = P // SLOT
E, HID = 8, 512
HT = HID // P
CAPACITY = max(1, int(S * 2.0 / E) + 1)
LN_EPS = 1e-05
DEN_EPS = 1e-05


AHEAD = 1


class Links:

    def __init__(self, eng, sem, base=0):
        self.eng, self.sem, self.base, self.n = eng, sem, base, 0

    def __call__(self, ins):
        self.n += 1
        ins.then_inc(self.sem, 1)
        self.eng.wait_ge(self.sem, self.base + self.n)


def split_lo(nc, lo, src, hi):
    return nc.vector.tensor_tensor(lo, src, hi.bitcast(F32), ALU.subtract)


def product(nc, out, w, x, start=True, stop=True):
    (wh, wl), (xh, xl) = w, x
    nc.tensor.matmul(out, wl, xh, start=start, stop=False)
    nc.tensor.matmul(out, wh, xh, start=False, stop=False)
    return nc.tensor.matmul(out, wh, xl, start=False, stop=stop)


def prob_d2_kernel(nc, x, kern, wo0, w_r, w_k, w_v, mu_r, mu_k, wq1, wk1, wv1, wo1, gamma, beta,
                   router, w1, b1, w2, b2, out):
    x_dram = nc.dram_tensor("x_scratch", [P, NT, D], F32, kind="Internal").ap()
    gate_dram = nc.dram_tensor("gate_scratch", [B * E, S], F32, kind="Internal").ap()
    ctx = ExitStack()
    with ctx:
        def sb(name, shape, dt=F32):
            return ctx.enter_context(nc.sbuf_tensor(name, shape, dt))

        XH = sb("XH", [P, (B + 1) * S], F32R)
        XL = sb("XL", [P, (B + 1) * S], F32R)
        ACCT = sb("ACCT", [P, (B + 1) * S])
        ident = sb("ident", [P, P])
        causal = sb("causal", [P, P])
        head_mask = sb("head_mask", [P, HPT])
        WVO_T = sb("WVO_T", [P, 2, P])
        WV1H = sb("WV1H", [P, P], F32R)
        WV1L = sb("WV1L", [P, P], F32R)
        WQKH = sb("WQKH", [P, 2 * FT, P], F32R)
        WQKL = sb("WQKL", [P, 2 * FT, P], F32R)
        RT = sb("RT", [P, E])
        B1_T = sb("B1_T", [P, (E + 1) * HT])
        B2_T = sb("B2_T", [P, E + 1])
        MU = sb("MU", [P, 2])
        GB = sb("GB", [P, 2])
        SC = sb("SC", [P, TILES, B * E])
        STATS = sb("STATS", [P, NT, 6])
        MEAN = sb("MEAN", [P, NT])
        RSTD = sb("RSTD", [P, NT])
        LN = sb("LN", [P, 4, NT])

        stream = ctx.enter_context(ExitStack())
        X = stream.enter_context(nc.sbuf_tensor("X", [P, NT, D], F32))

        first_layer = ctx.enter_context(ExitStack())

        def sb1(name, shape, dt=F32):
            return first_layer.enter_context(nc.sbuf_tensor(name, shape, dt))

        WQKH1 = sb1("WQKH1", [P, 2, PAIRS, P], F32R)
        WQKL1 = sb1("WQKL1", [P, 2, PAIRS, P], F32R)
        WVH = sb1("WVH", [P, H * DH], F32R)
        WVL = sb1("WVL", [P, H * DH], F32R)
        WO = sb1("WO", [P, PAIRS, D])
        WR_T = sb1("WR_T", [P, 3, P])

        def batch(b):
            return XH[:, bass.ds(b * S, S)], XL[:, bass.ds(b * S, S)]

        PS = ctx.enter_context(nc.psum_tensor("PS", [P, 8, 512], F32))

        with ExitStack() as st:
            def tb(name, shape, dt=F32):
                return st.enter_context(nc.sbuf_tensor(name, shape, dt))
            WVS = tb("WVS", [P, H * DH])
            WQS = tb("WQS", [P, H, DH])
            WKS = tb("WKS", [P, H, DH])
            block_mean = tb("block_mean", [P, P])
            centre = tb("centre", [P, P])
            RAW = tb("RAW", [P, 5, P])
            RAW1 = tb("RAW1", [P, 2 * FT, P])
            RAWR = tb("RAWR", [E, P])
            RAWB1 = tb("RAWB1", [E * HT, P])
            RAWB2 = tb("RAWB2", [E, P])
            loaded = st.enter_context(nc.semaphore("loaded"))
            x_loaded = [st.enter_context(nc.semaphore(f"x_loaded{q}")) for q in range(4)]
            consts = st.enter_context(nc.semaphore("consts"))
            transposed = st.enter_context(nc.semaphore("transposed"))
            v_links = st.enter_context(nc.semaphore("v_links0"))
            g_links = st.enter_context(nc.semaphore("g_links0"))
            with nc.Block() as block:
                @block.scalar
                def _(act):
                    for q in range(4):
                        act.dma_start(X[:, q * NT // 4:(q + 1) * NT // 4, :],
                                      x.rearrange("b (t p) d -> p (b t) d", p=P)[:, q * NT // 4:(q + 1) * NT // 4, :]
                                      ).then_inc(x_loaded[q], 16)

                @block.sync
                def _(sp):
                    def load(dst, src):
                        sp.dma_start(dst, src).then_inc(loaded, 16)
                    load(WQS[:], kern[0].rearrange("h m d -> m h d"))
                    load(WKS[:], kern[1].rearrange("h m d -> m h d"))
                    load(WVS[:].rearrange("m (h d) -> m h d", h=H), kern[2].rearrange("h m d -> m h d"))
                    wo_v = wo0[0].rearrange("(d j s) m -> s d j m", j=PAIRS, s=2)
                    for s in range(2):
                        load(WO[DH * s:DH * (s + 1), :, :], wo_v[s])
                    for k, w in enumerate((w_r, w_k, w_v, wv1, wo1)):
                        load(RAW[:, k, :], w)
                    load(RAW1[:, 0:FT, :], wq1.rearrange("(f p) c -> p f c", p=P))
                    load(RAW1[:, FT:2 * FT, :], wk1.rearrange("(f p) c -> p f c", p=P))
                    load(RAWR[:], router)
                    load(RAWB1[:], b1.rearrange("e (j p) -> (e j) p", p=P))
                    load(RAWB2[:], b2)
                    load(MU[:, 0:1], mu_r.rearrange("(p a) -> p a", a=1))
                    load(MU[:, 1:2], mu_k.rearrange("(p a) -> p a", a=1))
                    for k, w in enumerate((gamma, beta)):
                        g = w.rearrange("(p a) -> p a", a=1)
                        for r in range(HPT):
                            sp.dma_start(GB[FEAT * r:FEAT * (r + 1), k:k + 1], g).then_inc(loaded, 16)

                LOADS = (17 + 2 * HPT) * 16

                @block.gpsimd
                def _(pool):
                    link = Links(pool, g_links)
                    link(nc.gpsimd.memset(ident[:], 0.0))
                    link(nc.gpsimd.affine_select(out=ident[:], in_=ident[:], compare_op=ALU.not_equal, fill=1.0,
                                                 base=0, pattern=[[-1, P]], channel_multiplier=1))
                    bm = block_mean[:].rearrange("p (g j) -> p g j", j=FEAT)
                    link(nc.gpsimd.memset(block_mean[:], 1.0 / FEAT))
                    link(nc.gpsimd.affine_select(out=bm, in_=bm, compare_op=ALU.is_ge, fill=0.0,
                                                 base=0, pattern=[[-FEAT, HPT], [0, FEAT]], channel_multiplier=1))
                    link(nc.gpsimd.affine_select(out=bm, in_=bm, compare_op=ALU.is_ge, fill=0.0,
                                                 base=FEAT - 1, pattern=[[FEAT, HPT], [0, FEAT]], channel_multiplier=-1))
                    link(nc.gpsimd.memset(head_mask[:], 1.0))
                    link(nc.gpsimd.affine_select(out=head_mask[:], in_=head_mask[:], compare_op=ALU.is_ge, fill=0.0,
                                                 base=0, pattern=[[-FEAT, HPT]], channel_multiplier=1))
                    link(nc.gpsimd.affine_select(out=head_mask[:], in_=head_mask[:], compare_op=ALU.is_ge, fill=0.0,
                                                 base=FEAT - 1, pattern=[[FEAT, HPT]], channel_multiplier=-1))
                    link(nc.gpsimd.tensor_tensor(head_mask[:, 0:HPG], head_mask[:, 0:HPG], head_mask[:, HPG:2 * HPG], ALU.add))
                    link(nc.gpsimd.memset(causal[:], 1.0))
                    link(nc.gpsimd.affine_select(out=causal[:], in_=causal[:], compare_op=ALU.is_ge, fill=0.0,
                                                 base=0, pattern=[[1, P]], channel_multiplier=-1))
                    nc.gpsimd.tensor_tensor(centre[:], ident[:], block_mean[:], ALU.subtract).then_inc(consts, 1)

                @block.tensor
                def _(pe):
                    pe.wait_ge(consts, 1)
                    pe.wait_ge(loaded, LOADS)
                    for k in range(3):
                        nc.tensor.transpose(PS[:, 0, k * P:(k + 1) * P], RAW[:, k, :], ident[:])
                    for k in range(2):
                        nc.tensor.transpose(PS[:, 1, k * P:(k + 1) * P], RAW[:, 3 + k, :], ident[:])
                    nc.tensor.transpose(PS[:, 1, 256:256 + E], RAWR[:], ident[0:E, 0:E])
                    nc.tensor.transpose(PS[:, 1, 288:288 + E * HT], RAWB1[:], ident[0:E * HT, 0:E * HT])
                    nc.tensor.transpose(PS[:, 1, 352:352 + E], RAWB2[:], ident[0:E, 0:E])
                    for f in range(2 * FT):
                        last = nc.tensor.matmul(PS[:, 2, f * P:(f + 1) * P], RAW1[:, f, :], centre[:], start=True, stop=True)
                    last.then_inc(transposed, 1)

                @block.vector
                def _(dve):
                    link = Links(dve, v_links)
                    nc.vector.memset(XH[:, B * S:(B + 1) * S].bitcast(F32), 0.0)
                    nc.vector.memset(XL[:, B * S:(B + 1) * S].bitcast(F32), 0.0)
                    nc.vector.memset(ACCT[:, 0:S], 0.0)
                    for t in range(NT):
                        if t % (NT // 4) == 0:
                            dve.wait_ge(x_loaded[t // (NT // 4)], 16)
                        nc.vector.bn_stats(STATS[:, t, :], X[:, t, :])
                    dve.wait_ge(loaded, LOADS)
                    link(nc.vector.tensor_copy(WVH[:], WVS[:]))
                    split_lo(nc, WVL[:], WVS[:], WVH[:])
                    for k, (w, scale) in enumerate(((WQS, SCALE), (WKS, 1.0))):
                        flat = w[:].rearrange("p h d -> p (h d)")
                        hi, lo = WQKH1[:, k, :, :].rearrange("p j n -> p (j n)"), WQKL1[:, k, :, :].rearrange("p j n -> p (j n)")
                        link(nc.vector.tensor_scalar(hi, flat, scale, None, ALU.mult))
                        nc.vector.scalar_tensor_tensor(lo, flat, scale, hi.bitcast(F32), ALU.mult, ALU.subtract)
                    dve.wait_ge(transposed, 1)
                    nc.vector.tensor_copy(WVO_T[:].rearrange("p k n -> p (k n)"), PS[:, 1, 0:256])
                    nc.vector.tensor_copy(WR_T[:].rearrange("p k n -> p (k n)"), PS[:, 0, 0:384])
                    nc.vector.tensor_copy(RT[:], PS[:, 1, 256:256 + E])
                    nc.vector.memset(B1_T[:, E * HT:], 0.0)
                    nc.vector.memset(B2_T[:, E:], 0.0)
                    nc.vector.tensor_copy(B1_T[:, 0:E * HT], PS[:, 1, 288:288 + E * HT])
                    nc.vector.tensor_copy(B2_T[:, 0:E], PS[:, 1, 352:352 + E])
                    link(nc.vector.tensor_copy(WV1H[:], PS[:, 1, 0:P]))
                    split_lo(nc, WV1L[:], PS[:, 1, 0:P], WV1H[:])
                    qk = PS[:, 2, :].rearrange("p (f n) -> p f n", n=P)
                    link(nc.vector.tensor_copy(WQKH[:], qk))
                    split_lo(nc, WQKL[:], qk, WQKH[:])

        def moments(dve, link):
            n = NT
            link(nc.vector.tensor_tensor(LN[:, 0, :], STATS[:, :, 1], STATS[:, :, 4], ALU.add))
            link(nc.vector.tensor_tensor(LN[:, 1, :], STATS[:, :, 1], STATS[:, :, 4], ALU.subtract))
            link(nc.vector.tensor_scalar(MEAN[:], LN[:, 0, :], 0.5, None, ALU.mult))
            link(nc.vector.tensor_tensor(LN[:, 2, :], STATS[:, :, 2], STATS[:, :, 5], ALU.add))
            link(nc.vector.scalar_tensor_tensor(LN[:, 1, :], LN[:, 1, :], 0.25, LN[:, 1, :], ALU.mult, ALU.mult))
            link(nc.vector.scalar_tensor_tensor(LN[:, 2, :], LN[:, 2, :], 1.0 / D, LN[:, 1, :], ALU.mult, ALU.add))
            link(nc.vector.tensor_scalar(LN[:, 2, :], LN[:, 2, :], LN_EPS, None, ALU.add))

        def rstd(dve, link):
            link(nc.vector.reciprocal(LN[:, 0, :], LN[:, 3, :]))
            link(nc.vector.tensor_tensor(LN[:, 0, :], LN[:, 0, :], LN[:, 2, :], ALU.mult))
            link(nc.vector.tensor_tensor(LN[:, 0, :], LN[:, 0, :], LN[:, 3, :], ALU.add))
            link(nc.vector.tensor_scalar(LN[:, 0, :], LN[:, 0, :], 0.5, None, ALU.mult))
            link(nc.vector.reciprocal(RSTD[:], LN[:, 0, :]))

        def layernorm_stage(tag, with_router):
            with ExitStack() as st:
                def tb(name, shape, dt=F32):
                    return st.enter_context(nc.sbuf_tensor(name + tag, shape, dt))

                def tsem(name):
                    return st.enter_context(nc.semaphore(name + tag))
                XS = tb("XS", [P, 2, TILES, D])
                XT = tb("XT", [P, 2, S])
                LG = tb("LG", [P, NT, E])
                LX = tb("LX", [P, NT])
                v_links, var_ready, root_ready = tsem("v_links"), tsem("var"), tsem("root")
                normed, turned, stored, kept, logits, shifted, expd, raised, lowered, lower_begun = map(
                    tsem, ("normed", "turned", "stored", "kept", "logits", "shifted", "expd", "raised", "lowered", "lower_begun"))
                with nc.Block() as block:
                    @block.scalar
                    def _(act):
                        act.wait_ge(var_ready, 1)
                        nc.scalar.activation(LN[:, 3, :], LN[:, 2, :], ACT.Sqrt).then_inc(root_ready, 1)
                        with act.Fori(0, B // 2) as b0_half:
                            for p in range(2):
                                b = 2 * b0_half + p
                                act.wait_ge(turned, b + 1)
                                act.wait_ge(lowered, b + 1)
                                nc.scalar.activation(XT[:, p, :], PS[:, p, :], ACT.Copy).then_inc(kept, 1)
                        if with_router:
                            act.wait_ge(shifted, 1)
                            nc.scalar.activation(LG[:], LG[:], ACT.Exp).then_inc(expd, 1)

                    @block.tensor
                    def _(pe):
                        with pe.Fori(0, B // 2) as b0_half:
                            for p in range(2):
                                b = 2 * b0_half + p
                                pe.wait_ge(normed, b + 1)
                                for t in range(TILES):
                                    last = nc.tensor.transpose(PS[:, p, t * P:(t + 1) * P], XS[:, p, t, :], ident[:])
                                last.then_inc(turned, 1)
                            if with_router:
                                for p in range(2):
                                    b = 2 * b0_half + p
                                    pe.wait_ge(kept, b + 1)
                                    for t in range(TILES):
                                        last = nc.tensor.matmul(PS[:, 2, bass.ds((b * TILES + t) * E, E)],
                                                                XT[:, p, t * P:(t + 1) * P], RT[:], start=True, stop=True)
                                    last.then_inc(logits, 1)

                    @block.vector
                    def _(dve):
                        link = Links(dve, v_links)
                        moments(dve, link)
                        nc.vector.tensor_scalar(LN[:, 1, :], LN[:, 1, :], 1.0, None, ALU.mult).then_inc(var_ready, 1)
                        dve.wait_ge(root_ready, 1)
                        rstd(dve, link)
                        with dve.Fori(0, B // 2) as b0_half:
                            for p in range(2):
                                b = 2 * b0_half + p
                                if with_router:
                                    dve.wait_ge(logits, b0_half * 2 + AHEAD)
                                for t in range(TILES):
                                    tok = b * TILES + t
                                    last = nc.vector.tensor_scalar(XS[:, p, t, :], X[:, bass.ds(tok, 1), :].rearrange("p a d -> p (a d)"),
                                                                   MEAN[:, bass.ds(tok, 1)], RSTD[:, bass.ds(tok, 1)],
                                                                   ALU.subtract, ALU.mult)
                                last.then_inc(normed, 1)
                            for p in range(2):
                                b = 2 * b0_half + p
                                dve.wait_ge(kept, b + 1)
                                nc.vector.tensor_copy(batch(b)[0], XT[:, p, :]).then_inc(raised, 1)
                        if with_router:
                            dve.wait_ge(logits, B + AHEAD)
                            lg = PS[:, 2, 0:NT * E].rearrange("p (t e) -> p t e", e=E)
                            wide = LX[:].unsqueeze(2).broadcast_to([P, NT, E])
                            link(nc.vector.tensor_reduce(LX[:], lg, AX.X, ALU.max))
                            nc.vector.tensor_tensor(LG[:], lg, wide, ALU.subtract).then_inc(shifted, 1)
                            dve.wait_ge(expd, 1)
                            link(nc.vector.tensor_reduce(LX[:], LG[:], AX.X, ALU.add))
                            link(nc.vector.reciprocal(LX[:], LX[:]))
                            for b in range(B):
                                nc.vector.tensor_tensor(SC[:, :, b * E:(b + 1) * E], LG[:, b * TILES:(b + 1) * TILES, :],
                                                        LX[:, b * TILES:(b + 1) * TILES].unsqueeze(2).broadcast_to([P, TILES, E]),
                                                        ALU.mult)

                    @block.gpsimd
                    def _(pool):
                        pool.sem_inc(lowered, 2)
                        with pool.Fori(0, B // 2) as b0_half:
                            for p in range(2):
                                b = 2 * b0_half + p
                                pool.wait_ge(raised, b + 1)
                                pool.sem_inc(lower_begun, 1)
                                hi, lo = batch(b)
                                nc.gpsimd.tensor_tensor(lo, XT[:, p, :], hi.bitcast(F32), ALU.subtract).then_inc(lowered, 1)

                    if with_router:
                        @block.sync
                        def _(sp):
                            sp.sem_inc(logits, AHEAD)
                            sp.dma_start(x_dram, X[:]).then_inc(stored, 16)
                            sp.wait_ge(stored, 16)

        layernorm_stage("1", False)

        with ExitStack() as st:
            def tb(name, shape, dt=F32):
                return st.enter_context(nc.sbuf_tensor(name, shape, dt))

            def tsem(name):
                return st.enter_context(nc.semaphore(name))
            STAGE = tb("STAGE", [P, 2, 2, S], F32R)
            QS = tb("QS", [P, 2, 2, S], F32R)
            KS = tb("KS", [P, 2, 2, 2, S], F32R)
            PR = tb("PR", [P, 2, 2, S])
            PT = tb("PT", [P, 2, 2, TILES, S])
            VT = tb("VT", [P, S])
            WARM = tb("WARM1", [P, 1])
            V = tb("V", [P, 2, TILES, P])
            OT = tb("OT", [P, S])
            NMAX = tb("NMAX", [P, 2, 2])
            RSUM = tb("RSUM", [P, 2, 2])
            RINV = tb("RINV", [P, 2, 2])
            s_ready = tsem("s_ready")
            max_ready = tsem("max_ready")
            exp_ready = tsem("exp_ready")
            inv_ready = tsem("inv_ready")
            p_ready = tsem("p_ready")
            t_ready = tsem("t_ready")
            ta_copied = tsem("ta_copied")
            tb_copied = tsem("tb_copied")
            q_ready = tsem("q_ready1")
            k_ready = tsem("k_ready1")
            q_split = tsem("q_split")
            k_split = tsem("k_split")
            vt_ready = tsem("vt_ready")
            vt_copied = tsem("vt_copied")
            v_ready = tsem("v_ready")
            v_copied = tsem("v_copied")
            o_ready = tsem("o_ready")
            o_copied = tsem("o_copied")
            wo_ready = tsem("wo_ready")
            added = tsem("added")
            zeros = tsem("zeros")
            moved = tsem("moved")
            MOVES = 8 * 16
            high_ready = tsem("high_ready")
            norm_begun = tsem("norm_begun")

            with nc.Block() as block:
                @block.tensor
                def _(pe):
                    def scores(n, par, i):
                        if i == 0:
                            pe.wait_ge(moved, MOVES * (n + 1))
                        for s in range(2):
                            for part in (1, 0):
                                last = nc.tensor.matmul(PS[:, 2 * (i % 2) + s, :], QS[:, par, s, i * P:(i + 1) * P],
                                                        KS[:, par, s, part, :], start=(part == 1), stop=(part == 0))
                        last.then_inc(s_ready, 1)

                    def project_q(n, pair, b):
                        product(nc, PS[:, 6, :], (WQKH1[:, 0, pair, :], WQKL1[:, 0, pair, :]), batch(b)).then_inc(q_ready, 1)

                    def project_k(n, pair, b):
                        product(nc, PS[:, 7, :], (WQKH1[:, 1, pair, :], WQKL1[:, 1, pair, :]), batch(b)).then_inc(k_ready, 1)

                    def values_t(n, pair, b):
                        pe.wait_ge(q_split, n + 1)
                        cols = slice(pair * P, (pair + 1) * P)
                        product(nc, PS[:, 6, :], (WVH[:, cols], WVL[:, cols]), batch(b)).then_inc(vt_ready, 1)

                    def values(n):
                        pe.wait_ge(vt_copied, n + 1)
                        for t in range(TILES):
                            last = nc.tensor.transpose(PS[:, 7, t * P:(t + 1) * P], VT[:, t * P:(t + 1) * P], ident[:])
                        last.then_inc(v_ready, 1)

                    def turn(c, par):
                        pe.wait_ge(p_ready, c + 1 + AHEAD)
                        pe.wait_ge(ta_copied, c + 1 + AHEAD)
                        pe.wait_ge(tb_copied, c + 1 + AHEAD)
                        for s in range(2):
                            for t in range(TILES):
                                last = nc.tensor.transpose(PS[:, 4 + s, t * P:(t + 1) * P], PR[:, par, s, t * P:(t + 1) * P],
                                                           ident[:])
                        last.then_inc(t_ready, 1)

                    def outputs(n, par, tiles):
                        if tiles[0] == 0:
                            pe.wait_ge(ta_copied, 4 * n + 5 + AHEAD)
                            pe.wait_ge(tb_copied, 4 * n + 5 + AHEAD)
                            pe.wait_ge(v_copied, n + 1 + AHEAD)
                        for t in tiles:
                            for s in range(2):
                                last = nc.tensor.matmul(PS[DH * s:DH * (s + 1), 7, :], V[:, par, t, DH * s:DH * (s + 1)],
                                                        PT[:, par, s, t, :], start=(t == 0), stop=(t == TILES - 1),
                                                        skip_group_check=True)
                        if tiles[-1] == TILES - 1:
                            last.then_inc(o_ready, 1)

                    def project_out(n, pair):
                        pe.wait_ge(o_copied, n + 2)
                        nc.tensor.matmul(PS[:, 6, :], WO[:, pair, :], OT[:], start=True, stop=True).then_inc(wo_ready, 1)

                    pe.wait_ge(zeros, 1)
                    project_q(0, 0, 0)
                    project_k(0, 0, 0)
                    values_t(0, 0, 0)
                    pe.wait_ge(k_split, 1)
                    values(0)
                    with pe.Fori(0, B) as b:
                        for h in range(PAIRS):
                            n = b * PAIRS + h
                            par, nxt = h % 2, (h + 1) % PAIRS
                            nb = b + (h + 1) // PAIRS
                            scores(n, par, 0)
                            pe.wait_ge(added, n + AHEAD)
                            project_q(n + 1, nxt, nb)
                            pe.wait_ge(v_copied, n + 1 + AHEAD)
                            project_k(n + 1, nxt, nb)
                            turn(4 * n - 1, 1)
                            scores(n, par, 1)
                            values_t(n + 1, nxt, nb)
                            pe.wait_ge(k_split, n + 2)
                            outputs(n - 1, 1 - par, range(0, 2))
                            turn(4 * n, 0)
                            scores(n, par, 2)
                            outputs(n - 1, 1 - par, range(2, TILES))
                            turn(4 * n + 1, 1)
                            scores(n, par, 3)
                            pe.wait_ge(vt_copied, n + 2)
                            project_out(n - 1, (h - 1) % PAIRS)
                            values(n + 1)
                            turn(4 * n + 2, 0)
                    n = B * PAIRS
                    turn(4 * n - 1, 1)
                    pe.wait_ge(v_copied, n + 1 + AHEAD)
                    outputs(n - 1, 1, range(TILES))
                    pe.wait_ge(added, n + AHEAD)
                    project_out(n - 1, PAIRS - 1)

                @block.vector
                def _(dve):
                    def row_max(c, par):
                        dve.wait_ge(s_ready, c + 1)
                        nc.vector.tensor_reduce(NMAX[:, par, :], PS[:, 2 * par:2 * par + 2, :], AX.X, ALU.max,
                                                negate=True).then_inc(max_ready, 1)

                    def invert(c, par):
                        dve.wait_ge(exp_ready, c + 1)
                        nc.vector.reciprocal(RINV[:, par, :], RSUM[:, par, :]).then_inc(inv_ready, 1)

                    def copy_turned(c, par, i):
                        dve.wait_ge(t_ready, c + 2)
                        nc.vector.tensor_copy(PT[:, par, 0, :, i * P:(i + 1) * P],
                                              PS[:, 4, :].rearrange("p (t q) -> p t q", q=P)).then_inc(ta_copied, 1)

                    def split_low(n, s):
                        dve.wait_ge(high_ready, 2 * n + s + 1)
                        split_lo(nc, STAGE[:, s, 1, :], PS[:, 6 + s, :], STAGE[:, s, 0, :]).then_inc((q_split, k_split)[s], 1)

                    def copy_vt(n):
                        dve.wait_ge(vt_ready, n + 1)
                        nc.vector.tensor_copy(VT[:], PS[:, 6, :]).then_inc(vt_copied, 1)

                    def copy_o(n):
                        dve.wait_ge(o_ready, n + 2)
                        nc.vector.tensor_copy(OT[:], PS[:, 7, :]).then_inc(o_copied, 1)

                    def accumulate(n, block_at, first):
                        dve.wait_ge(wo_ready, n + 2)
                        dve.wait_ge(added, n + 1 + AHEAD)
                        acc = ACCT[:, bass.ds(block_at * S, S)]
                        if first:
                            nc.vector.tensor_copy(acc, PS[:, 6, :]).then_inc(added, 1)
                        else:
                            nc.vector.tensor_tensor(acc, PS[:, 6, :], acc, ALU.add).then_inc(added, 1)

                    dve.sem_inc(ta_copied, AHEAD)
                    dve.sem_inc(added, AHEAD)
                    nc.vector.memset(WARM[:], 0.0)
                    nc.vector.memset(PR[:, 1, :, :], 0.0)
                    nc.vector.memset(PT[:, 1, :, :, :], 0.0)
                    nc.vector.memset(V[:, 1, :, :], 0.0).then_inc(zeros, 1)
                    split_low(0, 0)
                    split_low(0, 1)
                    copy_vt(0)
                    with dve.Fori(0, B) as b:
                        for h in range(PAIRS):
                            n = b * PAIRS + h
                            par = h % 2
                            row_max(4 * n, 0)
                            split_low(n + 1, 0)
                            split_low(n + 1, 1)
                            copy_turned(4 * n - 1, 1 - par, 3)
                            invert(4 * n, 0)
                            row_max(4 * n + 1, 1)
                            copy_vt(n + 1)
                            invert(4 * n + 1, 1)
                            copy_turned(4 * n, par, 0)
                            row_max(4 * n + 2, 0)
                            copy_o(n - 1)
                            invert(4 * n + 2, 0)
                            copy_turned(4 * n + 1, par, 1)
                            row_max(4 * n + 3, 1)
                            accumulate(n - 1, b if h == 0 else b + 1, h == 1)
                            invert(4 * n + 3, 1)
                            copy_turned(4 * n + 2, par, 2)
                    n = B * PAIRS
                    copy_turned(4 * n - 1, 1, 3)
                    copy_o(n - 1)
                    accumulate(n - 1, B, False)

                @block.scalar
                def _(act):
                    def exps(c, par):
                        act.wait_ge(max_ready, c + 1)
                        for s in range(2):
                            last = nc.scalar.activation(PR[:, par, s, :], PS[:, 2 * par + s, :], ACT.Exp,
                                                        bias=NMAX[:, par, s:s + 1], accum_out=RSUM[:, par, s:s + 1])
                        last.then_inc(exp_ready, 1)

                    def take_high(n, s):
                        act.wait_ge((q_ready, k_ready)[s], n + 1)
                        if not isinstance(n, int):
                            act.wait_ge(moved, MOVES * n)
                        nc.scalar.activation(STAGE[:, s, 0, :], PS[:, 6 + s, :], ACT.Copy).then_inc(high_ready, 1)

                    def copy_turned(c, par, i):
                        act.wait_ge(t_ready, c + 2)
                        nc.scalar.activation(PT[:, par, 1, :, i * P:(i + 1) * P],
                                             PS[:, 5, :].rearrange("p (t q) -> p t q", q=P), ACT.Copy).then_inc(tb_copied, 1)

                    def copy_v(n, par):
                        act.wait_ge(v_ready, n + 1)
                        nc.scalar.activation(V[:, par, :, :], PS[:, 7, :].rearrange("p (t q) -> p t q", q=P),
                                             ACT.Copy).then_inc(v_copied, 1)

                    act.sem_inc(tb_copied, AHEAD)
                    act.sem_inc(v_copied, AHEAD)
                    act.wait_ge(zeros, 1)
                    nc.scalar.activation(WARM[:], WARM[:], ACT.Exp)
                    take_high(0, 0)
                    take_high(0, 1)
                    copy_v(0, 0)
                    with act.Fori(0, B) as b:
                        for h in range(PAIRS):
                            n = b * PAIRS + h
                            par = h % 2
                            take_high(n + 1, 0)
                            take_high(n + 1, 1)
                            exps(4 * n, 0)
                            copy_turned(4 * n - 1, 1 - par, 3)
                            exps(4 * n + 1, 1)
                            copy_turned(4 * n, par, 0)
                            exps(4 * n + 2, 0)
                            copy_turned(4 * n + 1, par, 1)
                            exps(4 * n + 3, 1)
                            copy_v(n + 1, 1 - par)
                            copy_turned(4 * n + 2, par, 2)
                    copy_turned(4 * B * PAIRS - 1, 1, 3)

                @block.sync
                def _(sp):
                    def move(n, par):
                        halves = slice(0, DH), slice(DH, P)
                        sp.wait_ge(q_split, n + 1)
                        for s in range(2):
                            sp.dma_start(QS[halves[s], par, s, :].bitcast(F32), STAGE[halves[s], 0, 0, :].bitcast(F32)).then_inc(moved, 16)
                            sp.dma_start(QS[halves[1 - s], par, s, :].bitcast(F32),
                                         STAGE[halves[s], 0, 1, :].bitcast(F32)).then_inc(moved, 16)
                        sp.wait_ge(k_split, n + 1)
                        for s in range(2):
                            for half in halves:
                                sp.dma_start(KS[half, par, s, :, :].bitcast(F32),
                                             STAGE[halves[s], 1, :, :].bitcast(F32)).then_inc(moved, 16)

                    move(0, 0)
                    with sp.Fori(0, B * PAIRS // 2) as n_half:
                        for p in range(2):
                            move(2 * n_half + p + 1, 1 - p)
                    sp.wait_ge(moved, MOVES * (B * PAIRS + 1))

                @block.gpsimd
                def _(pool):
                    def normalise(c, par):
                        pool.wait_ge(inv_ready, c + 1)
                        pool.sem_inc(norm_begun, 1)
                        for s in range(2):
                            last = nc.gpsimd.tensor_scalar(PR[:, par, s, :], PR[:, par, s, :], RINV[:, par, s:s + 1], 1.0,
                                                           ALU.mult, ALU.mult)
                        last.then_inc(p_ready, 1)

                    pool.sem_inc(p_ready, AHEAD)
                    with pool.Fori(0, 2 * B * PAIRS) as c0_half:
                        c0 = 2 * c0_half
                        for p in range(2):
                            normalise(c0 + p, p)

        with ExitStack() as st:
            def tb(name, shape, dt=F32):
                return st.enter_context(nc.sbuf_tensor(name, shape, dt))

            def tsem(name):
                return st.enter_context(nc.semaphore(name))
            XP = tb("XP", [P, 2, S + 1])
            XD = tb("XD", [P, 2, S])
            XR = tb("XR", [P, 2, 2, S])
            R = tb("R", [P, 2, S])
            K = tb("K", [P, 2, S])
            Y = tb("Y", [P, 2, S])
            X1 = tb("X1", [P, 2, TILES, D])
            links, mixed, rk_ready, r_done, k_done, v_ready, y_done, y_turned = map(
                tsem, ("links2", "mixed", "rk_ready", "r_done", "k_done", "v2_ready", "y_done", "y_turned"))
            k_pos = tsem("k_pos")
            with nc.Block() as block:
                @block.vector
                def _(dve):
                    def mix(b, p, base):
                        link = Links(dve, links, base)
                        hi, lo = batch(b)
                        link(nc.vector.tensor_tensor(XP[:, p, 1:S + 1], hi.bitcast(F32), lo.bitcast(F32), ALU.add))
                        link(nc.vector.tensor_tensor(XD[:, p, :], XP[:, p, 1:S + 1], XP[:, p, 0:S], ALU.subtract))
                        for k in range(2):
                            last = nc.vector.scalar_tensor_tensor(XR[:, p, k, :], XD[:, p, :], MU[:, k:k + 1], XP[:, p, 0:S],
                                                                  ALU.mult, ALU.add)
                        last.then_inc(mixed, 1)
                        return link

                    def gate(b, p, base):
                        link = Links(dve, links, base)
                        dve.wait_ge(v_ready, b + 1)
                        dve.wait_ge(r_done, b + 1)
                        link(nc.vector.tensor_tensor(Y[:, p, :], PS[:, 4 + p, :], R[:, p, :], ALU.mult))
                        nc.vector.tensor_tensor(Y[:, p, :], Y[:, p, :], ACCT[:, bass.ds((b + 1) * S, S)],
                                                ALU.add).then_inc(y_done, 1)

                    def finish(b, p, base):
                        link = Links(dve, links, base)
                        dve.wait_ge(y_turned, b + 1)
                        link(nc.vector.tensor_tensor(X1[:, p, :, :], PS[:, 6 + p, :].rearrange("p (t d) -> p t d", d=D),
                                                     X[:, bass.ds(b * TILES, TILES), :], ALU.add))
                        for t in range(TILES):
                            nc.vector.bn_stats(STATS[:, bass.ds(b * TILES + t, 1), :].rearrange("p a s -> p (a s)"), X1[:, p, t, :])
                        link(nc.vector.tensor_copy(X[:, bass.ds(b * TILES, TILES), :], X1[:, p, :, :]))

                    link = Links(dve, links)
                    link(nc.vector.memset(XP[:, 0, 0:1], 0.0))
                    link(nc.vector.memset(XP[:, 1, 0:1], 0.0))
                    mix(0, 0, 2)
                    mix(1, 1, 4)
                    gate(0, 0, 6)
                    with dve.Fori(0, B // 2 - 1) as b_half:
                        for q in range(2):
                            b, p, base = 2 * b_half + q + 1, 1 - q, 7 + 5 * (2 * b_half + q)
                            mix(b + 1, 1 - p, base)
                            gate(b, p, base + 2)
                            finish(b - 1, 1 - p, base + 3)
                    base = 7 + 5 * (B - 2)
                    mix(B, 0, base)
                    gate(B - 1, 1, base + 2)
                    finish(B - 2, 0, base + 3)
                    finish(B - 1, 1, base + 5)

                @block.tensor
                def _(pe):
                    def receptance_and_key(b, p):
                        pe.wait_ge(mixed, b + 1)
                        for k in range(2):
                            last = nc.tensor.matmul(PS[:, 2 * p + k, :], WR_T[:, k, :], XR[:, p, k, :], start=True, stop=True)
                        last.then_inc(rk_ready, 1)

                    receptance_and_key(0, 0)
                    with pe.Fori(0, B // 2) as b0_half:
                        for p in range(2):
                            b = 2 * b0_half + p
                            pe.wait_ge(k_done, b + 1)
                            nc.tensor.matmul(PS[:, 4 + p, :], WR_T[:, 2, :], K[:, p, :], start=True, stop=True).then_inc(v_ready, 1)
                            receptance_and_key(b + 1, 1 - p)
                            pe.wait_ge(y_done, b + 1)
                            for t in range(TILES):
                                last = nc.tensor.transpose(PS[:, 6 + p, t * P:(t + 1) * P], Y[:, p, t * P:(t + 1) * P], ident[:])
                            last.then_inc(y_turned, 1)

                @block.scalar
                def _(act):
                    def gates(b, p):
                        act.wait_ge(rk_ready, b + 1)
                        nc.scalar.activation(K[:, p, :], PS[:, 2 * p + 1, :], ACT.Relu).then_inc(k_pos, 1)
                        nc.scalar.activation(R[:, p, :], PS[:, 2 * p, :], ACT.Sigmoid).then_inc(r_done, 1)
                        act.wait_ge(k_pos, b + 1)
                        nc.scalar.activation(K[:, p, :], K[:, p, :], ACT.Square).then_inc(k_done, 1)

                    gates(0, 0)
                    with act.Fori(0, B // 2) as b0_half:
                        for p in range(2):
                            gates(2 * b0_half + p + 1, 1 - p)

        first_layer.close()
        layernorm_stage("2", True)
        stream.close()

        with ExitStack() as st:
            def tb(name, shape, dt=F32):
                return st.enter_context(nc.sbuf_tensor(name, shape, dt))

            def tsem(name):
                return st.enter_context(nc.semaphore(name))
            RING, AWAY = 4, 3
            SC_AHEAD = RING * TILES
            V1 = tb("V1", [P, TILES, H1, SLOT])
            A = tb("A", [P, 2 * HPG, TILES, S])
            YN = tb("YN", [P, TILES, P])
            EPS = tb("EPS", [P, 2])
            EP4 = tb("EP4", [P, HPG])
            SCT = tb("SCT", [B * E, S])
            LEFT = tb("LEFT", [B * E, S])
            TOP = tb("TOP", [B * E, 8])
            LAST = tb("LAST", [B * E, 8])
            ROUNDS = CAPACITY // 8 // B
            turned, gated, stored, cleared, taken, take_begun = map(
                tsem, ("sc_turned", "gated", "gate_stored", "cleared", "taken", "take_begun"))
            XB = tb("XB", [P, 2, S], F32R)
            PJ = tb("PJ", [P, TILES, S])
            VAR = tb("VAR", [P, TILES, 2 * H1])
            QK = tb("QK", [P, S])
            SQ = QK
            STAGE = tb("STAGE4", [P, 2, 2, S], F32R)
            QS = tb("QS4", [P, GROUPS, S], F32R)
            KS = tb("KS4", [P, GROUPS, 2, S], F32R)
            KMH = tb("KMH", [P, RING, S], F32R)
            KML = tb("KML", [P, RING, S], F32R)
            ND = tb("ND", [P, S])
            RD = tb("RD", [P, TILES, HPG])
            YT = ACCT[:, 0:S]
            links, pj_ready, pj_copied, squared, summed, root_done, pj_normed, xb_ready = map(
                tsem, ("links4", "pj_ready", "pj_copied", "squared4", "summed4", "root_done", "pj_normed", "xb_ready"))
            qk_turned, q_ready, k_ready, kh_ready, kl_ready, v_ready, v_copied = map(
                tsem, ("qk_turned", "q_ready", "k_ready", "kh_ready", "kl_ready", "v_ready4", "v_copied4"))
            sc_ready, sq_done, masked, nd_ready, nd_copied, five_ready, five_read = map(
                tsem, ("sc_ready", "sq_done", "masked", "nd_ready", "nd_copied", "five_ready", "five_read"))
            mask_begun, q_moved, k_moved = map(tsem, ("mask_begun", "q_moved", "k_moved"))
            MOVES = 4 * 16
            FIVES = GROUPS + 2
            with nc.Block() as block:
                @block.tensor
                def _(pe):
                    def project(n, t, bank):
                        for k, (x, w) in enumerate(((1, WQKH), (0, WQKH), (0, WQKL))):
                            last = nc.tensor.matmul(PS[:, bank, :], XB[:, x, t * P:(t + 1) * P], w[:].rearrange("p f n -> p (f n)"),
                                                    start=(k == 0), stop=(k == 2))
                        last.then_inc(pj_ready, 1)

                    def turn(m, f, bank):
                        for t in range(TILES):
                            last = nc.tensor.transpose(PS[:, bank, t * P:(t + 1) * P], PJ[:, t, (FT * m + f) * P:(FT * m + f + 1) * P],
                                                       ident[:])
                        last.then_inc(qk_turned, 1)

                    def values():
                        for t in range(TILES):
                            for k, (x, w) in enumerate(((1, WV1H), (0, WV1H), (0, WV1L))):
                                last = nc.tensor.matmul(PS[:, 5, t * P:(t + 1) * P], XB[:, x, t * P:(t + 1) * P], w[:],
                                                        start=(k == 0), stop=(k == 2))
                        last.then_inc(v_ready, 1)

                    def scores(b, h):
                        hh = H1 * b + h
                        slot = h % RING
                        if h % HPT == 0:
                            pe.wait_ge(q_moved, MOVES * (FT * b + h // HPT + 1))
                        pe.wait_ge(kh_ready, hh + 1)
                        pe.wait_ge(kl_ready, hh + 1)
                        for t in range(TILES):
                            pe.wait_ge(sq_done, TILES * hh + t + 1)
                            keys = slice(t * P, (t + 1) * P)
                            queries = QS[:, h // HPG, t * P:S]
                            nc.tensor.matmul(PS[:, t, t * P:S], KML[:, slot, keys], queries, start=True, stop=False)
                            nc.tensor.matmul(PS[:, t, t * P:S], KMH[:, slot, keys], queries, start=False, stop=True).then_inc(sc_ready, 1)

                    def outputs(g, r):
                        pe.wait_ge(masked, HPG * (g + 1) + AHEAD)
                        pe.wait_ge(nd_copied, g + 1 + AHEAD)
                        for t in range(TILES):
                            for i in range(HPG):
                                last = nc.tensor.matmul(PS[SLOT * i:SLOT * (i + 1), 4, t * P:S], V1[:, t, HPG * (r % GROUPS) + i, :],
                                                        A[:, HPG * (r % 2) + i, t, t * P:S], start=(t == 0), stop=(t == TILES - 1),
                                                        skip_group_check=True)
                        last.then_inc(nd_ready, 1)

                    def turn_outputs(g, r, use):
                        pe.wait_ge(nd_copied, g + 2 + AHEAD)
                        pe.wait_ge(five_read, use + AHEAD)
                        for t in range(TILES):
                            last = nc.tensor.transpose(PS[:, 5, t * P:(t + 1) * P], ND[:, t * P:(t + 1) * P], ident[:])
                        last.then_inc(five_ready, 1)

                    def turn_back(use):
                        pe.wait_ge(five_read, use + AHEAD)
                        for t in range(TILES):
                            last = nc.tensor.transpose(PS[:, 5, t * P:(t + 1) * P], YN[:, t, :], ident[:])
                        last.then_inc(five_ready, 1)

                    def project_out(use):
                        pe.wait_ge(five_read, use + AHEAD)
                        nc.tensor.matmul(PS[:, 5, :], WVO_T[:, 1, :], YT, start=True, stop=True).then_inc(five_ready, 1)

                    for t in range(TILES):
                        last = nc.tensor.transpose(PS[0:B * E, 0, t * P:(t + 1) * P], SC[:, t, :], ident[:])
                    last.then_inc(turned, 1)
                    pe.sem_inc(sc_ready, SC_AHEAD)
                    pe.wait_ge(xb_ready, 1)
                    for t in range(TILES):
                        if t >= 2:
                            pe.wait_ge(pj_copied, t - 1)
                        project(t, t, 6 + t % 2)
                    pe.wait_ge(cleared, 6 + HPG)
                    pe.wait_ge(pj_normed, 1)
                    turn(0, 0, 6)
                    turn(1, 0, 7)
                    with pe.Fori(0, B) as b:
                        g, use = GROUPS * b, FIVES * b
                        for h in range(H1):
                            scores(b, h)
                            if h == 0:
                                pe.wait_ge(k_ready, 2 * b + 1)
                                turn(0, 1, 6)
                                turn(1, 1, 7)
                                pe.wait_ge(five_read, use + AHEAD)
                                values()
                            elif h == 1:
                                outputs(g - 1, -1)
                            elif h == 2:
                                pe.wait_ge(xb_ready, b + 2)
                                pe.wait_ge(k_ready, 2 * b + 2)
                                project(4 * b + 4, 0, 6)
                            elif h == 3:
                                pe.wait_ge(v_copied, b + 1)
                                turn_outputs(g - 1, 3, use)
                                project(4 * b + 5, 1, 7)
                            elif h == 4:
                                turn_back(use + 1)
                                pe.wait_ge(pj_copied, TILES * b + TILES + 1)
                                project(4 * b + 6, 2, 6)
                            elif h == 5:
                                outputs(g, 0)
                                pe.wait_ge(pj_copied, TILES * b + TILES + 2)
                                project(4 * b + 7, 3, 7)
                                project_out(use + 2)
                            elif h == 7:
                                turn_outputs(g, 0, use + 3)
                            elif h == 9:
                                outputs(g + 1, 1)
                            if h == 9:
                                pe.wait_ge(pj_normed, b + 2)
                                turn(0, 0, 6)
                                turn(1, 0, 7)
                            elif h == 11:
                                turn_outputs(g + 1, 1, use + 4)
                            elif h == 13:
                                outputs(g + 2, 2)
                            elif h == 15:
                                turn_outputs(g + 2, 2, use + 5)
                    outputs(GROUPS * B - 1, GROUPS - 1)
                    turn_outputs(GROUPS * B - 1, GROUPS - 1, FIVES * B)
                    turn_back(FIVES * B + 1)
                    project_out(FIVES * B + 2)

                @block.scalar
                def _(act):
                    def squares(hh, h):
                        for t in range(TILES):
                            act.wait_ge(sc_ready, TILES * hh + t + 1 + SC_AHEAD)
                            nc.scalar.activation(A[:, h % (2 * HPG), t, t * P:S], PS[:, t, t * P:S], ACT.Square,
                                                 scale=FEAT ** -0.5).then_inc(sq_done, 1)

                    def copy_projection(n, t, bank):
                        act.wait_ge(pj_ready, n + 1)
                        if not isinstance(n, int) or n:
                            act.wait_ge(summed, n)
                        nc.scalar.activation(SQ[:], PS[:, bank, :], ACT.Square).then_inc(squared, 1)
                        nc.scalar.activation(PJ[:, t, :], PS[:, bank, :], ACT.Copy).then_inc(pj_copied, 1)

                    def root(b):
                        act.wait_ge(summed, TILES * b + TILES)
                        nc.scalar.activation(VAR[:], VAR[:], ACT.Sqrt, bias=EPS[:, 0:1], scale=1.0 / FEAT).then_inc(root_done, 1)

                    def copy_outputs(g, prior):
                        act.wait_ge(nd_ready, g + 2)
                        if prior is not None:
                            act.wait_ge(five_ready, prior)
                        nc.scalar.activation(ND[:], PS[:, 4, :], ACT.Identity, bias=EPS[:, 1:2]).then_inc(nd_copied, 1)

                    act.sem_inc(sq_done, TILES)
                    act.sem_inc(nd_copied, AHEAD)
                    act.wait_ge(cleared, 4 + HPG)
                    for t in range(TILES):
                        copy_projection(t, t, 6 + t % 2)
                    root(0)
                    with act.Fori(0, B) as b:
                        for h in range(H1):
                            squares(H1 * b + h, h)
                            if 2 <= h < 6:
                                copy_projection(TILES * b + h + 2, h - 2, 6 + h % 2)
                            if h == 7:
                                root(b + 1)
                            if h % 4 == 1:
                                copy_outputs(GROUPS * b + h // 4 - 1, {1: None, 5: FIVES * b + 1, 9: FIVES * b + 4, 13: FIVES * b + 5}[h])
                    copy_outputs(GROUPS * B - 1, FIVES * B)

                @block.vector
                def _(dve):
                    def load_batch(b):
                        hi, lo = batch(b)
                        nc.vector.tensor_copy(XB[:, 0, :], hi.bitcast(F32))
                        nc.vector.tensor_copy(XB[:, 1, :], lo.bitcast(F32)).then_inc(xb_ready, 1)

                    def sum_squares(b, t):
                        dve.wait_ge(squared, TILES * b + t + 1)
                        nc.vector.tensor_reduce(VAR[:, t, :], SQ[:].rearrange("p (h i) -> p h i", i=FEAT), AX.X,
                                                ALU.add).then_inc(summed, 1)

                    def norm(b, link):
                        dve.wait_ge(root_done, b + 1)
                        link(nc.vector.reciprocal(VAR[:], VAR[:]))
                        for t in range(TILES):
                            heads = PJ[:, t, :].rearrange("p (h i) -> p h i", i=FEAT)
                            last = nc.vector.tensor_tensor(heads, heads,
                                                           VAR[:, t, :].unsqueeze(2).broadcast_to([P, 2 * H1, FEAT]), ALU.mult)
                        last.then_inc(pj_normed, 1)

                    def take_turned(m, u, bank, link):
                        dve.wait_ge(qk_turned, 2 * u + m + 1)
                        if m == 1:
                            dve.wait_ge(q_ready, u + 1)
                        if not isinstance(u, int):
                            dve.wait_ge((q_moved, k_moved)[m], MOVES * u)
                        link(nc.vector.tensor_scalar(QK[:], PS[:, bank, :], GB[:, 0:1], GB[:, 1:2], ALU.mult, ALU.add))
                        link(nc.vector.tensor_copy(STAGE[:, m, 0, :], QK[:]))
                        split_lo(nc, STAGE[:, m, 1, :], QK[:], STAGE[:, m, 0, :]).then_inc((q_ready, k_ready)[m], 1)

                    def mask_high(hh, h):
                        dve.wait_ge(sc_ready, TILES * (hh - RING + 1) + SC_AHEAD)
                        nc.vector.tensor_scalar(KMH[:, h % RING, :], KS[:, h // HPG, 0, :].bitcast(F32), head_mask[:, h % HPG:h % HPG + 1],
                                                None, ALU.mult).then_inc(kh_ready, 1)

                    def divide(r, use, link):
                        dve.wait_ge(five_ready, use + 1)
                        dve.wait_ge(five_read, use + AHEAD)
                        slots = PS[:, 5, :].rearrange("p (t h s) -> p t h s", h=HPG, s=SLOT)
                        link(nc.vector.reciprocal(RD[:].unsqueeze(3), slots[:, :, :, HD:HD + 1]))
                        y = YN[:, :, SLOT * r:SLOT * (r + 1)].rearrange("p t (h d) -> p t h d", d=HD)
                        nc.vector.tensor_tensor(y, slots[:, :, :, 0:HD], RD[:].unsqueeze(3).broadcast_to([P, TILES, HPG, HD]),
                                                ALU.mult).then_inc(five_read, 1)

                    def copy_back(use):
                        dve.wait_ge(five_ready, use + 1)
                        nc.vector.tensor_copy(YT, PS[:, 5, :]).then_inc(five_read, 1)

                    def add_output(b, use):
                        dve.wait_ge(five_ready, use + 1)
                        nc.vector.tensor_copy(ACCT[:, bass.ds((b + 1) * S, S)], PS[:, 5, :]).then_inc(five_read, 1)

                    def take(n):
                        for r in range(ROUNDS):
                            nc.vector.max(TOP[:], LEFT[:]).then_inc(taken, 1)
                            dve.wait_ge(taken, n + 2 * r + 2)
                            dve.sem_inc(take_begun, 1)
                            nc.vector.match_replace(LEFT[:], TOP[:], LEFT[:], -1.0).then_inc(taken, 1)
                            dve.wait_ge(taken, n + 2 * r + 3)
                            dve.sem_inc(take_begun, 1)

                    def take_rest(n):
                        rest = CAPACITY - 8 * ROUNDS * B
                        link = Links(dve, taken, n)
                        while rest > 0:
                            link(nc.vector.max(TOP[:], LEFT[:]))
                            if rest < 8:
                                link(nc.vector.memset(LAST[:], -1.0))
                                link(nc.vector.tensor_copy(LAST[:, 0:rest], TOP[:, 0:rest]))
                            link(nc.vector.match_replace(LEFT[:], LAST[:] if rest < 8 else TOP[:], LEFT[:], -1.0))
                            rest -= 8
                        nc.vector.scalar_tensor_tensor(LEFT[:], LEFT[:], 0.0, SCT[:], ALU.is_lt, ALU.mult).then_inc(gated, 1)

                    load_batch(0)
                    dve.wait_ge(turned, 1)
                    nc.vector.tensor_copy(SCT[:], PS[0:B * E, 0, :])
                    nc.vector.tensor_copy(LEFT[:], PS[0:B * E, 0, :]).then_inc(taken, 1)
                    dve.sem_inc(five_read, AHEAD)
                    for t in range(TILES):
                        sum_squares(0, t)
                    link = Links(dve, links)
                    norm(0, link)
                    take_turned(0, 0, 6, link)
                    take_turned(1, 0, 7, link)
                    dve.wait_ge(k_moved, MOVES)
                    mask_high(0, 0)
                    mask_high(1, 1)
                    mask_high(2, 2)
                    PER_B = 4 * 2 + GROUPS + 1
                    base = link.n
                    with dve.Fori(0, B) as b:
                        link = Links(dve, links, base + PER_B * b)
                        use = FIVES * b
                        for h in range(H1):
                            if h == H1 - AWAY:
                                dve.wait_ge(k_moved, MOVES * (2 * b + 3))
                            elif h == HPT - AWAY:
                                dve.wait_ge(k_moved, MOVES * (2 * b + 2))
                            mask_high(H1 * b + h + AWAY, (h + AWAY) % H1)
                            if h == 1:
                                take_turned(0, 2 * b + 1, 6, link)
                                take_turned(1, 2 * b + 1, 7, link)
                                dve.wait_ge(v_ready, b + 1)
                                load_batch(b + 1)
                            elif h == 2:
                                dve.wait_ge(nd_ready, GROUPS * b + 1)
                                nc.vector.tensor_copy(V1[:, :, :, 0:HD].rearrange("p t h d -> p (t h) d"),
                                                      PS[:, 5, :].rearrange("p (c d) -> p c d", d=HD)).then_inc(v_copied, 1)
                            elif h == 3:
                                sum_squares(b + 1, 0)
                                divide(3, use, link)
                            elif h == 4:
                                sum_squares(b + 1, 1)
                                copy_back(use + 1)
                            elif h == 5:
                                sum_squares(b + 1, 2)
                                add_output(b - 1, use + 2)
                            elif h == 6:
                                sum_squares(b + 1, 3)
                            elif h == 7:
                                divide(0, use + 3, link)
                            elif h == 8:
                                norm(b + 1, link)
                            elif h == 9:
                                take_turned(0, 2 * b + 2, 6, link)
                            elif h == 10:
                                take_turned(1, 2 * b + 2, 7, link)
                            elif h == 11:
                                divide(1, use + 4, link)
                            elif h == 14:
                                take(2 * ROUNDS * b)
                            elif h == 15:
                                divide(2, use + 5, link)
                    take_rest(2 * ROUNDS * B + 1)
                    link = Links(dve, links, base + PER_B * B)
                    divide(3, FIVES * B, link)
                    copy_back(FIVES * B + 1)
                    add_output(B - 1, FIVES * B + 2)

                @block.sync
                def _(sp):
                    def move(u, f):
                        halves = slice(0, P // 2), slice(P // 2, P)
                        sp.wait_ge(q_ready, u + 1)
                        for a in range(2):
                            for part in range(2):
                                sp.dma_start(QS[halves[part], 2 * f + a, :].bitcast(F32),
                                             STAGE[halves[a], 0, part, :].bitcast(F32)).then_inc(q_moved, 16)
                        sp.wait_ge(k_ready, u + 1)
                        for a in range(2):
                            for half in halves:
                                sp.dma_start(KS[half, 2 * f + a, :, :].bitcast(F32),
                                             STAGE[halves[a], 1, :, :].bitcast(F32)).then_inc(k_moved, 16)

                    move(0, 0)
                    with sp.Fori(0, B) as b:
                        move(2 * b + 1, 1)
                        move(2 * b + 2, 0)
                    sp.wait_ge(q_moved, MOVES * (FT * B + 1))
                    sp.wait_ge(k_moved, MOVES * (FT * B + 1))
                    sp.wait_ge(gated, 1)
                    sp.dma_start(gate_dram, LEFT[:]).then_inc(stored, 16)
                    sp.wait_ge(stored, 16)

                @block.gpsimd
                def _(pool):
                    def mask_low(hh, h):
                        pool.wait_ge(sc_ready, TILES * (hh - RING + 1) + SC_AHEAD)
                        pool.sem_inc(mask_begun, 1)
                        nc.gpsimd.tensor_scalar(KML[:, h % RING, :], KS[:, h // HPG, 1, :].bitcast(F32), head_mask[:, h % HPG:h % HPG + 1],
                                                1.0, ALU.mult, ALU.mult).then_inc(kl_ready, 1)

                    nc.gpsimd.memset(EPS[:, 0:1], LN_EPS)
                    nc.gpsimd.memset(EPS[:, 1:2], 0.0).then_inc(cleared, 1)
                    pool.wait_ge(cleared, 1)
                    nc.gpsimd.memset(EP4[:], DEN_EPS).then_inc(cleared, 1)
                    pool.wait_ge(cleared, 2)
                    for n, (base, sign) in enumerate(((-HD, 1), (2 * HD - 1, -1))):
                        nc.gpsimd.affine_select(out=EP4[:], in_=EP4[:], compare_op=ALU.is_ge, fill=0.0, base=base,
                                                pattern=[[-SLOT * sign, HPG]], channel_multiplier=sign).then_inc(cleared, 1)
                        pool.wait_ge(cleared, 3 + n)
                    for i in range(HPG):
                        nc.gpsimd.tensor_tensor(EPS[:, 1:2], EPS[:, 1:2], EP4[:, i:i + 1], ALU.add).then_inc(cleared, 1)
                        pool.wait_ge(cleared, 5 + i)
                    nc.gpsimd.memset(YN[:], 0.0)
                    nc.gpsimd.memset(V1[:], 0.0).then_inc(cleared, 1)
                    pool.wait_ge(cleared, 5 + HPG)
                    nc.gpsimd.memset(V1[:, :, :, HD:2 * HD], 1.0)
                    nc.gpsimd.memset(A[:, HPG:2 * HPG, :, :], 0.0).then_inc(cleared, 1)
                    pool.sem_inc(masked, AHEAD)
                    pool.wait_ge(k_moved, MOVES)
                    mask_low(0, 0)
                    mask_low(1, 1)
                    mask_low(2, 2)
                    with pool.Fori(0, B) as b:
                        for h in range(H1):
                            if h == H1 - AWAY:
                                pool.wait_ge(k_moved, MOVES * (2 * b + 3))
                            elif h == HPT - AWAY:
                                pool.wait_ge(k_moved, MOVES * (2 * b + 2))
                            mask_low(H1 * b + h + AWAY, (h + AWAY) % H1)
                            pool.wait_ge(sq_done, TILES * (H1 * b + h + 1) + TILES)
                            slot = A[:, h % (2 * HPG), 0, 0:P]
                            diag = bass.AP(slot.tensor, slot.offset, [A[:].ap[0], [S + P, TILES], [1, P]])
                            nc.gpsimd.tensor_tensor(diag, diag, causal[:].unsqueeze(1).broadcast_to([P, TILES, P]),
                                                    ALU.mult).then_inc(masked, 1)

        X = sb("X2", [P, NT, D])
        with ExitStack() as st:
            def tb(name, shape, dt=F32):
                return st.enter_context(nc.sbuf_tensor(name, shape, dt))

            def tsem(name):
                return st.enter_context(nc.semaphore(name))
            W1 = tb("W1", [P, 2, HID])
            W2 = tb("W2", [P, 2, HID])
            W1H = tb("W1H", [P, 2, HID], F32R)
            W1L = tb("W1L", [P, 2, HID], F32R)
            W2H = tb("W2H", [P, 2, HID], F32R)
            W2L = tb("W2L", [P, 2, HID], F32R)
            BC = tb("BC", [P, 2, HT + 1])
            HB = tb("HB", [P, 2, HT, S])
            HH = tb("HH", [P, 2, HT, S], F32R)
            HL = tb("HL", [P, 2, HT, S], F32R)
            GT = tb("GT", [P, 2, S])
            TMP = tb("TMP", [P, 2, S])
            WARM = tb("WARM5", [P, 1])
            w_sem = [tsem(f"w_loaded{k}") for k in range(2)]
            g_sem = [tsem(f"gates_loaded{k}") for k in range(2)]
            b_ready, h_ready, gelu_done, high_done, low_done, y_ready, scaled, added, w_split, links = map(
                tsem, ("b_ready", "h_ready5", "gelu_done", "high_done", "low_done", "y_ready5", "scaled", "added5", "w_split", "links5"))
            w_high, add_begun, e_begun, odd_done, warmed, x_back, first_w2 = map(
                tsem, ("w_high", "add_begun", "e_begun", "odd_done", "warmed5", "x_back", "first_w2"))
            TWO = 2
            with nc.Block() as block:
                @block.sync
                def _(sp):
                    def load_weights(e, k):
                        sp.dma_start(W1[:, k, :], w1[bass.ds(e, 1)].rearrange("a d n -> (a d) n")).then_inc(w_sem[k], 16)
                        sp.dma_start(W2[:, k, :].rearrange("p (j d) -> p j d", d=D),
                                     w2[bass.ds(e, 1)].rearrange("a (j p) d -> (a p) j d", p=P)).then_inc(w_sem[k], 16)

                    def gates_of(e):
                        with sp.Fori(0, B // 2) as b_half:
                            for p in range(2):
                                b = 2 * b_half + p
                                sp.wait_ge(scaled, e * B + b - 1 + TWO)
                                sp.dma_start(GT[:, p, :], gate_dram[bass.ds(b * E + e, 1), :].broadcast_to([P, S])).then_inc(g_sem[p], 16)

                    load_weights(0, 0)
                    load_weights(1, 1)
                    sp.dma_start(X[:], x_dram).then_inc(x_back, 16)
                    with sp.Fori(0, E // 2 - 1) as e_half:
                        for k in range(2):
                            sp.wait_ge(w_split, 2 * e_half + k + 1)
                            if k == 0:
                                sp.wait_ge(first_w2, 2)
                            load_weights(2 * e_half + k + 2, k)
                            gates_of(2 * e_half + k)
                    gates_of(E - 2)
                    sp.wait_ge(w_split, E - 1)
                    sp.sem_inc(w_sem[0], 32)
                    gates_of(E - 1)
                    sp.wait_ge(x_back, 16)

                @block.tensor
                def _(pe):
                    def hidden(n, k, b, j):
                        cols = slice(j * P, (j + 1) * P)
                        pe.wait_ge(gelu_done, HT * n + j + 1)
                        product(nc, PS[:, j, :], (W1H[:, k, cols], W1L[:, k, cols]), batch(b)).then_inc(h_ready, 1)

                    def output(n, k, p, j):
                        cols = slice(j * P, (j + 1) * P)
                        pe.wait_ge(low_done, HT * n + j + 1)
                        last = product(nc, PS[:, 4 + p, :], (W2H[:, k, cols], W2L[:, k, cols]),
                                       (HH[:, p, j, :], HL[:, p, j, :]), start=(j == 0), stop=(j == HT - 1))
                        if j == HT - 1:
                            last.then_inc(y_ready, 1)

                    def step(n, k, p, next_k, next_b):
                        hidden(n + 1, next_k, next_b, 0)
                        hidden(n + 1, next_k, next_b, 1)
                        hidden(n + 1, next_k, next_b, 2)
                        pe.wait_ge(scaled, n - 1 + TWO)
                        output(n, k, p, 0)
                        hidden(n + 1, next_k, next_b, 3)
                        output(n, k, p, 1)
                        output(n, k, p, 2)
                        output(n, k, p, 3)

                    pe.wait_ge(w_split, 1)
                    for j in range(HT):
                        hidden(0, 0, 0, j)
                    pe.wait_ge(first_w2, 2)
                    with pe.Fori(0, E // 2) as e_half:
                        for k in range(2):
                            e = 2 * e_half + k
                            with pe.Fori(0, B // 2 - 1) as b_half:
                                for p in range(2):
                                    b = 2 * b_half + p
                                    step(e * B + b, k, p, k, b + 1)
                            step(e * B + B - 2, k, 0, k, B - 1)
                            pe.wait_ge(w_split, e + 2)
                            step(e * B + B - 1, k, 1, 1 - k, 0)

                @block.scalar
                def _(act):
                    def high(n, p, j):
                        act.wait_ge(gelu_done, HT * n + j + 1 + HT)
                        nc.scalar.activation(HH[:, p, j, :], HB[:, p, j, :], ACT.Copy).then_inc(high_done, 1)

                    act.sem_inc(gelu_done, HT)
                    act.wait_ge(warmed, 1)
                    nc.scalar.activation(WARM[:], WARM[:], ACT.Gelu)
                    with act.Fori(0, E // 2) as e_half:
                        for k in range(2):
                            e = 2 * e_half + k
                            act.wait_ge(b_ready, e + 1)
                            act.sem_inc(e_begun, 1)
                            with act.Fori(0, B // 2) as b_half:
                                for p in range(2):
                                    n = e * B + 2 * b_half + p
                                    for j in range(HT):
                                        act.wait_ge(h_ready, HT * n + j + 1)
                                        nc.scalar.activation(HB[:, p, j, :], PS[:, j, :], ACT.Gelu,
                                                             bias=BC[:, k, j:j + 1]).then_inc(gelu_done, 1)
                                        if j % 2:
                                            high(n, p, j - 1)

                @block.vector
                def _(dve):
                    def biases(e, k):
                        nc.vector.tensor_copy(BC[:, k, 0:HT], B1_T[:, bass.ds(e * HT, HT)])
                        nc.vector.tensor_copy(BC[:, k, HT:HT + 1], B2_T[:, bass.ds(e, 1)]).then_inc(b_ready, 1)

                    dve.sem_inc(scaled, TWO)
                    nc.vector.memset(WARM[:], 0.0).then_inc(warmed, 1)
                    biases(0, 0)
                    dve.wait_ge(w_sem[0], 32)
                    nc.vector.tensor_copy(W2H[:, 0, :], W2[:, 0, :]).then_inc(first_w2, 1)
                    dve.wait_ge(first_w2, 1)
                    split_lo(nc, W2L[:, 0, :], W2[:, 0, :], W2H[:, 0, :]).then_inc(first_w2, 1)
                    with dve.Fori(0, E // 2) as e_half:
                        for k in range(2):
                            e = 2 * e_half + k
                            dve.wait_ge(scaled, e * B + TWO)
                            biases(e + 1, 1 - k)
                            with dve.Fori(0, B // 2) as b_half:
                                for p in range(2):
                                    b = 2 * b_half + p
                                    n = e * B + b
                                    for j in range(HT):
                                        if j % 2:
                                            dve.wait_ge(gelu_done, HT * n + j + 1 + HT)
                                            nc.vector.tensor_copy(HH[:, p, j, :], HB[:, p, j, :]).then_inc(odd_done, 1)
                                            dve.wait_ge(odd_done, HT // 2 * n + j // 2 + 1)
                                        else:
                                            dve.wait_ge(high_done, HT // 2 * n + j // 2 + 1)
                                        split_lo(nc, HL[:, p, j, :], HB[:, p, j, :], HH[:, p, j, :]).then_inc(low_done, 1)
                                    dve.wait_ge(y_ready, n + 1)
                                    dve.wait_ge(g_sem[p], 16 * e * (B // 2) + 16 * b_half + 16)
                                    dve.wait_ge(added, n - 1 + TWO)
                                    nc.vector.scalar_tensor_tensor(TMP[:, p, :], PS[:, 4 + p, :], BC[:, k, HT:HT + 1], GT[:, p, :],
                                                                   ALU.add, ALU.mult).then_inc(scaled, 1)

                @block.gpsimd
                def _(pool):
                    def prepare(e, k):
                        pool.wait_ge(w_sem[k], 16 * e + 32 - 16 * k)
                        pool.sem_inc(add_begun, 1)
                        nc.gpsimd.tensor_scalar(W1H[:, k, :], W1[:, k, :], 1.0, 1.0, ALU.mult, ALU.mult)
                        nc.gpsimd.tensor_scalar(W2H[:, k, :], W2[:, k, :], 1.0, 1.0, ALU.mult, ALU.mult).then_inc(w_high, 1)
                        pool.wait_ge(w_high, e + 1)
                        nc.gpsimd.tensor_tensor(W1L[:, k, :], W1[:, k, :], W1H[:, k, :].bitcast(F32), ALU.subtract)
                        nc.gpsimd.tensor_tensor(W2L[:, k, :], W2[:, k, :], W2H[:, k, :].bitcast(F32), ALU.subtract).then_inc(w_split, 1)

                    pool.sem_inc(added, TWO)
                    pool.wait_ge(w_sem[0], 32)
                    nc.gpsimd.tensor_scalar(W1H[:, 0, :], W1[:, 0, :], 1.0, 1.0, ALU.mult, ALU.mult).then_inc(w_high, 1)
                    pool.wait_ge(w_high, 1)
                    nc.gpsimd.tensor_tensor(W1L[:, 0, :], W1[:, 0, :], W1H[:, 0, :].bitcast(F32), ALU.subtract).then_inc(w_split, 1)
                    with pool.Fori(0, E // 2) as e_half:
                        for k in range(2):
                            e = 2 * e_half + k
                            prepare(e + 1, 1 - k)
                            with pool.Fori(0, B // 2) as b_half:
                                for p in range(2):
                                    b = 2 * b_half + p
                                    n = e * B + b
                                    pool.wait_ge(added, n + TWO)
                                    pool.wait_ge(scaled, n + 1 + TWO)
                                    pool.sem_inc(add_begun, 1)
                                    acc = ACCT[:, bass.ds((b + 1) * S, S)]
                                    nc.gpsimd.tensor_tensor(acc, acc, TMP[:, p, :], ALU.add).then_inc(added, 1)

        with ExitStack() as st:
            def tb(name, shape, dt=F32):
                return st.enter_context(nc.sbuf_tensor(name, shape, dt))

            def tsem(name):
                return st.enter_context(nc.semaphore(name))
            YC = tb("YC", [P, 2, S])
            RES = tb("RES", [P, 2, TILES, D])
            copied, turned, summed = map(tsem, ("copied6", "turned6", "summed6"))
            out_sem = [tsem(f"stored6_{p}") for p in range(2)]
            with nc.Block() as block:
                @block.vector
                def _(dve):
                    with dve.Fori(0, B // 2) as b0_half:
                        b0 = 2 * b0_half
                        for p in range(2):
                            b = b0 + p
                            nc.vector.tensor_copy(YC[:, p, :], ACCT[:, bass.ds((b + 1) * S, S)]).then_inc(copied, 1)
                        for p in range(2):
                            b = b0 + p
                            dve.wait_ge(turned, b + 1)
                            dve.wait_ge(out_sem[p], b0 * 8 + 16)
                            nc.vector.tensor_tensor(RES[:, p, :, :], PS[:, p, :].rearrange("p (t d) -> p t d", d=D),
                                                    X[:, bass.ds(b * TILES, TILES), :], ALU.add).then_inc(summed, 1)

                @block.tensor
                def _(pe):
                    with pe.Fori(0, B // 2) as b0_half:
                        b0 = 2 * b0_half
                        for p in range(2):
                            b = b0 + p
                            pe.wait_ge(copied, b + 1)
                            for t in range(TILES):
                                last = nc.tensor.transpose(PS[:, p, t * P:(t + 1) * P], YC[:, p, t * P:(t + 1) * P], ident[:])
                            last.then_inc(turned, 1)

                @block.sync
                def _(sp):
                    for p in range(2):
                        sp.sem_inc(out_sem[p], 16)
                    with sp.Fori(0, B // 2) as b0_half:
                        b0 = 2 * b0_half
                        for p in range(2):
                            b = b0 + p
                            sp.wait_ge(summed, b + 1)
                            sp.dma_start(out[bass.ds(b, 1)].rearrange("a (t p) d -> p (a t) d", p=P), RES[:, p, :, :]
                                         ).then_inc(out_sem[p], 16)
                    for p in range(2):
                        sp.wait_ge(out_sem[p], B // 2 * 16 + 16)


_INS = ['L0_attn_x', 'L0_attn_kernel', 'L0_attn_WO', 'L0_ffn_W_r', 'L0_ffn_W_k', 'L0_ffn_W_v', 'L0_ffn_mu_r',
        'L0_ffn_mu_k', 'L1_attn_Wq', 'L1_attn_Wk', 'L1_attn_Wv', 'L1_attn_Wo', 'L1_attn_gamma', 'L1_attn_beta',
        'L1_ffn_router_w', 'L1_ffn_w1', 'L1_ffn_b1', 'L1_ffn_w2', 'L1_ffn_b2']


def kernel(**inputs):
    import numpy as _np
    import concourse.bacc as _bacc
    from concourse import mybir as _mybir
    from concourse.bass_utils import run_bass_kernel_spmd as _run

    nc = _bacc.Bacc("TRN2", target_bir_lowering=False, num_devices=1)
    arrays, args = {}, []
    for name in _INS:
        a = _np.ascontiguousarray(inputs[name])
        arrays[f"in_{name}_dram"] = a
        args.append(nc.dram_tensor(f"in_{name}_dram", a.shape, _mybir.dt.from_np(a.dtype), kind="ExternalInput").ap())
    args.append(nc.dram_tensor("out_dram", (8, 512, 128), _mybir.dt.float32, kind="ExternalOutput").ap())
    prob_d2_kernel(nc, *args)
    r = _run(nc, [arrays], core_ids=[0])
    return r.results[0]["out_dram"]
```
